# Optimizing a Trainium2 kernel written in Bass

```python
import numpy as np
import jax
import jax.numpy as jnp

def _softmax(x, axis=-1):
    return jax.nn.softmax(x, axis=axis)

def _gelu(x):
    return jax.nn.gelu(x, approximate=True)

def _silu(x):
    return jax.nn.silu(x)

def _sigmoid(x):
    return jax.nn.sigmoid(x)

def _layernorm(x, axis=-1, eps=1e-05):
    m = jnp.mean(x, axis=axis, keepdims=True)
    v = jnp.var(x, axis=axis, keepdims=True)
    return (x - m) / jnp.sqrt(v + eps)

def _scatter_add(tgt, idx, src, axis=0):
    return tgt.at[idx].add(src)

def _segment_sum(src, seg, n):
    return jax.ops.segment_sum(src, seg, n)
kernel_name = 'mk_recurrent_d4_jaxref_r8_c3e849'

def setup_inputs(seed: int=0):
    np.random.seed(seed)
    _w = jnp.asarray

    def _L0_attn_setup():
        import jax, jax.numpy as jnp
        import numpy as np
        D = 128
        B = 16
        L = 256

        def _lin_init(key, din, dout):
            kw, kb = jax.random.split(key)
            s = 1.0 / np.sqrt(din)
            w = jax.random.uniform(kw, (dout, din), minval=-s, maxval=s, dtype=jnp.float32)
            b = jax.random.uniform(kb, (dout,), minval=-s, maxval=s, dtype=jnp.float32)
            return (w, b)

        def _rms_norm(x, w, eps=1e-06):
            x32 = x.astype(jnp.float32)
            y = x32 * jax.lax.rsqrt(jnp.mean(x32 * x32, axis=-1, keepdims=True) + eps)
            return y.astype(x.dtype) * w
        key = jax.random.key(seed)
        ks = jax.random.split(key, 9)
        fc_w, fc_b = _lin_init(ks[0], D, D)
        fc_r_w, fc_r_b = _lin_init(ks[1], D, D)
        fc_i_w, fc_i_b = _lin_init(ks[2], D, D)
        fc_gate_w, fc_gate_b = _lin_init(ks[3], D, D)
        mlp_gate_w, mlp_gate_b = _lin_init(ks[4], D, 3 * D)
        mlp_fc_w, mlp_fc_b = _lin_init(ks[5], D, 3 * D)
        out_w, out_b = _lin_init(ks[6], 3 * D, D)
        alpha = jax.random.uniform(ks[7], (1, 1, D), dtype=jnp.float32) * (0.999 - 0.9) + 0.9
        hidden_states = jax.random.normal(ks[8], (B, L, D), dtype=jnp.float32)
        return dict(hidden_states=hidden_states, alpha=alpha, fc_w=fc_w, fc_b=fc_b, fc_r_w=fc_r_w, fc_r_b=fc_r_b, fc_i_w=fc_i_w, fc_i_b=fc_i_b, fc_gate_w=fc_gate_w, fc_gate_b=fc_gate_b, norm_w=jnp.ones((D,), jnp.float32), norm2_w=jnp.ones((D,), jnp.float32), mlp_gate_w=mlp_gate_w, mlp_gate_b=mlp_gate_b, mlp_fc_w=mlp_fc_w, mlp_fc_b=mlp_fc_b, out_w=out_w, out_b=out_b)
    _L0_attn_in = _L0_attn_setup()

    def _L0_ffn_setup():
        import jax, jax.numpy as jnp
        import numpy as np
        DIM = 128
        DEPTH = 2
        HEADS = 8
        DIM_HEAD = 64
        WINDOW = 64
        INNER = HEADS * DIM_HEAD
        HID = int(DIM * 4 * 2 / 3)
        B, N = (2, 1024)
        QK_SCALE = 8.0

        def shift_token(t):
            t1, t2 = jnp.split(t, 2, axis=-1)
            t2 = jnp.pad(t2, ((0, 0), (1, 0), (0, 0)))[:, :-1]
            return jnp.concatenate([t1, t2], axis=-1)

        def l2norm(t):
            return t / jnp.clip(jnp.linalg.norm(t, axis=-1, keepdims=True), 1e-12)

        def rotate_half(x):
            x1, x2 = jnp.split(x, 2, axis=-1)
            return jnp.concatenate([-x2, x1], axis=-1)

        def rotary_xpos(q, k):
            n = q.shape[-2]
            half_idx = jnp.arange(0, DIM_HEAD, 2, dtype=jnp.float32)
            inv_freq = 1.0 / 10000.0 ** (half_idx / DIM_HEAD)
            t = jnp.arange(n, dtype=jnp.float32)
            freqs = t[:, None] * inv_freq[None, :]
            freqs = jnp.concatenate([freqs, freqs], axis=-1)
            base = (half_idx + 0.4 * DIM_HEAD) / (1.4 * DIM_HEAD)
            power = (t - n // 2) / float(WINDOW // 2)
            scale = base[None, :] ** power[:, None]
            scale = jnp.concatenate([scale, scale], axis=-1)
            cos, sin = (jnp.cos(freqs), jnp.sin(freqs))
            q = q * cos * scale + rotate_half(q) * sin * scale
            k = k * cos / scale + rotate_half(k) * sin / scale
            return (q, k)

        def local_attention(q, k, v):
            b, h, n, d = q.shape
            w = n // WINDOW
            bq = q.reshape(b, h, w, WINDOW, d) * QK_SCALE
            bk = k.reshape(b, h, w, WINDOW, d)
            bv = v.reshape(b, h, w, WINDOW, d)

            def look_around(t):
                p = jnp.pad(t, ((0, 0), (0, 0), (1, 0), (0, 0), (0, 0)))
                return jnp.concatenate([p[:, :, :w], p[:, :, 1:]], axis=3)
            bk, bv = (look_around(bk), look_around(bv))
            bt = jnp.arange(n).reshape(w, WINDOW)
            btp = jnp.pad(bt, ((1, 0), (0, 0)), constant_values=-1)
            btk = jnp.concatenate([btp[:w], btp[1:]], axis=1)
            sim = jnp.einsum('bhwid,bhwjd->bhwij', bq, bk)
            i = bt[:, :, None]
            j = btk[:, None, :]
            mask = (i < j) | (i > j + WINDOW) | (j == -1)
            sim = jnp.where(mask, -jnp.finfo(sim.dtype).max, sim)
            attn = jax.nn.softmax(sim, axis=-1)
            out = jnp.einsum('bhwij,bhwjd->bhwid', attn, bv)
            return out.reshape(b, h, n, d)

        def _layer(x, wqkv, qs, ksc, wo, lg, lb, w1, b1, w2, b2):
            b, n, _ = x.shape
            h = shift_token(x)
            qkv = h @ wqkv
            q, k, v = jnp.split(qkv, 3, axis=-1)
            to_heads = lambda t: t.reshape(b, n, HEADS, DIM_HEAD).transpose(0, 2, 1, 3)
            q, k, v = (to_heads(q), to_heads(k), to_heads(v))
            q = l2norm(q) * qs
            k = l2norm(k) * ksc
            q, k = rotary_xpos(q, k)
            o = local_attention(q, k, v)
            o = o.transpose(0, 2, 1, 3).reshape(b, n, INNER)
            x = x + o @ wo
            h = shift_token(x)
            mu = h.mean(-1, keepdims=True)
            var = h.var(-1, keepdims=True)
            h = (h - mu) / jnp.sqrt(var + 1e-05) * lg + lb
            h = h @ w1 + b1
            a, g = jnp.split(h, 2, axis=-1)
            h = a * jax.nn.gelu(g, approximate=False)
            x = x + h @ w2 + b2
            return x
        key = jax.random.key(seed)
        ks = jax.random.split(key, 6)
        return {'x': jax.random.normal(ks[0], (B, N, DIM), jnp.float32), 'wqkv': jax.random.normal(ks[1], (DEPTH, DIM, 3 * INNER), jnp.float32) * 0.02, 'q_scale': jnp.ones((DEPTH, DIM_HEAD), jnp.float32), 'k_scale': jnp.ones((DEPTH, DIM_HEAD), jnp.float32), 'wo': jax.random.normal(ks[2], (DEPTH, INNER, DIM), jnp.float32) * 0.02, 'ln_g': jnp.ones((DEPTH, DIM), jnp.float32), 'ln_b': jnp.zeros((DEPTH, DIM), jnp.float32), 'w1': jax.random.normal(ks[3], (DEPTH, DIM, 2 * HID), jnp.float32) * 0.02, 'b1': jnp.zeros((DEPTH, 2 * HID), jnp.float32), 'w2': jax.random.normal(ks[4], (DEPTH, HID, DIM), jnp.float32) * 0.02, 'b2': jnp.zeros((DEPTH, DIM), jnp.float32)}
    _L0_ffn_in = _L0_ffn_setup()

    def _L1_attn_setup():
        import math
        import jax, jax.numpy as jnp
        import numpy as np
        N_EMBD = 128
        N_HEAD = 16
        HEAD_DIM = N_EMBD // N_HEAD

        def alibi_slopes(n_heads):
            start = 2.0 ** (-2.0 ** (-(math.log2(n_heads) - 3)))
            return np.array([start * start ** i for i in range(n_heads)], dtype=np.float32)
        key = jax.random.key(seed)
        k1, k2, k3 = jax.random.split(key, 3)
        B, T, C = (2, 256, N_EMBD)
        x = jax.random.normal(k1, (B, T, C), dtype=jnp.float32)
        w_attn = jax.random.normal(k2, (3 * C, C), dtype=jnp.float32) * (1.0 / math.sqrt(C))
        w_proj = jax.random.normal(k3, (C, C), dtype=jnp.float32) * (1.0 / math.sqrt(C))
        return {'x': x, 'w_attn': w_attn, 'w_proj': w_proj}
    _L1_attn_in = _L1_attn_setup()

    def _L1_ffn_setup():
        import jax, jax.numpy as jnp
        import numpy as np
        B, T, D, H, E = (4, 256, 128, 512, 8)
        key = jax.random.key(seed)
        ks = jax.random.split(key, 7)
        x = jax.random.normal(ks[0], (B, T, D), dtype=jnp.float32)
        Wg = jax.random.normal(ks[1], (D, E), dtype=jnp.float32) / np.sqrt(D)
        bg = jax.random.normal(ks[2], (E,), dtype=jnp.float32) * 0.01
        W1 = jax.random.normal(ks[3], (E, D, H), dtype=jnp.float32) / np.sqrt(D)
        b1 = jax.random.normal(ks[4], (E, H), dtype=jnp.float32) * 0.01
        W2 = jax.random.normal(ks[5], (E, H, D), dtype=jnp.float32) / np.sqrt(H)
        b2 = jax.random.normal(ks[6], (E, D), dtype=jnp.float32) * 0.01
        return {'x': x, 'Wg': Wg, 'bg': bg, 'W1': W1, 'b1': b1, 'W2': W2, 'b2': b2}
    _L1_ffn_in = _L1_ffn_setup()

    def _L2_attn_setup():
        import jax, jax.numpy as jnp
        import numpy as np
        B, S, E = (4, 256, 128)
        H, KVH = (16, 4)
        D = E // H
        QL, KVL = (64, 32)
        ROPE_BASE = 10000.0

        def _rope(x):
            d = x.shape[-1]
            inv_freq = 1.0 / ROPE_BASE ** (jnp.arange(0, d, 2, dtype=jnp.float32) / d)
            t = jnp.arange(x.shape[1], dtype=jnp.float32)
            freqs = jnp.outer(t, inv_freq)
            cos = jnp.cos(freqs)[None, :, None, :].astype(x.dtype)
            sin = jnp.sin(freqs)[None, :, None, :].astype(x.dtype)
            x1, x2 = (x[..., ::2], x[..., 1::2])
            r1 = x1 * cos - x2 * sin
            r2 = x1 * sin + x2 * cos
            return jnp.stack([r1, r2], axis=-1).reshape(x.shape)
        key = jax.random.key(seed)
        ks = jax.random.split(key, 7)
        s = 0.02
        return {'x': jax.random.normal(ks[0], (B, S, E), dtype=jnp.float32), 'Wqa': jax.random.normal(ks[1], (E, QL), dtype=jnp.float32) * s, 'Wqb': jax.random.normal(ks[2], (QL, E), dtype=jnp.float32) * s, 'Wkva': jax.random.normal(ks[3], (E, KVL), dtype=jnp.float32) * s, 'Wkvb': jax.random.normal(ks[4], (KVL, KVH * D * 2), dtype=jnp.float32) * s, 'Wout': jax.random.normal(ks[5], (E, E), dtype=jnp.float32) * s, 'bout': jax.random.normal(ks[6], (E,), dtype=jnp.float32) * s}
    _L2_attn_in = _L2_attn_setup()

    def _L2_ffn_setup():
        import jax, jax.numpy as jnp
        import numpy as np
        EMB = 128
        FF = 4 * EMB

        def _ternary(w):
            scale = jnp.maximum(jnp.mean(jnp.abs(w)), 1e-08)
            w_t = jnp.clip(jnp.round(w / scale), -1.0, 1.0)
            return w + jax.lax.stop_gradient(w_t - w)
        key = jax.random.key(seed)
        kx, k1, k2, kb1, kb2 = jax.random.split(key, 5)
        x = jax.random.normal(kx, (4, 256, EMB), dtype=jnp.float32)
        lim1 = 1.0 / np.sqrt(EMB)
        lim2 = 1.0 / np.sqrt(FF)
        W1 = jax.random.uniform(k1, (FF, EMB), jnp.float32, -lim1, lim1)
        b1 = jax.random.uniform(kb1, (FF,), jnp.float32, -lim1, lim1)
        W2 = jax.random.uniform(k2, (EMB, FF), jnp.float32, -lim2, lim2)
        b2 = jax.random.uniform(kb2, (EMB,), jnp.float32, -lim2, lim2)
        return {'x': x, 'W1': W1, 'b1': b1, 'W2': W2, 'b2': b2}
    _L2_ffn_in = _L2_ffn_setup()

    def _L3_attn_setup():
        import jax, jax.numpy as jnp
        import numpy as np
        N_EMBD = 128
        N_HEAD = 16
        HEAD_DIM = N_EMBD // N_HEAD
        KV_RANK = 32
        Q_RANK = 64
        ROPE_DIM = 32
        B, T = (2, 256)
        EPS = 1e-06

        def _rope_tables(T, dim):
            inv_freq = 1.0 / 10000.0 ** (np.arange(0, dim, 2, dtype=np.float32) / dim)
            t = np.arange(T, dtype=np.float32)
            freqs = np.outer(t, inv_freq)
            emb = np.concatenate([freqs, freqs], -1)
            return (jnp.asarray(np.cos(emb)), jnp.asarray(np.sin(emb)))

        def _apply_rope(x, cos, sin):
            d2 = x.shape[-1] // 2
            x1, x2 = (x[..., :d2], x[..., d2:])
            rot = jnp.concatenate([-x2, x1], axis=-1)
            return x * cos[None, None, :, :] + rot * sin[None, None, :, :]
        key = jax.random.key(seed)
        ks = jax.random.split(key, 10)

        def w(k, fan_in, fan_out):
            return jax.random.normal(k, (fan_in, fan_out), dtype=jnp.float32) * fan_in ** (-0.5)
        return {'x': jax.random.normal(ks[0], (B, T, N_EMBD), dtype=jnp.float32), 'W_kv': w(ks[1], N_EMBD, KV_RANK), 'g_kv': jnp.ones((KV_RANK,), dtype=jnp.float32), 'W_kdec': w(ks[2], KV_RANK, N_HEAD * HEAD_DIM), 'W_vdec': w(ks[3], KV_RANK, N_HEAD * HEAD_DIM), 'W_q': w(ks[4], N_EMBD, Q_RANK), 'W_qdec': w(ks[5], Q_RANK, N_HEAD * HEAD_DIM), 'W_krope': w(ks[6], N_EMBD, N_HEAD * ROPE_DIM), 'W_qrope': w(ks[7], Q_RANK, N_HEAD * ROPE_DIM), 'W_o': w(ks[8], N_HEAD * HEAD_DIM, N_EMBD)}
    _L3_attn_in = _L3_attn_setup()

    def _L3_ffn_setup():
        import jax, jax.numpy as jnp
        import numpy as np
        B, N, D = (4, 256, 128)
        SPARSITY = 0.01
        key = jax.random.key(seed)
        k1, k2, k3 = jax.random.split(key, 3)
        x = jax.random.normal(k1, (B, N, D), dtype=jnp.float32)
        spatial = jax.random.normal(k2, (D, D), dtype=jnp.float32) * 0.02
        freq = jnp.fft.fft(spatial, axis=-1)
        k = int(D * SPARSITY)
        mag = jnp.abs(freq)
        kth = jax.lax.top_k(mag, k)[0][:, -1:]
        w_sparse = jnp.where(mag >= kth, freq, 0.0 + 0j)
        bias = jax.random.normal(k3, (D,), dtype=jnp.float32) * 0.01
        return {'x': x, 'w_freq_real': jnp.real(w_sparse).astype(jnp.float32), 'w_freq_imag': jnp.imag(w_sparse).astype(jnp.float32), 'bias': bias}
    _L3_ffn_in = _L3_ffn_setup()
    _d = {'L0_attn_hidden_states': _L0_attn_in['hidden_states'], 'L0_attn_alpha': _L0_attn_in['alpha'], 'L0_attn_fc_w': _L0_attn_in['fc_w'], 'L0_attn_fc_b': _L0_attn_in['fc_b'], 'L0_attn_fc_r_w': _L0_attn_in['fc_r_w'], 'L0_attn_fc_r_b': _L0_attn_in['fc_r_b'], 'L0_attn_fc_i_w': _L0_attn_in['fc_i_w'], 'L0_attn_fc_i_b': _L0_attn_in['fc_i_b'], 'L0_attn_fc_gate_w': _L0_attn_in['fc_gate_w'], 'L0_attn_fc_gate_b': _L0_attn_in['fc_gate_b'], 'L0_attn_norm_w': _L0_attn_in['norm_w'], 'L0_attn_norm2_w': _L0_attn_in['norm2_w'], 'L0_attn_mlp_gate_w': _L0_attn_in['mlp_gate_w'], 'L0_attn_mlp_gate_b': _L0_attn_in['mlp_gate_b'], 'L0_attn_mlp_fc_w': _L0_attn_in['mlp_fc_w'], 'L0_attn_mlp_fc_b': _L0_attn_in['mlp_fc_b'], 'L0_attn_out_w': _L0_attn_in['out_w'], 'L0_attn_out_b': _L0_attn_in['out_b'], 'L0_ffn_wqkv': _L0_ffn_in['wqkv'], 'L0_ffn_q_scale': _L0_ffn_in['q_scale'], 'L0_ffn_k_scale': _L0_ffn_in['k_scale'], 'L0_ffn_wo': _L0_ffn_in['wo'], 'L0_ffn_ln_g': _L0_ffn_in['ln_g'], 'L0_ffn_ln_b': _L0_ffn_in['ln_b'], 'L0_ffn_w1': _L0_ffn_in['w1'], 'L0_ffn_b1': _L0_ffn_in['b1'], 'L0_ffn_w2': _L0_ffn_in['w2'], 'L0_ffn_b2': _L0_ffn_in['b2'], 'L1_attn_w_attn': _L1_attn_in['w_attn'], 'L1_attn_w_proj': _L1_attn_in['w_proj'], 'L1_ffn_Wg': _L1_ffn_in['Wg'], 'L1_ffn_bg': _L1_ffn_in['bg'], 'L1_ffn_W1': _L1_ffn_in['W1'], 'L1_ffn_b1': _L1_ffn_in['b1'], 'L1_ffn_W2': _L1_ffn_in['W2'], 'L1_ffn_b2': _L1_ffn_in['b2'], 'L2_attn_Wqa': _L2_attn_in['Wqa'], 'L2_attn_Wqb': _L2_attn_in['Wqb'], 'L2_attn_Wkva': _L2_attn_in['Wkva'], 'L2_attn_Wkvb': _L2_attn_in['Wkvb'], 'L2_attn_Wout': _L2_attn_in['Wout'], 'L2_attn_bout': _L2_attn_in['bout'], 'L2_ffn_W1': _L2_ffn_in['W1'], 'L2_ffn_b1': _L2_ffn_in['b1'], 'L2_ffn_W2': _L2_ffn_in['W2'], 'L2_ffn_b2': _L2_ffn_in['b2'], 'L3_attn_W_kv': _L3_attn_in['W_kv'], 'L3_attn_g_kv': _L3_attn_in['g_kv'], 'L3_attn_W_kdec': _L3_attn_in['W_kdec'], 'L3_attn_W_vdec': _L3_attn_in['W_vdec'], 'L3_attn_W_q': _L3_attn_in['W_q'], 'L3_attn_W_qdec': _L3_attn_in['W_qdec'], 'L3_attn_W_krope': _L3_attn_in['W_krope'], 'L3_attn_W_qrope': _L3_attn_in['W_qrope'], 'L3_attn_W_o': _L3_attn_in['W_o'], 'L3_ffn_w_freq_real': _L3_ffn_in['w_freq_real'], 'L3_ffn_w_freq_imag': _L3_ffn_in['w_freq_imag'], 'L3_ffn_bias': _L3_ffn_in['bias']}
    _x0 = _d['L0_attn_hidden_states']
    _d['L0_attn_hidden_states'] = jax.random.normal(jax.random.fold_in(jax.random.key(seed), 1), (16, 256, 128), dtype=_x0.dtype)
    del _x0
    return _d

def reference(L0_attn_hidden_states, L0_attn_alpha, L0_attn_fc_w, L0_attn_fc_b, L0_attn_fc_r_w, L0_attn_fc_r_b, L0_attn_fc_i_w, L0_attn_fc_i_b, L0_attn_fc_gate_w, L0_attn_fc_gate_b, L0_attn_norm_w, L0_attn_norm2_w, L0_attn_mlp_gate_w, L0_attn_mlp_gate_b, L0_attn_mlp_fc_w, L0_attn_mlp_fc_b, L0_attn_out_w, L0_attn_out_b, L0_ffn_wqkv, L0_ffn_q_scale, L0_ffn_k_scale, L0_ffn_wo, L0_ffn_ln_g, L0_ffn_ln_b, L0_ffn_w1, L0_ffn_b1, L0_ffn_w2, L0_ffn_b2, L1_attn_w_attn, L1_attn_w_proj, L1_ffn_Wg, L1_ffn_bg, L1_ffn_W1, L1_ffn_b1, L1_ffn_W2, L1_ffn_b2, L2_attn_Wqa, L2_attn_Wqb, L2_attn_Wkva, L2_attn_Wkvb, L2_attn_Wout, L2_attn_bout, L2_ffn_W1, L2_ffn_b1, L2_ffn_W2, L2_ffn_b2, L3_attn_W_kv, L3_attn_g_kv, L3_attn_W_kdec, L3_attn_W_vdec, L3_attn_W_q, L3_attn_W_qdec, L3_attn_W_krope, L3_attn_W_qrope, L3_attn_W_o, L3_ffn_w_freq_real, L3_ffn_w_freq_imag, L3_ffn_bias):

    def _L0_attn_ref(hidden_states, alpha, fc_w, fc_b, fc_r_w, fc_r_b, fc_i_w, fc_i_b, fc_gate_w, fc_gate_b, norm_w, norm2_w, mlp_gate_w, mlp_gate_b, mlp_fc_w, mlp_fc_b, out_w, out_b):
        import jax, jax.numpy as jnp
        import numpy as np
        D = 128
        B = 16
        L = 256

        def _lin_init(key, din, dout):
            kw, kb = jax.random.split(key)
            s = 1.0 / np.sqrt(din)
            w = jax.random.uniform(kw, (dout, din), minval=-s, maxval=s, dtype=jnp.float32)
            b = jax.random.uniform(kb, (dout,), minval=-s, maxval=s, dtype=jnp.float32)
            return (w, b)

        def _rms_norm(x, w, eps=1e-06):
            x32 = x.astype(jnp.float32)
            y = x32 * jax.lax.rsqrt(jnp.mean(x32 * x32, axis=-1, keepdims=True) + eps)
            return y.astype(x.dtype) * w
        residual = hidden_states
        h = _rms_norm(hidden_states, norm_w)
        gate = jax.nn.gelu(h @ fc_gate_w.T + fc_gate_b, approximate=False)
        hs = h @ fc_w.T + fc_b
        r = jax.nn.sigmoid(h @ fc_r_w.T + fc_r_b)
        i = jax.nn.sigmoid(h @ fc_i_w.T + fc_i_b)
        a = jnp.exp(-8.0 * jax.nn.softplus(alpha) * r)
        s = jnp.sqrt(1.0 - a * a) * hs * i

        def step(carry, xs):
            a_t, s_t = xs
            o = a_t * carry + s_t
            return (o, o)
        a_l = jnp.swapaxes(a, 0, 1)
        s_l = jnp.swapaxes(s, 0, 1)
        _, out_l = jax.lax.scan(step, jnp.zeros_like(s_l[0]), (a_l, s_l))
        out = jnp.swapaxes(out_l, 0, 1)
        hs2 = out * gate + residual
        h2 = _rms_norm(hs2, norm2_w)
        g2 = jax.nn.gelu(h2 @ mlp_gate_w.T + mlp_gate_b, approximate=False)
        f2 = h2 @ mlp_fc_w.T + mlp_fc_b
        return f2 * g2 @ out_w.T + out_b + hs2

    def _L0_ffn_ref(x, wqkv, q_scale, k_scale, wo, ln_g, ln_b, w1, b1, w2, b2):
        import jax, jax.numpy as jnp
        import numpy as np
        DIM = 128
        DEPTH = 2
        HEADS = 8
        DIM_HEAD = 64
        WINDOW = 64
        INNER = HEADS * DIM_HEAD
        HID = int(DIM * 4 * 2 / 3)
        B, N = (2, 1024)
        QK_SCALE = 8.0

        def shift_token(t):
            t1, t2 = jnp.split(t, 2, axis=-1)
            t2 = jnp.pad(t2, ((0, 0), (1, 0), (0, 0)))[:, :-1]
            return jnp.concatenate([t1, t2], axis=-1)

        def l2norm(t):
            return t / jnp.clip(jnp.linalg.norm(t, axis=-1, keepdims=True), 1e-12)

        def rotate_half(x):
            x1, x2 = jnp.split(x, 2, axis=-1)
            return jnp.concatenate([-x2, x1], axis=-1)

        def rotary_xpos(q, k):
            n = q.shape[-2]
            half_idx = jnp.arange(0, DIM_HEAD, 2, dtype=jnp.float32)
            inv_freq = 1.0 / 10000.0 ** (half_idx / DIM_HEAD)
            t = jnp.arange(n, dtype=jnp.float32)
            freqs = t[:, None] * inv_freq[None, :]
            freqs = jnp.concatenate([freqs, freqs], axis=-1)
            base = (half_idx + 0.4 * DIM_HEAD) / (1.4 * DIM_HEAD)
            power = (t - n // 2) / float(WINDOW // 2)
            scale = base[None, :] ** power[:, None]
            scale = jnp.concatenate([scale, scale], axis=-1)
            cos, sin = (jnp.cos(freqs), jnp.sin(freqs))
            q = q * cos * scale + rotate_half(q) * sin * scale
            k = k * cos / scale + rotate_half(k) * sin / scale
            return (q, k)

        def local_attention(q, k, v):
            b, h, n, d = q.shape
            w = n // WINDOW
            bq = q.reshape(b, h, w, WINDOW, d) * QK_SCALE
            bk = k.reshape(b, h, w, WINDOW, d)
            bv = v.reshape(b, h, w, WINDOW, d)

            def look_around(t):
                p = jnp.pad(t, ((0, 0), (0, 0), (1, 0), (0, 0), (0, 0)))
                return jnp.concatenate([p[:, :, :w], p[:, :, 1:]], axis=3)
            bk, bv = (look_around(bk), look_around(bv))
            bt = jnp.arange(n).reshape(w, WINDOW)
            btp = jnp.pad(bt, ((1, 0), (0, 0)), constant_values=-1)
            btk = jnp.concatenate([btp[:w], btp[1:]], axis=1)
            sim = jnp.einsum('bhwid,bhwjd->bhwij', bq, bk)
            i = bt[:, :, None]
            j = btk[:, None, :]
            mask = (i < j) | (i > j + WINDOW) | (j == -1)
            sim = jnp.where(mask, -jnp.finfo(sim.dtype).max, sim)
            attn = jax.nn.softmax(sim, axis=-1)
            out = jnp.einsum('bhwij,bhwjd->bhwid', attn, bv)
            return out.reshape(b, h, n, d)

        def _layer(x, wqkv, qs, ksc, wo, lg, lb, w1, b1, w2, b2):
            b, n, _ = x.shape
            h = shift_token(x)
            qkv = h @ wqkv
            q, k, v = jnp.split(qkv, 3, axis=-1)
            to_heads = lambda t: t.reshape(b, n, HEADS, DIM_HEAD).transpose(0, 2, 1, 3)
            q, k, v = (to_heads(q), to_heads(k), to_heads(v))
            q = l2norm(q) * qs
            k = l2norm(k) * ksc
            q, k = rotary_xpos(q, k)
            o = local_attention(q, k, v)
            o = o.transpose(0, 2, 1, 3).reshape(b, n, INNER)
            x = x + o @ wo
            h = shift_token(x)
            mu = h.mean(-1, keepdims=True)
            var = h.var(-1, keepdims=True)
            h = (h - mu) / jnp.sqrt(var + 1e-05) * lg + lb
            h = h @ w1 + b1
            a, g = jnp.split(h, 2, axis=-1)
            h = a * jax.nn.gelu(g, approximate=False)
            x = x + h @ w2 + b2
            return x
        for l in range(DEPTH):
            x = _layer(x, wqkv[l], q_scale[l], k_scale[l], wo[l], ln_g[l], ln_b[l], w1[l], b1[l], w2[l], b2[l])
        return x

    def _L1_attn_ref(x, w_attn, w_proj):
        import math
        import jax, jax.numpy as jnp
        import numpy as np
        N_EMBD = 128
        N_HEAD = 16
        HEAD_DIM = N_EMBD // N_HEAD

        def alibi_slopes(n_heads):
            start = 2.0 ** (-2.0 ** (-(math.log2(n_heads) - 3)))
            return np.array([start * start ** i for i in range(n_heads)], dtype=np.float32)
        B, T, C = x.shape
        H, D = (N_HEAD, HEAD_DIM)
        qkv = x @ w_attn.T
        q, k, v = jnp.split(qkv, 3, axis=-1)
        q = q.reshape(B, T, H, D).transpose(0, 2, 1, 3)
        k = k.reshape(B, T, H, D).transpose(0, 2, 1, 3)
        v = v.reshape(B, T, H, D).transpose(0, 2, 1, 3)
        att = jnp.einsum('bhqd,bhkd->bhqk', q, k) * (1.0 / math.sqrt(D))
        pos = jnp.arange(T)
        rel = pos[None, :] - pos[:, None]
        slopes = jnp.asarray(alibi_slopes(H))[:, None, None]
        causal = rel <= 0
        bias = jnp.where(causal, slopes * rel, -jnp.inf)
        att = att + bias[None]
        att = jax.nn.softmax(att, axis=-1)
        y = jnp.einsum('bhqk,bhkd->bhqd', att, v)
        y = y.transpose(0, 2, 1, 3).reshape(B, T, C)
        return y @ w_proj.T

    def _L1_ffn_ref(x, Wg, bg, W1, b1, W2, b2):
        import jax, jax.numpy as jnp
        import numpy as np
        B, T, D, H, E = (4, 256, 128, 512, 8)
        gate_scores = x @ Wg + bg
        top1 = jnp.argmax(gate_scores, axis=-1)
        onehot = jax.nn.one_hot(top1, Wg.shape[-1], dtype=x.dtype)
        h = jax.nn.relu(jnp.einsum('btd,edh->beth', x, W1) + b1[None, :, None, :])
        y = jnp.einsum('beth,ehd->betd', h, W2) + b2[None, :, None, :]
        out = jnp.einsum('betd,bte->btd', y, onehot)
        return out

    def _L2_attn_ref(x, Wqa, Wqb, Wkva, Wkvb, Wout, bout):
        import jax, jax.numpy as jnp
        import numpy as np
        B, S, E = (4, 256, 128)
        H, KVH = (16, 4)
        D = E // H
        QL, KVL = (64, 32)
        ROPE_BASE = 10000.0

        def _rope(x):
            d = x.shape[-1]
            inv_freq = 1.0 / ROPE_BASE ** (jnp.arange(0, d, 2, dtype=jnp.float32) / d)
            t = jnp.arange(x.shape[1], dtype=jnp.float32)
            freqs = jnp.outer(t, inv_freq)
            cos = jnp.cos(freqs)[None, :, None, :].astype(x.dtype)
            sin = jnp.sin(freqs)[None, :, None, :].astype(x.dtype)
            x1, x2 = (x[..., ::2], x[..., 1::2])
            r1 = x1 * cos - x2 * sin
            r2 = x1 * sin + x2 * cos
            return jnp.stack([r1, r2], axis=-1).reshape(x.shape)
        b, s, _ = x.shape
        scale = D ** (-0.5)
        q = (x @ Wqa @ Wqb).reshape(b, s, H, D)
        kv = (x @ Wkva @ Wkvb).reshape(b, s, KVH, D, 2)
        k, v = (kv[..., 0], kv[..., 1])
        q = _rope(q)
        k = _rope(k)
        g = H // KVH
        k = jnp.repeat(k, g, axis=2)
        v = jnp.repeat(v, g, axis=2)
        scores = jnp.einsum('bqhd,bkhd->bhqk', q, k) * scale
        causal = jnp.triu(jnp.ones((s, s), dtype=bool), k=1)
        scores = jnp.where(causal[None, None], -jnp.inf, scores)
        w = jax.nn.softmax(scores, axis=-1)
        out = jnp.einsum('bhqk,bkhd->bqhd', w, v).reshape(b, s, E)
        return out @ Wout + bout

    def _L2_ffn_ref(x, W1, b1, W2, b2):
        import jax, jax.numpy as jnp
        import numpy as np
        EMB = 128
        FF = 4 * EMB

        def _ternary(w):
            scale = jnp.maximum(jnp.mean(jnp.abs(w)), 1e-08)
            w_t = jnp.clip(jnp.round(w / scale), -1.0, 1.0)
            return w + jax.lax.stop_gradient(w_t - w)
        h = jnp.einsum('bsd,fd->bsf', x, _ternary(W1)) + b1
        h = jax.nn.gelu(h, approximate=False)
        out = jnp.einsum('bsf,df->bsd', h, _ternary(W2)) + b2
        return out

    def _L3_attn_ref(x, W_kv, g_kv, W_kdec, W_vdec, W_q, W_qdec, W_krope, W_qrope, W_o):
        import jax, jax.numpy as jnp
        import numpy as np
        N_EMBD = 128
        N_HEAD = 16
        HEAD_DIM = N_EMBD // N_HEAD
        KV_RANK = 32
        Q_RANK = 64
        ROPE_DIM = 32
        B, T = (2, 256)
        EPS = 1e-06

        def _rope_tables(T, dim):
            inv_freq = 1.0 / 10000.0 ** (np.arange(0, dim, 2, dtype=np.float32) / dim)
            t = np.arange(T, dtype=np.float32)
            freqs = np.outer(t, inv_freq)
            emb = np.concatenate([freqs, freqs], -1)
            return (jnp.asarray(np.cos(emb)), jnp.asarray(np.sin(emb)))

        def _apply_rope(x, cos, sin):
            d2 = x.shape[-1] // 2
            x1, x2 = (x[..., :d2], x[..., d2:])
            rot = jnp.concatenate([-x2, x1], axis=-1)
            return x * cos[None, None, :, :] + rot * sin[None, None, :, :]
        Bx, Tx, C = x.shape
        kv_c = x @ W_kv
        kv_c = kv_c * jax.lax.rsqrt(jnp.mean(kv_c * kv_c, axis=-1, keepdims=True) + EPS) * g_kv
        q_c = x @ W_q

        def heads(y, d):
            return y.reshape(Bx, Tx, N_HEAD, d).transpose(0, 2, 1, 3)
        k_content = heads(kv_c @ W_kdec, HEAD_DIM)
        v = heads(kv_c @ W_vdec, HEAD_DIM)
        q_content = heads(q_c @ W_qdec, HEAD_DIM)
        k_rope = heads(x @ W_krope, ROPE_DIM)
        q_rope = heads(q_c @ W_qrope, ROPE_DIM)
        cos, sin = _rope_tables(Tx, ROPE_DIM)
        q_rope = _apply_rope(q_rope, cos, sin)
        k_rope = _apply_rope(k_rope, cos, sin)
        q = jnp.concatenate([q_content, q_rope], axis=-1)
        k = jnp.concatenate([k_content, k_rope], axis=-1)
        scale = 1.0 / jnp.sqrt(jnp.float32(q.shape[-1]))
        scores = jnp.einsum('bhqd,bhkd->bhqk', q, k) * scale
        causal = jnp.tril(jnp.ones((Tx, Tx), dtype=bool))
        scores = jnp.where(causal[None, None], scores, jnp.float32(-jnp.inf))
        attn = jax.nn.softmax(scores, axis=-1)
        out = jnp.einsum('bhqk,bhkd->bhqd', attn, v)
        out = out.transpose(0, 2, 1, 3).reshape(Bx, Tx, N_HEAD * HEAD_DIM)
        return out @ W_o

    def _L3_ffn_ref(x, w_freq_real, w_freq_imag, bias):
        import jax, jax.numpy as jnp
        import numpy as np
        B, N, D = (4, 256, 128)
        SPARSITY = 0.01
        w = jax.lax.complex(w_freq_real, w_freq_imag)
        x_freq = jnp.fft.fft(x, axis=-1)
        y_freq = jnp.einsum('bnd,do->bno', x_freq, w)
        y = jnp.real(jnp.fft.ifft(y_freq, axis=-1))
        return y + bias
    x = L0_attn_hidden_states
    xn = _layernorm(x, axis=-1)
    s = _L0_attn_ref(xn, L0_attn_alpha, L0_attn_fc_w, L0_attn_fc_b, L0_attn_fc_r_w, L0_attn_fc_r_b, L0_attn_fc_i_w, L0_attn_fc_i_b, L0_attn_fc_gate_w, L0_attn_fc_gate_b, L0_attn_norm_w, L0_attn_norm2_w, L0_attn_mlp_gate_w, L0_attn_mlp_gate_b, L0_attn_mlp_fc_w, L0_attn_mlp_fc_b, L0_attn_out_w, L0_attn_out_b)
    g = _silu(_L0_ffn_ref(xn, L0_ffn_wqkv, L0_ffn_q_scale, L0_ffn_k_scale, L0_ffn_wo, L0_ffn_ln_g, L0_ffn_ln_b, L0_ffn_w1, L0_ffn_b1, L0_ffn_w2, L0_ffn_b2))
    x = x + s * g
    xn = _layernorm(x, axis=-1)
    s = _L1_attn_ref(xn, L1_attn_w_attn, L1_attn_w_proj)
    g = _silu(_L1_ffn_ref(xn, L1_ffn_Wg, L1_ffn_bg, L1_ffn_W1, L1_ffn_b1, L1_ffn_W2, L1_ffn_b2))
    x = x + s * g
    xn = _layernorm(x, axis=-1)
    s = _L2_attn_ref(xn, L2_attn_Wqa, L2_attn_Wqb, L2_attn_Wkva, L2_attn_Wkvb, L2_attn_Wout, L2_attn_bout)
    g = _silu(_L2_ffn_ref(xn, L2_ffn_W1, L2_ffn_b1, L2_ffn_W2, L2_ffn_b2))
    x = x + s * g
    xn = _layernorm(x, axis=-1)
    s = _L3_attn_ref(xn, L3_attn_W_kv, L3_attn_g_kv, L3_attn_W_kdec, L3_attn_W_vdec, L3_attn_W_q, L3_attn_W_qdec, L3_attn_W_krope, L3_attn_W_qrope, L3_attn_W_o)
    g = _silu(_L3_ffn_ref(xn, L3_ffn_w_freq_real, L3_ffn_w_freq_imag, L3_ffn_bias))
    x = x + s * g
    return x

_drawn_inputs = setup_inputs


def setup_inputs(seed=0):
    import zlib

    import numpy as np

    out = dict(_drawn_inputs(seed))
    spreads = {'L0_attn_norm_w': (1.0, 0.6),
     'L0_attn_norm2_w': (1.0, 0.6),
     'L0_ffn_q_scale': (1.0, 0.6),
     'L0_ffn_k_scale': (1.0, 0.6),
     'L0_ffn_ln_g': (1.0, 0.6),
     'L0_ffn_ln_b': (0.0, 0.8),
     'L0_ffn_b1': (0.0, 0.8),
     'L0_ffn_b2': (0.0, 0.379),
     'L3_attn_g_kv': (1.0, 0.6)}
    factors = {'L0_attn_alpha': 64.0,
     'L0_attn_fc_b': 8.0,
     'L0_attn_fc_r_w': 8.0,
     'L0_attn_fc_r_b': 27.498,
     'L0_attn_fc_i_w': 4.736,
     'L0_attn_fc_i_b': 8.0,
     'L0_attn_fc_gate_b': 8.0,
     'L0_attn_mlp_gate_b': 8.0,
     'L0_attn_mlp_fc_b': 8.0,
     'L0_attn_out_b': 4.834,
     'L0_ffn_wqkv': 3.395,
     'L0_ffn_wo': 3.326,
     'L0_ffn_w1': 5.884,
     'L0_ffn_w2': 5.523,
     'L1_ffn_bg': 64.0,
     'L1_ffn_b1': 64.0,
     'L1_ffn_b2': 64.0,
     'L2_attn_Wqa': 64.0,
     'L2_attn_Wqb': 64.0,
     'L2_ffn_b1': 58.199,
     'L2_ffn_b2': 200.0,
     'L3_attn_W_kdec': 54.512,
     'L3_attn_W_q': 33.926,
     'L3_attn_W_qdec': 53.096,
     'L3_attn_W_krope': 41.384,
     'L3_attn_W_qrope': 41.4,
     'L3_ffn_bias': 200.0,
     'L1_attn_w_attn': 3.428,
     'L1_attn_w_proj': 3.306,
     'L1_ffn_Wg': 3.623,
     'L1_ffn_W1': 4.084,
     'L1_ffn_W2': 3.482,
     'L2_attn_Wkva': 5.212,
     'L2_attn_Wkvb': 4.17,
     'L2_attn_Wout': 5.133,
     'L2_attn_bout': 2.672,
     'L3_attn_W_kv': 8.0,
     'L3_attn_W_vdec': 7.787,
     'L3_attn_W_o': 7.773,
     'L3_ffn_w_freq_real': 8.0,
     'L3_ffn_w_freq_imag': 8.0}
    for name, (base, spread) in spreads.items():
        noise = np.random.default_rng([zlib.crc32(name.encode()), seed]).standard_normal(out[name].shape)
        drawn = base * np.exp(spread * noise) if base else spread * noise
        out[name] = jnp.asarray(drawn.astype(out[name].dtype))
    for name, factor in factors.items():
        out[name] = (out[name] * factor).astype(out[name].dtype)
    return out
```

```python
from contextlib import ExitStack

import numpy as np

import concourse.bass as bass
from concourse import mybir

ALU = mybir.AluOpType
ACT = mybir.ActivationFunctionType
AX = mybir.AxisListType
F32 = mybir.dt.float32
BF16 = mybir.dt.bfloat16

P = 128
B, L = 16, 256
N = B * L
TILE = 512
NT = N // TILE
U = 4
H16, D8 = 16, 8
H8, D64 = 8, 64
HID = 341
HCH = [(0, 128), (128, 128), (256, HID - 256)]
FCH = [(0, 128), (128, 128), (256, 128)]
NEXP, EH = 8, 512
BIG = -1e30
CREDIT = 3


def const_cast():
    i = np.arange(P)
    ident = np.eye(P)
    causal = np.where(i[None, :] <= i[:, None], 0.0, BIG)
    band = lambda q, k: np.where((q - k >= 0) & (q - k <= 64), 0.0, BIG)
    q, k, j = i[:, None], i[None, :], np.arange(192)[None, :]
    local_q0 = band(q, k)
    local_q1 = band(q + 128, j + 64)
    local_k0 = band(j, i[:, None])
    sel = np.zeros((P, H16, P))
    for h in range(H16):
        sel[h, h] = sel[32 + h, h] = 1.0
    parts = [("ident", ident), ("causal_q", causal), ("causal_k", causal.T), ("local_q0", local_q0),
             ("local_q1", local_q1), ("local_k0", local_k0), ("sel", sel.reshape(P, -1))]
    return parts


def const_f32():
    c = np.arange(P)
    blk = (c[:, None] // 64 == c[None, :] // 64).astype(np.float64)
    return [("centre", np.eye(P) - 1.0 / P), ("mean", np.full((P, P), 1.0 / P)), ("block64", blk), ("identf", np.eye(P)),
            ("mean32", np.full((P, 32), 1.0 / 32)), ("ones", np.ones((P, P)))]


def const_local_rope():
    half = np.arange(0, D64, 2, dtype=np.float32)
    inv = np.float32(1.0) / np.float32(10000.0) ** (half / np.float32(D64))
    t = np.arange(L, dtype=np.float32)
    fr = (t[:, None] * inv[None, :]).astype(np.float32).astype(np.float64)
    fr = np.concatenate([fr, fr], -1).T
    base = (half.astype(np.float64) + 0.4 * D64) / (1.4 * D64)
    power = (t.astype(np.float64) - L // 2) / 32.0
    sc = base[None, :] ** power[:, None]
    sc = np.concatenate([sc, sc], -1).T
    sign = np.where(np.arange(D64) < 32, -1.0, 1.0)[:, None]
    two = lambda a: np.concatenate([a, a], 0)
    return [("qa", two(np.cos(fr) * sc)), ("qb", two(sign * np.sin(fr) * sc)),
            ("ka", two(np.cos(fr) / sc)), ("kb", two(sign * np.sin(fr) / sc))]


def const_rope8():
    inv = np.float32(1.0) / np.float32(10000.0) ** (np.arange(0, D8, 2, dtype=np.float32) / np.float32(D8))
    fr = np.outer(np.arange(L, dtype=np.float32), inv).astype(np.float32).astype(np.float64)
    d = np.arange(P) // H16
    cos, sin = np.cos(fr)[:, d // 2].T, np.sin(fr)[:, d // 2].T
    return [("cos", cos), ("sin", np.where(d % 2 == 0, -1.0, 1.0)[:, None] * sin)]


def const_rope32():
    inv = np.float32(1.0) / np.float32(10000.0) ** (np.arange(0, 32, 2, dtype=np.float32) / np.float32(32))
    fr = np.outer(np.arange(L, dtype=np.float32), inv).astype(np.float32).astype(np.float64)
    cos, sin = [], []
    for c in range(2):
        d = 8 * c + np.arange(P) // H16
        cos += [np.cos(fr)[:, d].T] * 2
        sin += [-np.sin(fr)[:, d].T, np.sin(fr)[:, d].T]
    return [("cos", np.concatenate(cos, 1)), ("sin", np.concatenate(sin, 1))]


def const_dft():
    a = 2 * np.pi * (np.outer(np.arange(P), np.arange(P)) % P) / P
    return [("dc", np.cos(a)), ("ds", np.sin(a)), ("dsn", -np.sin(a)), ("dcm", np.cos(a) / P), ("dsm", -np.sin(a) / P)]


def const_alibi():
    slopes = np.array([(2.0 ** -0.5) ** (h + 1) for h in range(H16)])
    v = (slopes[:, None] * np.sqrt(8.0) * np.arange(L)[None, :]).astype(np.float32)

    def bf(a):
        u = a.astype(np.float32).view(np.uint32)
        u = (u + 0x7FFF + ((u >> 16) & 1)) & np.uint32(0xFFFF0000)
        return u.view(np.float32)

    hi = bf(v)
    mid = bf(v - hi)
    lo = v - hi - mid
    rows = np.stack([hi, mid, lo]).reshape(3, -1)
    ones = np.ones_like(rows)
    return np.concatenate([ones, -rows], 0), np.concatenate([rows, ones], 0)


def widths(parts):
    at, where = 0, {}
    for name, n in parts:
        where[name] = (at, n)
        at += n
    return where, at


CAST = widths([(n, a.shape[1]) for n, a in const_cast()])
CONF = widths([(n, a.shape[1]) for n, a in const_f32()])
DH = [d * 1 + h * D8 for d in range(D8) for h in range(H16)]
W_L0A = widths([("fc", P), ("fr", P), ("fi", P), ("gate", P), ("mg", 3 * P), ("mf", 3 * P), ("mo", 3 * P), ("fc_b", 1),
                ("fr_b", 1), ("fi_b", 1), ("gate_b", 1), ("norm", 1), ("norm2", 1), ("alpha", 1), ("mo_b", 1),
                ("mg_b", 3), ("mf_b", 3)])
W_L0F = widths([("wq", 512), ("wqr", 512), ("wk", 512), ("wkr", 512), ("wv", 512), ("wo", 512), ("w1", 2 * HID),
                ("w2", 3 * P), ("qs", 1), ("qsr", 1), ("ks", 1), ("ksr", 1), ("lg", 1), ("lb", 1), ("b1a", 3),
                ("b1g", 3), ("b2", 1)])
W_L0T = widths([("qa", L), ("qb", L), ("ka", L), ("kb", L)])
W_L1 = widths([("wq", P), ("wk", P), ("wv", P), ("wo", P)])
W_MOE = widths([("wg", NEXP), ("bg", NEXP), ("w1", NEXP * EH), ("w2", NEXP * EH), ("b1", NEXP * 4), ("b2", P)])
W_L2 = widths([("qaT", P), ("qb", P), ("qbr", P), ("kvaT", P), ("kb", P), ("kbr", P), ("vb", P), ("wo", P), ("bo", 1),
               ("cos", L), ("sin", L), ("f1", 512), ("f1b", 4), ("f2", 512), ("f2b", 1)])
W_L3 = widths([("wkv", 32), ("gkv", 1), ("kd", P), ("vd", P), ("qT", P), ("qd", P), ("qr", 512), ("kr", 512), ("wo", P),
               ("cos", 4 * L), ("sin", 4 * L), ("dc", P), ("ds", P), ("dsn", P), ("dcm", P), ("dsm", P), ("fr", P),
               ("fi", P), ("fb", 1)])


def pack(tile, where):
    def part(name, lo=0, n=None, rows=P):
        at, width = where[name]
        n = width - lo if n is None else n
        return tile[0:rows, at + lo:at + lo + n]
    return part


class Core:
    pass


def at_least(eng, sem, value):
    if isinstance(value, int) and value <= 0:
        return
    eng.wait_ge(sem, value)


def tok(t, n=TILE):
    return bass.ds(t * n, n)


def layer_norm(k, call, src, dst, shift=False, affine=None):
    nc, s = k.nc, k.s
    base = call * NT
    with ExitStack() as ctx:
        sq = ctx.enter_context(nc.sbuf_tensor(f"ln_sq{call}", [P, U, TILE], F32))
        rs = ctx.enter_context(nc.sbuf_tensor(f"ln_rs{call}", [P, U, TILE], F32))
        y2 = ctx.enter_context(nc.sbuf_tensor(f"ln_y2{call}", [P, U, TILE], F32))
        hs = ctx.enter_context(nc.sbuf_tensor(f"ln_hs{call}", [P, U, TILE], F32)) if shift else None
        block = ctx.enter_context(nc.Block())

        if shift:
            @block.gpsimd
            def _(pool):
                rows = hs[64:128, :, :].rearrange("p u (b l) -> p (u b) l", l=L)
                nc.gpsimd.memset(rows[:, :, 0:1], 0.0).then_inc(s.ln_zero, 1)
                pool.wait_ge(s.ln_zero, k.shifts + 1)
                with pool.Fori(0, NT // U) as turn:
                    i = turn * U
                    for u in range(U):
                        t = i + u
                        pool.wait_ge(s.ln_free, base + t + 1)
                        nc.gpsimd.tensor_copy(hs[0:64, u, :], src[0:64, tok(t)])
                        nc.gpsimd.tensor_copy(hs[64:128, u, :].rearrange("p (b l) -> p b l", l=L)[:, :, 1:L],
                                              src[64:128, tok(t)].rearrange("p (b l) -> p b l", l=L)[:, :, 0:L - 1]
                                              ).then_inc(s.ln_shifted, 1)

        @block.tensor
        def _(pe):
            with pe.Fori(0, NT // U) as turn:
                i = turn * U
                for u in range(U):
                    t = i + u
                    pe.wait_ge(s.ln_free, base + t + 1)
                    if shift:
                        pe.wait_ge(s.ln_shifted, k.shifts * NT + t + 1)
                    x = hs[:, u, :] if shift else src[:, tok(t)]
                    nc.tensor.matmul(k.ps[:, u, :], k.cf("centre"), x, start=True, stop=True).then_inc(s.ln_centred, 1)
                for u in range(U):
                    pe.wait_ge(s.ln_squared, base + i + u + 1)
                    nc.tensor.matmul(k.ps[:, U + u, :], k.cf("mean"), sq[:, u, :], start=True, stop=True
                                     ).then_inc(s.ln_var, 1)

        @block.scalar
        def _(act):
            with act.Fori(0, NT // U) as turn:
                i = turn * U
                for u in range(U):
                    act.wait_ge(s.ln_centred, base + i + u + 1)
                    nc.scalar.activation(sq[:, u, :], k.ps[:, u, :], ACT.Square).then_inc(s.ln_squared, 1)
                for u in range(U):
                    act.wait_ge(s.ln_var, base + i + u + 1)
                    nc.scalar.activation(rs[:, u, :], k.ps[:, U + u, :], ACT.Abs_reciprocal_sqrt, bias=k.eps5[:, 0:1]
                                         ).then_inc(s.ln_rstd, 1)
                for u in range(U):
                    act.wait_ge(s.ln_rstd, base + i + u + 1)
                    nc.scalar.activation(y2[:, u, :], rs[:, u, :], ACT.Square).then_inc(s.ln_rstd2, 1)

        @block.vector
        def _(dve):
            with dve.Fori(0, NT // U) as turn:
                i = turn * U
                for u in range(U):
                    dve.wait_ge(s.ln_rstd2, base + i + u + 1)
                    nc.vector.scalar_tensor_tensor(out=y2[:, u, :], in0=k.ps[:, U + u, :], scalar=1e-5, in1=y2[:, u, :],
                                                   op0=ALU.add, op1=ALU.mult).then_inc(s.ln_vy2, 1)
                for u in range(U):
                    dve.wait_ge(s.ln_vy2, base + i + u + 1)
                    nc.vector.scalar_tensor_tensor(out=rs[:, u, :], in0=y2[:, u, :], scalar=-3.0, in1=rs[:, u, :],
                                                   op0=ALU.add, op1=ALU.mult).then_inc(s.ln_exact, 1)
                for u in range(U):
                    t = i + u
                    dve.wait_ge(s.ln_exact, base + t + 1)
                    nc.vector.scalar_tensor_tensor(out=dst[:, tok(t)], in0=rs[:, u, :], scalar=-0.5, in1=k.ps[:, u, :],
                                                   op0=ALU.mult, op1=ALU.mult).then_inc(s.ln_free, 1)
                    if affine:
                        dve.wait_ge(s.ln_free, base + U + t + 1)
                        nc.vector.tensor_scalar(dst[:, tok(t)], dst[:, tok(t)], affine[0], affine[1],
                                                ALU.mult, ALU.add).then_inc(s.ln_affine, 1)
    if shift:
        k.shifts += 1


def rms_norm(k, call, src, dst, weight, rows=P, mean="mean", before=None):
    nc, s = k.nc, k.s
    base = call * NT
    with ExitStack() as ctx:
        sq = ctx.enter_context(nc.sbuf_tensor(f"rms_sq{call}", [P, U, TILE], F32))
        rs = ctx.enter_context(nc.sbuf_tensor(f"rms_rs{call}", [P, U, TILE], F32))
        y2 = ctx.enter_context(nc.sbuf_tensor(f"rms_y2{call}", [P, U, TILE], F32))
        wh = ctx.enter_context(nc.sbuf_tensor(f"rms_wh{call}", [P, 1], F32))
        block = ctx.enter_context(nc.Block())

        @block.tensor
        def _(pe):
            with pe.Fori(0, NT // U) as turn:
                i = turn * U
                if before:
                    for u in range(U):
                        pe.wait_ge(s.rms_free, base + i + u + 1)
                        nc.tensor.matmul(k.ps[0:rows, u, :], before[0], before[1][:, tok(i + u)], start=True, stop=True
                                         ).then_inc(s.rms_product, 1)
                for u in range(U):
                    pe.wait_ge(s.rms_squared, base + i + u + 1)
                    pe.nop(nofuse=True)
                    nc.tensor.matmul(k.ps[0:rows, U + u, :], k.cf(mean, rows=rows, n=rows), sq[0:rows, u, :],
                                     start=True, stop=True).then_inc(s.rms_mean, 1)

        @block.scalar
        def _(act):
            with act.Fori(0, NT // U) as turn:
                i = turn * U
                for u in range(U):
                    act.wait_ge(s.rms_free, base + i + u + 1)
                    if before:
                        act.wait_ge(s.rms_product, i + u + 1)
                    x = k.ps[0:rows, u, :] if before else src[:, tok(i + u)]
                    nc.scalar.activation(sq[0:rows, u, :], x, ACT.Square).then_inc(s.rms_squared, 1)
                for u in range(U):
                    act.wait_ge(s.rms_mean, base + i + u + 1)
                    nc.scalar.activation(rs[0:rows, u, :], k.ps[0:rows, U + u, :], ACT.Abs_reciprocal_sqrt,
                                         bias=k.eps6[0:rows, 0:1]).then_inc(s.rms_rstd, 1)
                for u in range(U):
                    act.wait_ge(s.rms_rstd, base + i + u + 1)
                    nc.scalar.activation(y2[0:rows, u, :], rs[0:rows, u, :], ACT.Square).then_inc(s.rms_rstd2, 1)

        @block.vector
        def _(dve):
            nc.vector.tensor_scalar(wh[0:rows, :], weight, -0.5, None, ALU.mult).then_inc(s.rms_weight, 1)
            dve.wait_ge(s.rms_weight, call + 1)
            with dve.Fori(0, NT // U) as turn:
                i = turn * U
                for u in range(U):
                    dve.wait_ge(s.rms_rstd2, base + i + u + 1)
                    nc.vector.scalar_tensor_tensor(out=y2[0:rows, u, :], in0=k.ps[0:rows, U + u, :], scalar=1e-6,
                                                   in1=y2[0:rows, u, :], op0=ALU.add, op1=ALU.mult).then_inc(s.rms_vy2, 1)
                for u in range(U):
                    dve.wait_ge(s.rms_vy2, base + i + u + 1)
                    nc.vector.scalar_tensor_tensor(out=rs[0:rows, u, :], in0=y2[0:rows, u, :], scalar=-3.0,
                                                   in1=rs[0:rows, u, :], op0=ALU.add, op1=ALU.mult).then_inc(s.rms_exact, 1)
                for u in range(U):
                    dve.wait_ge(s.rms_exact, base + i + u + 1)
                    x = k.ps[0:rows, u, :] if before else src[:, tok(i + u)]
                    nc.vector.scalar_tensor_tensor(out=dst[0:rows, tok(i + u)], in0=x, scalar=wh[0:rows, :],
                                                   in1=rs[0:rows, u, :], op0=ALU.mult, op1=ALU.mult
                                                   ).then_inc(s.rms_free, 1)


def feed_forward(k, call, units, src, chunks, gate_w, gate_b, value_w, value_b, out_w, out_b, resid, dst):
    nc, s = k.nc, k.s
    nch = len(chunks)
    base = call * NT
    RH = 3 if value_w else 4
    with ExitStack() as ctx:
        gl = ctx.enter_context(nc.sbuf_tensor(f"ff_gl{call}", [P, RH, TILE], F32))
        hid = ctx.enter_context(nc.sbuf_tensor(f"ff_hid{call}", [P, RH, TILE], F32))
        block = ctx.enter_context(nc.Block())
        seq = [(u, c) for u in range(U) for c in range(nch)]

        @block.tensor
        def _(pe):
            with pe.Fori(0, NT // U) as turn:
                i = turn * U
                def outs(n):
                    u, c = seq[n]
                    unit = units + i * nch + n
                    pe.wait_ge(s.ff_value_used if value_w else s.ff_gelu, unit + 1 + CREDIT)
                    if c == 0:
                        pe.wait_ge(s.ff_out_used, base + i + u + 1)
                    lo, w = chunks[c]
                    m = nc.tensor.matmul(k.ps[:, 6 + u % 2, :], out_w(c, w), hid[0:w, n % RH, :],
                                         start=(c == 0), stop=(c == nch - 1))
                    m.then_inc(s.ff_hid_used, 1)
                for n, (u, c) in enumerate(seq):
                    lo, w = chunks[c]
                    unit = units + i * nch + n
                    pe.wait_ge(s.ff_gelu, unit + 1)
                    x = src[:, tok(i + u)]
                    nc.tensor.matmul(k.ps[0:w, n % RH, :], gate_w(lo, w), x, start=True, stop=True
                                     ).then_inc(s.ff_gate, 1)
                    if value_w:
                        pe.wait_ge(s.ff_value_used, unit + 1)
                        nc.tensor.matmul(k.ps[0:w, 3 + n % RH, :], value_w(lo, w), x, start=True, stop=True
                                         ).then_inc(s.ff_value, 1)
                    if n >= 2:
                        outs(n - 2)
                outs(len(seq) - 2)
                outs(len(seq) - 1)

        @block.scalar
        def _(act):
            with act.Fori(0, NT // U) as turn:
                i = turn * U
                for n, (u, c) in enumerate(seq):
                    lo, w = chunks[c]
                    unit = units + i * nch + n
                    act.wait_ge(s.ff_gate, unit + 1)
                    if value_w:
                        act.wait_ge(s.ff_value_used, unit + 1)
                        to = gl[0:w, n % RH, :]
                    else:
                        act.wait_ge(s.ff_hid_used, unit + 1)
                        to = hid[0:w, n % RH, :]
                    g = nc.scalar.activation(to, k.ps[0:w, n % RH, :], ACT.Gelu, bias=gate_b(c, w))
                    g.then_inc(s.ff_gelu, 1)

        @block.vector
        def _(dve):
            with dve.Fori(0, NT // U) as turn:
                i = turn * U
                def finish(u):
                    t = i + u
                    dve.wait_ge(s.ff_hid_used, units + (t + 1) * nch + CREDIT)
                    if resid is None:
                        m = nc.vector.tensor_scalar(dst[:, tok(t)], k.ps[:, 6 + u % 2, :], out_b, None, ALU.add)
                    else:
                        m = nc.vector.scalar_tensor_tensor(out=dst[:, tok(t)], in0=k.ps[:, 6 + u % 2, :], scalar=out_b,
                                                           in1=resid[:, tok(t)], op0=ALU.add, op1=ALU.add)
                    m.then_inc(s.ff_out_used, 1)
                for n, (u, c) in enumerate(seq):
                    lo, w = chunks[c]
                    unit = units + i * nch + n
                    if value_w:
                        dve.wait_ge(s.ff_gelu, unit + 1 + CREDIT)
                        dve.wait_ge(s.ff_value, unit + 1)
                        dve.wait_ge(s.ff_hid_used, unit + 1)
                        nc.vector.scalar_tensor_tensor(out=hid[0:w, n % RH, :], in0=k.ps[0:w, 3 + n % RH, :],
                                                       scalar=value_b(c, w), in1=gl[0:w, n % RH, :],
                                                       op0=ALU.add, op1=ALU.mult).then_inc(s.ff_value_used, 1)
                    if c == nch - 1 and u >= 1:
                        finish(u - 1)
                finish(U - 1)


def recurrent_mixer(k, w, work):
    nc, s = k.nc, k.s
    XN, S, Y = k.XN, k.S, k.Y
    Hb, GT = work
    R, Uv = Y, S
    rms_norm(k, 0, XN, Hb, w("norm"))

    with ExitStack() as ctx:
        ig = ctx.enter_context(nc.sbuf_tensor("mix_i", [P, 2, TILE], F32))
        block = ctx.enter_context(nc.Block())

        @block.tensor
        def _(pe):
            with pe.Fori(0, NT // 2) as turn:
                i = turn * 2
                for u in range(2):
                    pe.wait_ge(s.mix_used, i + u + 1)
                    for n, name in enumerate(("fr", "fi", "fc")):
                        nc.tensor.matmul(k.ps[:, 2 * n + u, :], w(name), Hb[:, tok(i + u)], start=True, stop=True
                                         ).then_inc(s.mix_product, 1)

        @block.scalar
        def _(act):
            with act.Fori(0, NT // 2) as turn:
                i = turn * 2
                for u in range(2):
                    act.wait_ge(s.mix_product, 3 * (i + u) + 2)
                    nc.scalar.activation(R[:, tok(i + u)], k.ps[:, u, :], ACT.Sigmoid, bias=w("fr_b"))
                    nc.scalar.activation(ig[:, u, :], k.ps[:, 2 + u, :], ACT.Sigmoid, bias=w("fi_b")
                                         ).then_inc(s.mix_sigmoid, 1)

        @block.vector
        def _(dve):
            with dve.Fori(0, NT // 2) as turn:
                i = turn * 2
                for u in range(2):
                    dve.wait_ge(s.mix_sigmoid, i + u + 1)
                    dve.wait_ge(s.mix_product, 3 * (i + u) + 3)
                    nc.vector.scalar_tensor_tensor(out=Uv[:, tok(i + u)], in0=k.ps[:, 4 + u, :], scalar=w("fc_b"),
                                                   in1=ig[:, u, :], op0=ALU.add, op1=ALU.mult).then_inc(s.mix_used, 1)

    with ExitStack() as ctx:
        a2 = ctx.enter_context(nc.sbuf_tensor("mix_a2", [P, 2 * TILE], F32))
        sp = ctx.enter_context(nc.sbuf_tensor("mix_sp", [P, 6], F32))
        block = ctx.enter_context(nc.Block())
        NC = N // (2 * TILE)

        @block.tensor
        def _(pe):
            for t in range(NT):
                nc.tensor.matmul(k.ps[:, t, :], w("gate"), Hb[:, t * TILE:(t + 1) * TILE], start=True, stop=True
                                 ).then_inc(s.gate_product, 1)

        @block.scalar
        def _(act):
            nc.scalar.activation(sp[:, 0:1], w("alpha"), ACT.Abs).then_inc(s.sp_step, 1)
            act.wait_ge(s.sp_step, 1)
            nc.scalar.activation(sp[:, 1:2], sp[:, 0:1], ACT.Exp, scale=-1.0).then_inc(s.sp_step, 1)
            act.wait_ge(s.sp_step, 2)
            nc.scalar.activation(sp[:, 2:3], sp[:, 1:2], ACT.Ln, bias=k.cf("ones", n=1)).then_inc(s.sp_step, 1)
            act.wait_ge(s.sp_coef, 1)
            for c in range(NC):
                cols = slice(c * 2 * TILE, (c + 1) * 2 * TILE)
                nc.scalar.activation(R[:, cols], R[:, cols], ACT.Exp, scale=sp[:, 4:5]).then_inc(s.decay, 1)
            for c in range(NC):
                act.wait_ge(s.decay2, c + 1)
                nc.scalar.activation(a2[:], a2[:], ACT.Sqrt, scale=-1.0, bias=k.cf("ones", n=1)).then_inc(s.keep, 1)
            for t in range(NT):
                act.wait_ge(s.gate_product, t + 1)
                nc.scalar.activation(GT[:, t * TILE:(t + 1) * TILE], k.ps[:, t, :], ACT.Gelu, bias=w("gate_b")
                                     ).then_inc(s.gate_ready, 1)

        @block.vector
        def _(dve):
            nc.vector.tensor_scalar(sp[:, 3:4], w("alpha"), 0.0, None, ALU.max).then_inc(s.sp_max, 1)
            dve.wait_ge(s.sp_max, 1)
            dve.wait_ge(s.sp_step, 3)
            nc.vector.tensor_tensor(sp[:, 5:6], sp[:, 3:4], sp[:, 2:3], ALU.add).then_inc(s.sp_max, 1)
            dve.wait_ge(s.sp_max, 2)
            nc.vector.tensor_scalar(sp[:, 4:5], sp[:, 5:6], -8.0, None, ALU.mult).then_inc(s.sp_coef, 1)
            for c in range(NC):
                cols = slice(c * 2 * TILE, (c + 1) * 2 * TILE)
                dve.wait_ge(s.decay, c + 1)
                at_least(dve, s.scaled, c)
                nc.vector.tensor_tensor(a2[:], R[:, cols], R[:, cols], ALU.mult).then_inc(s.decay2, 1)
                dve.wait_ge(s.decay2, c + 1)
                nc.vector.memset(R[:, cols].rearrange("p (b l) -> p b l", l=L)[:, :, 0:1], 0.0).then_inc(s.reset, 1)
                dve.wait_ge(s.keep, c + 1)
                nc.vector.tensor_tensor(Uv[:, cols], Uv[:, cols], a2[:], ALU.mult).then_inc(s.scaled, 1)
                dve.wait_ge(s.scaled, c + 1)
                dve.wait_ge(s.reset, c + 1)
                nc.vector.tensor_tensor_scan(Uv[:, cols], R[:, cols], Uv[:, cols], 0.0, ALU.mult, ALU.add
                                             ).then_inc(s.scanned, 1)
            for t in range(NT):
                cols = slice(t * TILE, (t + 1) * TILE)
                dve.wait_ge(s.scanned, t // 2 + 1)
                dve.wait_ge(s.gate_ready, t + 1)
                nc.vector.tensor_tensor(Uv[:, cols], Uv[:, cols], GT[:, cols], ALU.mult).then_inc(s.gated, 1)
            for t in range(NT):
                cols = slice(t * TILE, (t + 1) * TILE)
                dve.wait_ge(s.gated, t + 1)
                nc.vector.tensor_tensor(Uv[:, cols], Uv[:, cols], XN[:, cols], ALU.add).then_inc(s.hs2, 1)

    rms_norm(k, 1, Uv, Hb, w("norm2"))
    feed_forward(k, 0, 0, Hb, FCH, lambda lo, n: w("mg", lo, n), lambda c, n: w("mg_b", c, 1),
                 lambda lo, n: w("mf", lo, n), lambda c, n: w("mf_b", c, 1),
                 lambda c, n: w("mo", c * P, P), w("mo_b"), S, S)


def rows_pipeline(eng, step, tail, slots):
    first = 2 * slots
    last = first + (B - 1 - first) // slots * slots
    for i in range(first):
        step(i, i % slots)
    with eng.Fori(2, last // slots) as turn:
        for n in range(slots):
            step(turn * slots + n, n)
    for i in range(last, B + tail):
        step(i, i % slots)


def live(i, lag):
    return not isinstance(i, int) or 0 <= i - lag < B


def local_attention(k, layer, w, rope, X0, Yd):
    nc, s, ps = k.nc, k.s, k.ps
    row0 = layer * B
    W65 = D64 + 1
    NS = 3
    with ExitStack() as ctx:
        sb = lambda n, shape, dt=F32: ctx.enter_context(nc.sbuf_tensor(f"la{layer}_{n}", shape, dt))
        hs = sb("hs", [P, NS, L])
        tab = sb("tab", [P, 4, L])
        QK = sb("qk", [P, NS, 2, 4, L])
        V = sb("v", [P, NS, 2, H8, W65])
        sq = sb("sq", [P, 2, L])
        vc = sb("vc", [P, 4, L])
        rn = sb("rn", [P, 4, L])
        y2 = sb("y2", [P, 4, L])
        ta = sb("ta", [P, 2, L])
        tb = sb("tb", [P, 2, L])
        tc = sb("tc", [P, 2, 4, L])
        nm = sb("nm", [P, 2, H8])
        nb = sb("nb", [P, 2, H8], BF16)
        m2 = sb("m2", [P, 2, P])
        mT = sb("mt", [P, 2, P], BF16)
        pr = sb("pr", [P, 2, 320])
        rec = sb("rec", [P, 2, 2])
        ot = sb("ot", [P, NS, 2, 4, P])
        oT = sb("oT", [P, 4, L])
        block = ctx.enter_context(nc.Block())

        @block.gpsimd
        def _(pool):
            nc.gpsimd.memset(V[:, :, :, :, D64:W65], 1.0).then_inc(s.la_init, 1)
            nc.gpsimd.memset(m2[:], 0.0).then_inc(s.la_init, 1)
            pool.wait_ge(s.la_init, 3 * layer + 2)
            nc.gpsimd.memset(hs[64:128, :, 0:1], 0.0).then_inc(s.la_init, 1)
            pool.wait_ge(s.la_init, 3 * layer + 3)

            def shift(i, n):
                at_least(pool, s.la_vprod, 2 * (row0 + i - NS + 1) if live(i, NS) else 0)
                nc.gpsimd.tensor_copy(hs[0:64, n, :], X0[0:64, bass.ds(i * L, L)])
                nc.gpsimd.tensor_copy(hs[64:128, n, 1:L], X0[64:128, bass.ds(i * L, L - 1)]).then_inc(s.la_shifted, 1)
                pool.wait_ge(s.la_shifted, row0 + i + 1)

            def step(i, n):
                b = row0 + i
                for h in range(8):
                    if live(i, 0):
                        pool.wait_ge(s.la_rot, 8 * b + h + 1)
                        if h % 4 == 0:
                            at_least(pool, s.la_qk, 2 * b + h // 4 - 1)
                        nc.gpsimd.tensor_tensor(tc[:, h // 4, h % 4, :], ta[:, h % 2, :], tb[:, h % 2, :], ALU.add
                                                ).then_inc(s.la_rotated, 1)
                    if h == 3 and live(i, -1):
                        pool.wait_ge(s.la_rotated, 8 * b + 4)
                        shift(i + 1, (n + 1) % NS)
            shift(0, 0)
            rows_pipeline(pool, step, 3, NS)

        @block.tensor
        def _(pe):
            pe.wait_ge(s.la_init, 3 * (layer + 1))

            def project(i, n, h):
                u = 8 * (row0 + i) + h
                if h == 0:
                    pe.wait_ge(s.la_shifted, row0 + i + 1)
                if h == 1:
                    at_least(pe, s.la_stored, row0 + i - 3 if live(i, 4) else 0)
                at_least(pe, s.la_rot, u - 1)
                at_least(pe, s.la_squared, u - 1)
                a, r = ("wq", "wqr") if h < 4 else ("wk", "wkr")
                c = (h % 4) * P
                nc.tensor.matmul(ps[:, h % 2, 0:L], w(a, c, P), hs[:, n, :], start=True, stop=True)
                nc.tensor.matmul(ps[:, h % 2, L:2 * L], w(r, c, P), hs[:, n, :], start=True, stop=True
                                 ).then_inc(s.la_product, 1)

            def norms(i, h):
                u = 8 * (row0 + i) + h
                if h % 4 == 0:
                    at_least(pe, s.la_clamped, 2 * (row0 + i) + h // 4)
                    if h == 0:
                        at_least(pe, s.la_vread, 2 * (row0 + i))
                pe.wait_ge(s.la_squared, u + 1)
                nc.tensor.matmul(ps[:, 2 + (h % 4) // 2, (h % 2) * L:(h % 2 + 1) * L], k.cf("block64"), sq[:, h % 2, :],
                                 start=True, stop=True).then_inc(s.la_norm, 1)

            def head(n, h):
                r = (h % 2) * 64
                return QK[r:r + 64, n, 0, h // 2, :], QK[r:r + 64, n, 1, h // 2, :]

            def maxima(i, n, h):
                u = 8 * (row0 + i) + h
                if h == 0:
                    pe.wait_ge(s.la_qk, 2 * (row0 + i + 1))
                at_least(pe, s.la_max, u)
                q, kk = head(n, h)
                nc.tensor.matmul(ps[:, 4, 0:128], q[:, 0:128], kk[:, 0:128], start=True, stop=False)
                nc.tensor.matmul(ps[:, 4, 0:128], k.cb("ident"), k.cb("local_q0"), start=False, stop=True)
                nc.tensor.matmul(ps[:, 4, 128:320], q[:, 128:256], kk[:, 64:256], start=True, stop=False)
                nc.tensor.matmul(ps[:, 4, 128:320], k.cb("ident"), k.cb("local_q1"), start=False, stop=True
                                 ).then_inc(s.la_score, 1)

            def shifts(i):
                b = row0 + i
                pe.wait_ge(s.la_m2, 3 * (b + 1))
                pe.wait_ge(s.la_vread, 2 * (b + 2) if live(i, -1) else 2 * (row0 + B))
                pe.nop(nofuse=True)
                for q in range(2):
                    m = nc.tensor.transpose(ps[:, 2, q * P:(q + 1) * P], m2[:, q, :], k.cf("identf"))
                m.then_inc(s.la_shift, 1)

            def keyed(i, n, h):
                u = 8 * (row0 + i) + h
                if h == 0:
                    pe.wait_ge(s.la_mt, row0 + i + 1)
                at_least(pe, s.la_prob, u - 1)
                q, kk = head(n, h)
                bank = 5 + h % 2
                sel = k.cb("sel", h * P, P)
                mt = mT[:].rearrange("h q t -> h (q t)")
                nc.tensor.matmul(ps[:, bank, 0:192], kk[:, 0:128], q[:, 0:192], start=True, stop=False)
                nc.tensor.matmul(ps[:, bank, 0:192], k.cb("ident"), k.cb("local_k0"), start=False, stop=False)
                nc.tensor.matmul(ps[:, bank, 0:192], sel, mt[:, 0:192], start=False, stop=True)
                nc.tensor.matmul(ps[:, bank, 192:320], kk[:, 128:256], q[:, 128:256], start=True, stop=False)
                nc.tensor.matmul(ps[:, bank, 192:320], k.cb("ident"), k.cb("local_k0", 0, P), start=False, stop=False)
                nc.tensor.matmul(ps[:, bank, 192:320], sel, mt[:, 128:256], start=False, stop=True
                                 ).then_inc(s.la_keyed, 1)

            def values(i, n, h):
                u = 8 * (row0 + i) + h
                pe.wait_ge(s.la_prob, u + 1)
                if h % 2 == 0:
                    at_least(pe, s.la_divided, 4 * (row0 + i) + h // 2)
                o0, o1 = (h % 2) * W65, (2 + h % 2) * W65
                p = pr[:, h % 2, :]
                nc.tensor.matmul(ps[:, 7, o0:o0 + W65], p[:, 0:128], V[:, n, 0, h, :], start=True, stop=True)
                nc.tensor.matmul(ps[:, 7, o1:o1 + W65], p[:, 192:320], V[:, n, 1, h, :], start=True, stop=True)
                nc.tensor.matmul(ps[0:64, 7, o1:o1 + W65], p[:, 128:192], V[:, n, 0, h, :], start=False, stop=True,
                                 skip_group_check=True).then_inc(s.la_attended, 1)

            def project_values(i, n):
                pe.wait_ge(s.la_clamped, 2 * (row0 + i + 1))
                for q in range(2):
                    nc.tensor.matmul(ps[:, 2 + q, :], hs[:, n, q * P:(q + 1) * P], w("wv"), start=True, stop=True
                                     ).then_inc(s.la_vprod, 1)

            def turn(i, o):
                b = row0 + i
                pe.wait_ge(s.la_divided, 4 * (b + 1))
                at_least(pe, s.la_stored, b)
                if live(i, -3):
                    pe.wait_ge(s.la_rot, 8 * (b + 4))
                    pe.wait_ge(s.la_squared, 8 * (b + 4))
                pe.nop(nofuse=True)
                for c in range(4):
                    for q in range(2):
                        at = (c % 2) * L + q * P
                        m = nc.tensor.transpose(ps[:, c // 2, at:at + P], ot[:, o, q, c, :], k.cf("identf"))
                m.then_inc(s.la_turn, 1)

            def output(i):
                pe.wait_ge(s.la_turned, 2 * (row0 + i + 1))
                for c in range(4):
                    m = nc.tensor.matmul(ps[:, 1, 0:L], w("wo", c * P, P), oT[:, c, :], start=(c == 0), stop=(c == 3))
                m.then_inc(s.la_out, 1)

            def step(i, n):
                n1, n2 = (n - 1) % NS, (n - 2) % NS
                if live(i, 2):
                    shifts(i - 2)
                for h in range(8):
                    if live(i, 0):
                        project(i, n, h)
                        if h >= 1:
                            norms(i, h - 1)
                    if live(i, 1):
                        maxima(i - 1, n1, h)
                    if live(i, 2):
                        keyed(i - 2, n2, h)
                        if h >= 1:
                            values(i - 2, n2, h - 1)
                if live(i, 0):
                    norms(i, 7)
                if live(i, 2):
                    values(i - 2, n2, 7)
                if live(i, 3):
                    turn(i - 3, n)
                if live(i, 0):
                    project_values(i, n)
                if live(i, 3):
                    output(i - 3)
            rows_pipeline(pe, step, 3, NS)

        @block.scalar
        def _(act):
            def step(i, n):
                b = row0 + i
                if live(i, 2):
                    act.wait_ge(s.la_shift, b - 1)
                    at_least(act, s.la_keyed, 8 * (b - 2))
                    nc.scalar.copy(mT[:].rearrange("h q t -> h (q t)"), ps[:, 2, 0:L]).then_inc(s.la_mt, 1)
                for h in range(8):
                    if live(i, 0):
                        u = 8 * b + h
                        act.wait_ge(s.la_product, u + 1)
                        at_least(act, s.la_norm, u - 1)
                        nc.scalar.activation(sq[:, h % 2, :], ps[:, h % 2, 0:L], ACT.Square).then_inc(s.la_squared, 1)
                    if live(i, 2):
                        v = 8 * (b - 2) + h
                        act.wait_ge(s.la_keyed, v + 1)
                        at_least(act, s.la_attended, v - 1)
                        nc.scalar.activation(pr[:, h % 2, :], ps[:, 5 + h % 2, 0:320], ACT.Exp, scale=8.0
                                             ).then_inc(s.la_prob, 1)
                    if live(i, 0) and h in (4, 7):
                        g = h // 5
                        act.wait_ge(s.la_clamped, 2 * b + g + 1)
                        at_least(act, s.la_qk, 2 * b + g)
                        nc.scalar.activation(rn[:], vc[:], ACT.Abs_reciprocal_sqrt).then_inc(s.la_rnorm, 1)
                        act.wait_ge(s.la_rnorm, 2 * b + g + 1)
                        nc.scalar.activation(y2[:], rn[:], ACT.Square).then_inc(s.la_rnorm2, 1)
                if live(i, 3):
                    act.wait_ge(s.la_turn, b - 2)
                    at_least(act, s.la_out, b - 3)
                    for c in range(2):
                        nc.scalar.copy(oT[:, 2 * c:2 * c + 2, :].rearrange("p c t -> p (c t)"), ps[:, c, :]
                                       ).then_inc(s.la_turned, 1)
                if live(i, 0):
                    for q in range(2):
                        act.wait_ge(s.la_vprod, 2 * b + q + 1)
                        if live(i, NS):
                            at_least(act, s.la_attended, 8 * (b - NS + 1))
                        if isinstance(i, int) and i == 0 and q == 0:
                            act.wait_ge(s.la_init, 3 * (layer + 1))
                        nc.scalar.copy(V[:, n, q, :, 0:D64], ps[:, 2 + q, :].rearrange("p (h d) -> p h d", d=D64)
                                       ).then_inc(s.la_vread, 1)
            rows_pipeline(act, step, 3, NS)

        @block.vector
        def _(dve):
            for j, (name, col) in enumerate((("qa", "qs"), ("qb", "qsr"), ("ka", "ks"), ("kb", "ksr"))):
                nc.vector.tensor_scalar(tab[:, j, :], rope(name), w(col), None, ALU.mult).then_inc(s.la_table, 1)
            dve.wait_ge(s.la_table, 4 * (layer + 1))
            dve.wait_ge(s.la_init, 3 * (layer + 1))

            flat = lambda v: v.rearrange("p c t -> p (c t)")

            def clamp(i, g):
                b = row0 + i
                dve.wait_ge(s.la_norm, 8 * b + 4 * (g + 1))
                at_least(dve, s.la_vy2, 2 * b + g)
                nc.vector.tensor_scalar(flat(vc[:]), ps[:, 2:4, :].rearrange("p a t -> p (a t)"), 1e-24, None, ALU.max
                                        ).then_inc(s.la_clamped, 1)

            def scale(i, n, g):
                b = row0 + i
                dve.wait_ge(s.la_rnorm2, 2 * b + g + 1)
                nc.vector.tensor_tensor(flat(y2[:]), flat(vc[:]), flat(y2[:]), ALU.mult).then_inc(s.la_vy2, 1)
                dve.wait_ge(s.la_vy2, 2 * b + g + 1)
                nc.vector.scalar_tensor_tensor(out=flat(rn[:]), in0=flat(y2[:]), scalar=-3.0, in1=flat(rn[:]),
                                               op0=ALU.add, op1=ALU.mult).then_inc(s.la_exact, 1)
                dve.wait_ge(s.la_exact, 2 * b + g + 1)
                dve.wait_ge(s.la_rotated, 8 * b + 4 * (g + 1))
                if live(i, NS):
                    at_least(dve, s.la_keyed, 8 * (b - NS + 1))
                nc.vector.scalar_tensor_tensor(out=flat(QK[:, n, g, :, :]), in0=flat(rn[:]), scalar=-0.5,
                                               in1=flat(tc[:, g, :, :]), op0=ALU.mult, op1=ALU.mult).then_inc(s.la_qk, 1)

            def divide(i, o, g):
                b = row0 + i
                dve.wait_ge(s.la_attended, 8 * b + 2 * (g + 1))
                out = ps[:, 7, 0:4 * W65].rearrange("p (q h c) -> p q h c", q=2, c=W65)
                nc.vector.reciprocal(rec[:], out[:, :, :, D64]).then_inc(s.la_rec, 1)
                if g == 0:
                    at_least(dve, s.la_turn, b - 2 if live(i, 3) else 0)
                dve.wait_ge(s.la_rec, 4 * b + g + 1)
                nc.vector.tensor_tensor(ot[:, o, :, g, :].rearrange("p q (h d) -> p q h d", d=D64), out[:, :, :, 0:D64],
                                        rec[:].unsqueeze(3).to_broadcast([P, 2, 2, D64]), ALU.mult
                                        ).then_inc(s.la_divided, 1)

            def step(i, n):
                b = row0 + i
                o = (n - 2) % NS
                for h in range(8):
                    if live(i, 0):
                        u = 8 * b + h
                        dve.wait_ge(s.la_squared, u + 1)
                        at_least(dve, s.la_rotated, u - 1)
                        nc.vector.tensor_tensor(ta[:, h % 2, :], ps[:, h % 2, 0:L], tab[:, 2 * (h // 4), :], ALU.mult)
                        nc.vector.tensor_tensor(tb[:, h % 2, :], ps[:, h % 2, L:2 * L], tab[:, 2 * (h // 4) + 1, :],
                                                ALU.mult).then_inc(s.la_rot, 1)
                    if live(i, 1):
                        v = 8 * (b - 1) + h
                        dve.wait_ge(s.la_score, v + 1)
                        if h == 0:
                            at_least(dve, s.la_m2, 3 * (b - 1))
                        nc.vector.tensor_reduce(nm[:, 0, h:h + 1], ps[:, 4, 0:128], AX.X, ALU.max, negate=True)
                        nc.vector.tensor_reduce(nm[:, 1, h:h + 1], ps[:, 4, 128:320], AX.X, ALU.max, negate=True
                                                ).then_inc(s.la_max, 1)
                    if live(i, 2) and h in (2, 4, 6):
                        divide(i - 2, o, h // 2 - 1)
                    if live(i, 0) and h == 4:
                        clamp(i, 0)
                    if live(i, 0) and h == 6:
                        scale(i, n, 0)
                if live(i, 0):
                    clamp(i, 1)
                if live(i, 2):
                    divide(i - 2, o, 3)
                if live(i, 1):
                    c = 3 * (b - 1)
                    dve.wait_ge(s.la_max, 8 * b)
                    nc.vector.tensor_copy(nb[:], nm[:]).then_inc(s.la_m2, 1)
                    dve.wait_ge(s.la_m2, c + 1)
                    at_least(dve, s.la_shift, b - 1)
                    nc.vector.tensor_copy(m2[:, :, 0:H8], nb[:]).then_inc(s.la_m2, 1)
                    nc.vector.tensor_tensor(m2[:, :, 32:32 + H8], nm[:], nb[:], ALU.subtract).then_inc(s.la_m2, 1)
                if live(i, 0):
                    scale(i, n, 1)
                if live(i, 3):
                    dve.wait_ge(s.la_out, b - 2)
                    nc.vector.tensor_tensor(Yd[:, bass.ds((i - 3) * L, L)], ps[:, 1, 0:L], X0[:, bass.ds((i - 3) * L, L)],
                                            ALU.add).then_inc(s.la_stored, 1)
            rows_pipeline(dve, step, 3, NS)


def attention(k, call, slots, kr, stack_dt, scale, rounds, value_w, out_w, out_b, make):
    nc, s, ps = k.nc, k.s, k.ps
    row0 = call * B
    W9 = D8 + 1
    rd0 = k.rounds
    sd0 = k.stack_dmas
    with ExitStack() as ctx:
        sb = lambda n, shape, dt=F32: ctx.enter_context(nc.sbuf_tensor(f"at{call}_{n}", shape, dt))
        a = Core()
        a.row0, a.rd0, a.slots = row0, rd0, slots
        a.xb = sb("xb", [P, slots, L])
        a.Qs = sb("qs", [kr, slots, H16 * L], stack_dt)
        a.Ks = sb("ks", [kr, slots, H16 * L], stack_dt)
        V = sb("v", [P, slots, 2, H16, W9])
        nm = sb("nm", [P, 2, H16])
        nb = sb("nb", [P, 2, H16], BF16)
        m2 = sb("m2", [P, 2, 48])
        mT = sb("mt", [48, L], BF16)
        pr = sb("pr", [P, 2, 2, 384])
        rec = sb("rec", [P, 2, H16])
        ot = sb("ot", [P, 2, P])
        oT = sb("oT", [P, L])
        make(a, sb)
        nst = len(a.stack_loads(0))
        k.rounds += rounds * B
        k.stack_dmas += nst * B
        block = ctx.enter_context(nc.Block())

        @block.sync
        def _(sp):
            a.fill_constant_rows(sp)

            def step(i, n):
                if not live(i, 0):
                    return
                b = row0 + i
                a.wait_parts(sp, i)
                sp.nop(nofuse=True)
                at_least(sp, s.at_stacked, 16 * (sd0 + nst * i))
                sp.nop(nofuse=True)
                for dst, src in a.scratch_stores():
                    sp.dma_start(dst, src).then_inc(s.at_scratch, 16)
                sp.wait_ge(s.at_scratch, 32 * (b + 1))
                sp.nop(nofuse=True)
                if live(i, slots):
                    at_least(sp, s.at_keyed, 8 * (b - slots + 1))
                    sp.nop(nofuse=True)
                for dst, src in a.stack_loads(n):
                    sp.dma_start(dst, src).then_inc(s.at_stacked, 16)
            rows_pipeline(sp, step, 3, slots)

        @block.gpsimd
        def _(pool):
            nc.gpsimd.memset(V[:, :, :, :, D8:W9], 1.0).then_inc(s.at_init, 1)
            nc.gpsimd.memset(m2[:], 0.0).then_inc(s.at_init, 1)

            def fetch(i, n):
                if live(i, slots):
                    at_least(pool, s.at_vprod, row0 + i - slots + 1)
                nc.gpsimd.tensor_copy(a.xb[:, n, :], k.XN[:, bass.ds(i * L, L)]).then_inc(s.at_fetched, 1)
                a.fetch_more(pool, i, n)

            def step(i, n):
                if live(i, -1):
                    fetch(i + 1, (n + 1) % slots)
                for p in range(8):
                    if live(i, 0):
                        a.pool_round(pool, i, n, p)
            fetch(0, 0)
            rows_pipeline(pool, step, 3, slots)

        @block.tensor
        def _(pe):
            pe.wait_ge(s.at_init, 2 * (call + 1))

            def product(i, n, r):
                if r == 0:
                    pe.wait_ge(s.at_fetched, row0 + i + 1)
                at_least(pe, s.at_used, rd0 + rounds * i + r)
                a.product(i, n, r).then_inc(s.at_product, 1)

            def value_rows(i, n):
                a.wait_value_input(pe, i)
                at_least(pe, s.at_vread, row0 + i)
                if live(i, 3):
                    at_least(pe, s.at_stored, row0 + i - 2)
                for q in range(2):
                    m = nc.tensor.matmul(ps[:, 1, q * P:(q + 1) * P], a.value_in(n)[:, q * P:(q + 1) * P], value_w,
                                         start=True, stop=True)
                m.then_inc(s.at_vprod, 1)

            def maxima(i, n, p):
                u = 8 * (row0 + i) + p
                if p == 0:
                    pe.wait_ge(s.at_stacked, 16 * (sd0 + nst * (i + 1)))
                at_least(pe, s.at_max, u)
                for e in range(2):
                    q = a.Qs[:, n, (2 * p + e) * L:(2 * p + e + 1) * L]
                    kk = a.Ks[:, n, (2 * p + e) * L:(2 * p + e + 1) * L]
                    o = ps[:, 2 + e, :]
                    nc.tensor.matmul(o[:, 0:128], q[:, 0:128], kk[:, 0:128], start=True, stop=False)
                    nc.tensor.matmul(o[:, 0:128], k.cb("ident"), k.cb("causal_q"), start=False, stop=True)
                    nc.tensor.matmul(o[:, 128:384], q[:, 128:256], kk[:, 0:256], start=True, stop=False)
                    m = nc.tensor.matmul(o[:, 256:384], k.cb("ident"), k.cb("causal_q"), start=False, stop=True)
                m.then_inc(s.at_score, 1)

            def shifts(i):
                pe.wait_ge(s.at_m2, 3 * (row0 + i + 1))
                pe.nop(nofuse=True)
                for q in range(2):
                    m = nc.tensor.transpose(ps[0:48, 6, q * P:(q + 1) * P], m2[:, q, :], k.cf("identf"))
                m.then_inc(s.at_shift, 1)

            def keyed(i, n, p):
                u = 8 * (row0 + i) + p
                if p == 0:
                    pe.wait_ge(s.at_mt, row0 + i + 1)
                at_least(pe, s.at_prob, u)
                for e in range(2):
                    h = 2 * p + e
                    q, kk = a.Qs[:, n, h * L:(h + 1) * L], a.Ks[:, n, h * L:(h + 1) * L]
                    o = ps[:, 4 + e, :]
                    sel = k.cb("sel", h * P, P, rows=48)
                    nc.tensor.matmul(o[:, 0:256], kk[:, 0:128], q[:, 0:256], start=True, stop=False)
                    nc.tensor.matmul(o[:, 0:128], k.cb("ident"), k.cb("causal_k"), start=False, stop=False)
                    nc.tensor.matmul(o[:, 0:256], sel, mT[:, 0:256], start=False, stop=True)
                    nc.tensor.matmul(o[:, 256:384], kk[:, 128:256], q[:, 128:256], start=True, stop=False)
                    nc.tensor.matmul(o[:, 256:384], k.cb("ident"), k.cb("causal_k"), start=False, stop=False)
                    m = nc.tensor.matmul(o[:, 256:384], sel, mT[:, 128:256], start=False, stop=True)
                m.then_inc(s.at_keyed, 1)

            def values(i, n, p):
                u = 8 * (row0 + i) + p
                pe.wait_ge(s.at_prob, u + 1)
                if p == 0:
                    at_least(pe, s.at_divided, row0 + i)
                    pe.wait_ge(s.at_vread, row0 + i + 1)
                for e in range(2):
                    h = 2 * p + e
                    o0, o1 = h * W9, (H16 + h) * W9
                    w = pr[:, p % 2, e, :]
                    nc.tensor.matmul(ps[:, 7, o0:o0 + W9], w[:, 0:128], V[:, n, 0, h, :], start=True, stop=True)
                    nc.tensor.matmul(ps[:, 7, o1:o1 + W9], w[:, 128:256], V[:, n, 0, h, :], start=True, stop=False)
                    m = nc.tensor.matmul(ps[:, 7, o1:o1 + W9], w[:, 256:384], V[:, n, 1, h, :], start=False, stop=True)
                m.then_inc(s.at_attended, 1)

            def turn(i):
                pe.wait_ge(s.at_divided, row0 + i + 1)
                pe.nop(nofuse=True)
                for q in range(2):
                    m = nc.tensor.transpose(ps[:, 6, L + q * P:L + (q + 1) * P], ot[:, q, :], k.cf("identf"))
                m.then_inc(s.at_turn, 1)

            def output(i):
                pe.wait_ge(s.at_turned, row0 + i + 1)
                at_least(pe, s.at_stored, row0 + i)
                pe.wait_ge(s.at_vread, row0 + i + 3 if live(i, -2) else row0 + B)
                nc.tensor.matmul(ps[:, 1, L:2 * L], out_w, oT[:], start=True, stop=True).then_inc(s.at_out, 1)

            def step(i, n):
                if live(i, 0):
                    product(i, n, 0)
                if live(i, 1):
                    value_rows(i - 1, (n - 1) % slots)
                if live(i, 2):
                    shifts(i - 2)
                for p in range(8):
                    if live(i, 0) and 1 <= p < rounds:
                        product(i, n, p)
                    if live(i, 1):
                        maxima(i - 1, (n - 1) % slots, p)
                    if live(i, 2):
                        keyed(i - 2, (n - 2) % slots, p)
                        if p >= 1:
                            values(i - 2, (n - 2) % slots, p - 1)
                    if live(i, 3) and p == 2:
                        turn(i - 3)
                    if live(i, 3) and p == 4:
                        output(i - 3)
                if live(i, 2):
                    values(i - 2, (n - 2) % slots, 7)
            rows_pipeline(pe, step, 3, slots)

        @block.scalar
        def _(act):
            act.wait_ge(s.at_init, 2 * (call + 1))

            def step(i, n):
                b = row0 + i
                if live(i, 1):
                    act.wait_ge(s.at_vprod, b)
                    if live(i, 1 + slots):
                        at_least(act, s.at_attended, 8 * (b - slots))
                    nc.scalar.copy(V[:, (n - 1) % slots, :, :, 0:D8],
                                   ps[:, 1, 0:L].rearrange("p (q h d) -> p q h d", q=2, d=D8)).then_inc(s.at_vread, 1)
                if live(i, 2):
                    act.wait_ge(s.at_shift, b - 1)
                    at_least(act, s.at_keyed, 8 * (b - 2))
                    nc.scalar.copy(mT[:], ps[0:48, 6, 0:L]).then_inc(s.at_mt, 1)
                for p in range(8):
                    if live(i, 0):
                        a.act_round(act, i, n, p)
                    if live(i, 2):
                        v = 8 * (b - 2) + p
                        act.wait_ge(s.at_keyed, v + 1)
                        at_least(act, s.at_attended, v - 1)
                        nc.scalar.activation(pr[:, p % 2, :, :], ps[:, 4:6, 0:384], ACT.Exp, scale=scale
                                             ).then_inc(s.at_prob, 1)
                    if live(i, 3) and p == 2:
                        act.wait_ge(s.at_turn, b - 2)
                        at_least(act, s.at_out, b - 3)
                        nc.scalar.copy(oT[:], ps[:, 6, L:2 * L]).then_inc(s.at_turned, 1)
            rows_pipeline(act, step, 3, slots)

        @block.vector
        def _(dve):
            a.vector_init(dve)
            dve.wait_ge(s.at_init, 2 * (call + 1))

            def step(i, n):
                b = row0 + i
                for p in range(8):
                    if live(i, 0):
                        a.vector_round(dve, i, n, p)
                    if live(i, 1):
                        dve.wait_ge(s.at_score, 8 * (b - 1) + p + 1)
                        if p == 0:
                            at_least(dve, s.at_m2, 3 * (b - 1))
                        nc.vector.tensor_reduce(nm[:, 0, 2 * p:2 * p + 2], ps[:, 2:4, 0:128], AX.X, ALU.max, negate=True)
                        nc.vector.tensor_reduce(nm[:, 1, 2 * p:2 * p + 2], ps[:, 2:4, 128:384], AX.X, ALU.max,
                                                negate=True).then_inc(s.at_max, 1)
                    if live(i, 3) and p == 5:
                        dve.wait_ge(s.at_out, b - 2)
                        to = k.S[:, bass.ds((i - 3) * L, L)]
                        if out_b is None:
                            m = nc.vector.tensor_copy(to, ps[:, 1, L:2 * L])
                        else:
                            m = nc.vector.tensor_scalar(to, ps[:, 1, L:2 * L], out_b, None, ALU.add)
                        m.then_inc(s.at_stored, 1)
                if live(i, 1):
                    c = 3 * (b - 1)
                    dve.wait_ge(s.at_max, 8 * b)
                    nc.vector.tensor_copy(nb[:], nm[:]).then_inc(s.at_m2, 1)
                    dve.wait_ge(s.at_m2, c + 1)
                    at_least(dve, s.at_shift, b - 1)
                    nc.vector.tensor_copy(m2[:, :, 0:H16], nb[:]).then_inc(s.at_m2, 1)
                    nc.vector.tensor_tensor(m2[:, :, 32:48], nm[:], nb[:], ALU.subtract).then_inc(s.at_m2, 1)
                if live(i, 2):
                    dve.wait_ge(s.at_attended, 8 * (b - 1))
                    out = ps[:, 7, 0:2 * H16 * W9].rearrange("p (q h c) -> p q h c", q=2, c=W9)
                    nc.vector.reciprocal(rec[:], out[:, :, :, D8]).then_inc(s.at_rec, 1)
                    at_least(dve, s.at_turn, b - 2)
                    dve.wait_ge(s.at_rec, b - 1)
                    nc.vector.tensor_tensor(ot[:].rearrange("p q (h d) -> p q h d", d=D8), out[:, :, :, 0:D8],
                                            rec[:].unsqueeze(3).to_broadcast([P, 2, H16, D8]), ALU.mult
                                            ).then_inc(s.at_divided, 1)
            rows_pipeline(dve, step, 3, slots)


def nothing(*_):
    pass


def split_stacks(k, a, sb, name):
    nc, s = k.nc, k.s
    a.parts = sb("parts", [P, 3, 2 * L], BF16)
    a.res = sb("res", [P, 2 * L])
    scr = nc.dram_tensor(f"scratch_{name}", (2, 3, P, L), BF16)
    flat = [scr[j].rearrange("s (d h) t -> (s d) (h t)", h=H16) for j in range(2)]
    a.scratch_stores = lambda: [(scr[j].rearrange("s p t -> p s t"), a.parts[:, :, j * L:(j + 1) * L]) for j in range(2)]
    a.stack_loads = lambda n: (
        [(a.Qs[0:24, n, :], flat[0][0:24]), (a.Qs[24:40, n, :], flat[0][0:16]), (a.Qs[40:48, n, :], flat[0][0:8])]
        + [(a.Ks[8 * j:8 * j + 8, n, :], flat[1][0:8]) for j in range(3)]
        + [(a.Ks[24 + 8 * j:32 + 8 * j, n, :], flat[1][8:16]) for j in range(2)]
        + [(a.Ks[40:48, n, :], flat[1][16:24])])
    a.wait_parts = lambda sp, i: sp.wait_ge(s.at_parts, a.row0 + i + 1)

    def leading(act, i, src):
        at_least(act, s.at_scratch, 32 * (a.row0 + i))
        nc.scalar.copy(a.parts[:, 0, :], src).then_inc(s.at_hi, 1)

    def rest(dve, i, src):
        dve.wait_ge(s.at_hi, a.row0 + i + 1)
        at_least(dve, s.at_parts, a.row0 + i)
        return nc.vector.tensor_tensor(a.res[:], src, a.parts[:, 0, :], ALU.subtract)

    def middle(act, i):
        act.wait_ge(s.at_res, a.row0 + i + 1)
        nc.scalar.copy(a.parts[:, 1, :], a.res[:]).then_inc(s.at_mid, 1)

    def last(dve, i):
        dve.wait_ge(s.at_mid, a.row0 + i + 1)
        nc.vector.tensor_tensor(a.parts[:, 2, :], a.res[:], a.parts[:, 1, :], ALU.subtract).then_inc(s.at_parts, 1)
    a.leading, a.rest, a.middle, a.last = leading, rest, middle, last


def alibi_attention(k, w, alibi):
    nc, s, ps = k.nc, k.s, k.ps

    def make(a, sb):
        split_stacks(k, a, sb, "alibi")
        rows16 = sb("alibi", [64, H16 * L], BF16)
        a.fetch_more = a.pool_round = nothing
        a.wait_value_input = nothing
        a.value_in = lambda n: a.xb[:, n, :]

        def fill(sp):
            for j in range(2):
                sp.dma_start(k.Y[32 * j:32 * j + 6, :], alibi[j]).then_inc(s.alibi_loaded, 16)
            sp.wait_ge(s.alibi_cast, 2)
            for n in range(a.slots):
                sp.dma_start(a.Qs[48:54, n, :], rows16[0:6, :]).then_inc(s.alibi_rows, 16)
                sp.dma_start(a.Ks[48:54, n, :], rows16[32:38, :]).then_inc(s.alibi_rows, 16)
            sp.wait_ge(s.alibi_rows, 32 * a.slots)
        a.fill_constant_rows = fill

        def init(dve):
            dve.wait_ge(s.alibi_loaded, 32)
            for j in range(2):
                nc.vector.tensor_copy(rows16[32 * j:32 * j + 6, :], k.Y[32 * j:32 * j + 6, :]).then_inc(s.alibi_cast, 1)
        a.vector_init = init

        def product(i, n, r):
            nc.tensor.matmul(ps[:, 0, 0:L], w("wq"), a.xb[:, n, :], start=True, stop=True)
            return nc.tensor.matmul(ps[:, 0, L:2 * L], w("wk"), a.xb[:, n, :], start=True, stop=True)
        a.product = product

        def act_round(act, i, n, p):
            if p == 0:
                act.wait_ge(s.at_product, a.rd0 + i + 1)
                a.leading(act, i, ps[:, 0, :])
            if p == 1:
                a.middle(act, i)
        a.act_round = act_round

        def vector_round(dve, i, n, p):
            if p == 0:
                a.rest(dve, i, ps[:, 0, :]).then_inc(s.at_res, 1)
                dve.wait_ge(s.at_res, a.row0 + i + 1)
                nc.vector.sem_inc(s.at_used, 1)
            if p == 1:
                a.last(dve, i)
        a.vector_round = vector_round

    attention(k, 0, 3, 54, BF16, float(1 / np.sqrt(8.0)), 1, w("wv"), w("wo"), None, make)


def rope8_attention(k, w, fold):
    nc, s, ps = k.nc, k.s, k.ps

    def make(a, sb):
        split_stacks(k, a, sb, "rope8")
        ta, tb, tq = sb("ta", [P, 2, L]), sb("tb", [P, 2, L]), sb("tq", [P, 2, L])
        a.fetch_more = a.fill_constant_rows = a.wait_value_input = a.vector_init = nothing
        a.value_in = lambda n: a.xb[:, n, :]

        def product(i, n, r):
            nc.tensor.matmul(ps[:, 0, 0:L], fold[:, 2 * r, :], a.xb[:, n, :], start=True, stop=True)
            return nc.tensor.matmul(ps[:, 0, L:2 * L], fold[:, 2 * r + 1, :], a.xb[:, n, :], start=True, stop=True)
        a.product = product

        def vector_round(dve, i, n, p):
            if p < 2:
                dve.wait_ge(s.at_product, a.rd0 + 2 * i + p + 1)
                at_least(dve, s.at_sum, 2 * i + p - 1)
                nc.vector.tensor_tensor(ta[:, p, :], ps[:, 0, 0:L], w("cos"), ALU.mult)
                nc.vector.tensor_tensor(tb[:, p, :], ps[:, 0, L:2 * L], w("sin"), ALU.mult).then_inc(s.at_used, 1)
            if p == 2:
                a.rest(dve, i, tq[:].rearrange("p a t -> p (a t)")).then_inc(s.at_res, 1)
            if p == 3:
                a.last(dve, i)
        a.vector_round = vector_round

        def pool_round(pool, i, n, p):
            if p < 2:
                pool.wait_ge(s.at_used, a.rd0 + 2 * i + p + 1)
                at_least(pool, s.at_res, a.row0 + i)
                nc.gpsimd.tensor_tensor(tq[:, p, :], ta[:, p, :], tb[:, p, :], ALU.add).then_inc(s.at_sum, 1)
        a.pool_round = pool_round

        def act_round(act, i, n, p):
            if p == 2:
                act.wait_ge(s.at_sum, 2 * i + 2)
                a.leading(act, i, tq[:].rearrange("p a t -> p (a t)"))
            if p == 3:
                a.middle(act, i)
        a.act_round = act_round

    attention(k, 1, 3, 48, BF16, float(D8 ** -0.5), 2, fold[:, 4, :], w("wo"), w("bo"), make)


def latent_attention(k, w, fold, kvn):
    nc, s, ps = k.nc, k.s, k.ps

    def make(a, sb):
        ta, tb = sb("ta", [P, 2, 2 * L]), sb("tb", [P, 2, 2 * L])
        qk = sb("parts", [P, 2, 5, L])
        a.kvb = sb("kvb", [32, a.slots, L])
        scr = nc.dram_tensor("scratch_latent", (2, 5 * P, L), F32)
        a.scratch_stores = lambda: [(scr[j].rearrange("(c p) t -> p c t", p=P), qk[:, j, :, :]) for j in range(2)]
        a.stack_loads = lambda n: [(st[:, n, :], scr[j].rearrange("(d h) t -> d (h t)", h=H16))
                                   for j, st in enumerate((a.Qs, a.Ks))]
        a.fill_constant_rows = a.vector_init = nothing
        a.value_in = lambda n: a.kvb[:, n, :]
        a.wait_value_input = lambda pe, i: pe.wait_ge(s.at_kv, i + 1)

        def wait_parts(sp, i):
            sp.wait_ge(s.at_content, i + 1)
            sp.nop(nofuse=True)
            sp.wait_ge(s.at_sum, 2 * B + 4 * (i + 1))
        a.wait_parts = wait_parts

        def fetch_more(pool, i, n):
            nc.gpsimd.tensor_copy(a.kvb[:, n, :], kvn[0:32, bass.ds(i * L, L)]).then_inc(s.at_kv, 1)
        a.fetch_more = fetch_more

        def product(i, n, r):
            x = a.xb[:, n, :]
            if r == 0:
                nc.tensor.matmul(ps[:, 0, 0:L], fold[:, 0:P], x, start=True, stop=True)
                nc.tensor.wait_ge(s.at_kv, i + 1)
                return nc.tensor.matmul(ps[:, 0, L:2 * L], w("kd", rows=32), a.kvb[:, n, :], start=True, stop=True)
            c = (r - 1) % 2
            src = fold[:, P:5 * P] if r < 3 else w("kr")
            nc.tensor.matmul(ps[:, 0, 0:L], src[:, c * P:(c + 1) * P], x, start=True, stop=True)
            return nc.tensor.matmul(ps[:, 0, L:2 * L], src[:, (c + 2) * P:(c + 3) * P], x, start=True, stop=True)
        a.product = product

        def act_round(act, i, n, p):
            if p == 0:
                act.wait_ge(s.at_product, a.rd0 + 5 * i + 1)
                at_least(act, s.at_scratch, 32 * (a.row0 + i))
                nc.scalar.copy(qk[:, :, 0, :], ps[:, 0, :].rearrange("p (a t) -> p a t", a=2)).then_inc(s.at_content, 1)
                act.wait_ge(s.at_content, i + 1)
                nc.scalar.sem_inc(s.at_used, 1)
        a.act_round = act_round

        def vector_round(dve, i, n, p):
            if 1 <= p < 5:
                c, e = (p - 1) % 2, p % 2
                dve.wait_ge(s.at_product, a.rd0 + 5 * i + p + 1)
                at_least(dve, s.at_sum, 2 * B + 4 * i + p - 2)
                two = ps[:, 0, :].rearrange("p (a t) -> p a t", a=2)
                sin = w("sin", c * 2 * L, 2 * L)
                nc.vector.tensor_tensor(ta[:, e, :], ps[:, 0, :], w("cos", c * 2 * L, 2 * L), ALU.mult)
                nc.vector.tensor_tensor(tb[:, e, 0:L], two[:, 1, :], sin[:, 0:L], ALU.mult)
                nc.vector.tensor_tensor(tb[:, e, L:2 * L], two[:, 0, :], sin[:, L:2 * L], ALU.mult).then_inc(s.at_used, 1)
        a.vector_round = vector_round

        def pool_round(pool, i, n, p):
            if 1 <= p < 5:
                c, e = (p - 1) % 2, p % 2
                pool.wait_ge(s.at_used, a.rd0 + 5 * i + p + 1)
                if p == 1:
                    at_least(pool, s.at_scratch, 32 * (a.row0 + i))
                nc.gpsimd.tensor_tensor(qk[:, (p - 1) // 2, 1 + c:4 + c:2, :], ta[:, e, :].rearrange("p (a t) -> p a t", a=2),
                                        tb[:, e, :].rearrange("p (a t) -> p a t", a=2), ALU.add).then_inc(s.at_sum, 1)
        a.pool_round = pool_round

    attention(k, 2, 2, 40, F32, float(40.0 ** -0.5), 5, w("vd", rows=32), w("wo"), None, make)


def experts(k, w):
    nc, s, ps = k.nc, k.s, k.ps
    with ExitStack() as ctx:
        sb = lambda n, shape, dt=F32: ctx.enter_context(nc.sbuf_tensor(f"moe_{n}", shape, dt))
        xt = sb("xt", [P, 2, TILE])
        gs = sb("gs", [P, N // P, NEXP])
        best = sb("best", [P, N // P])
        pick = sb("pick", [P, N // P])
        at = sb("at", [P, N // P, NEXP])
        hot = sb("hot", [P, N // P, NEXP])
        io = sb("io", [P, NEXP])
        hotT = sb("hott", [NEXP, N])
        hotb = sb("hotb", [NEXP, N], BF16)
        hr = sb("hr", [P, 3, TILE])
        hm = sb("hm", [P, 3, TILE])

        with nc.Block() as block:
            @block.gpsimd
            def _(pool):
                for e in range(NEXP):
                    m = nc.gpsimd.memset(io[:, e:e + 1], float(e))
                m.then_inc(s.moe_iota, 1)
                for t in range(NT):
                    at_least(pool, s.moe_scores, t - 1)
                    nc.gpsimd.tensor_copy(xt[:, t % 2, :], k.XN[:, t * TILE:(t + 1) * TILE]).then_inc(s.moe_fetched, 1)

            @block.tensor
            def _(pe):
                for t in range(NT):
                    pe.wait_ge(s.moe_fetched, t + 1)
                    for q in range(4):
                        o = ps[:, t, q * NEXP:(q + 1) * NEXP]
                        nc.tensor.matmul(o, xt[:, t % 2, q * P:(q + 1) * P], w("wg"), start=True, stop=False)
                        m = nc.tensor.matmul(o, k.cf("ones", rows=1), w("bg", rows=1), start=False, stop=True)
                    m.then_inc(s.moe_scores, 1)
                pe.wait_ge(s.moe_hot, 5)
                for t in range(NT):
                    for q in range(4):
                        m = nc.tensor.transpose(ps[0:NEXP, t, q * P:(q + 1) * P], hot[:, 4 * t + q, :], k.cf("identf"))
                    m.then_inc(s.moe_turn, 1)

            @block.vector
            def _(dve):
                dve.wait_ge(s.moe_scores, NT)
                dve.wait_ge(s.moe_iota, 1)
                flat = gs[:].rearrange("p (t q) e -> p t (q e)", q=4)
                nc.vector.tensor_copy(flat, ps[:, :, 0:4 * NEXP]).then_inc(s.moe_hot, 1)
                dve.wait_ge(s.moe_hot, 1)
                nc.vector.tensor_reduce(best[:], gs[:], AX.X, ALU.max).then_inc(s.moe_hot, 1)
                dve.wait_ge(s.moe_hot, 2)
                wide = [P, N // P, NEXP]
                iota = io[:].unsqueeze(1).to_broadcast(wide)
                nc.vector.tensor_tensor(at[:], gs[:], best[:].unsqueeze(2).to_broadcast(wide), ALU.is_equal
                                        ).then_inc(s.moe_hot, 1)
                dve.wait_ge(s.moe_hot, 3)
                nc.vector.scalar_tensor_tensor(out=hot[:], in0=at[:], scalar=-16.0, in1=iota, op0=ALU.mult, op1=ALU.add
                                               ).then_inc(s.moe_hot, 1)
                dve.wait_ge(s.moe_hot, 4)
                nc.vector.tensor_reduce(pick[:], hot[:], AX.X, ALU.min).then_inc(s.moe_pick, 1)
                dve.wait_ge(s.moe_pick, 1)
                nc.vector.tensor_tensor(hot[:], hot[:], pick[:].unsqueeze(2).to_broadcast(wide), ALU.is_equal
                                        ).then_inc(s.moe_hot, 1)
                for t in range(NT):
                    dve.wait_ge(s.moe_turn, t + 1)
                    nc.vector.tensor_copy(hotT[:, t * TILE:(t + 1) * TILE], ps[0:NEXP, t, :]).then_inc(s.moe_turned, 1)

            @block.scalar
            def _(act):
                for t in range(NT):
                    act.wait_ge(s.moe_turned, t + 1)
                    nc.scalar.copy(hotb[:, t * TILE:(t + 1) * TILE], hotT[:, t * TILE:(t + 1) * TILE])

        with nc.Block() as block:
            units = [(e, c) for e in range(NEXP) for c in range(EH // P)]
            M = len(units)

            def slot(n):
                return n % 3

            @block.tensor
            def _(pe):
                pe.wait_ge(s.load_moe, 16)

                def body(t, par):
                    def out(n):
                        e, c = units[n]
                        pe.wait_ge(s.moe_masked, t * M + n + 1)
                        if n == 0:
                            at_least(pe, s.moe_stored, t - 1)
                            pe.nop(nofuse=True)
                            nc.tensor.matmul(ps[:, 5 + par, :], w("b2", rows=NEXP), hotT[:, tok(t)], start=True, stop=False)
                        nc.tensor.matmul(ps[:, 5 + par, :], w("w2", n * P, P), hm[:, slot(n + 2 * par), :],
                                         start=False, stop=(n == M - 1)).then_inc(s.moe_out, 1)
                    for n, (e, c) in enumerate(units):
                        if c == 0:
                            at_least(pe, s.moe_masked, t * M + n - 4)
                            pe.nop(nofuse=True)
                            nc.tensor.matmul(ps[:, 3 + e % 2, :], k.cb("sel", e * P, P, rows=NEXP), hotb[:, tok(t)],
                                             start=True, stop=True)
                        at_least(pe, s.moe_relu, t * M + n - 2)
                        nc.tensor.matmul(ps[:, slot(n + 2 * par), :], w("w1", n * P, P), k.XN[:, tok(t)],
                                         start=True, stop=True).then_inc(s.moe_hidden, 1)
                        if n >= 2:
                            out(n - 2)
                    out(M - 2)
                    out(M - 1)
                for t in range(2):
                    body(t, t)
                with pe.Fori(1, NT // 2) as turn:
                    i = turn * 2
                    for par in range(2):
                        body(i + par, par)

            @block.scalar
            def _(act):
                def body(t, par):
                    for n in range(M):
                        act.wait_ge(s.moe_hidden, t * M + n + 1)
                        at_least(act, s.moe_masked, t * M + n - 2)
                        nc.scalar.activation(hr[:, slot(n + 2 * par), :], ps[:, slot(n + 2 * par), :], ACT.Relu,
                                             bias=w("b1", n, 1)).then_inc(s.moe_relu, 1)
                for t in range(2):
                    body(t, t)
                with act.Fori(1, NT // 2) as turn:
                    i = turn * 2
                    for par in range(2):
                        body(i + par, par)

            @block.vector
            def _(dve):
                def body(t, par):
                    for n, (e, c) in enumerate(units):
                        dve.wait_ge(s.moe_relu, t * M + n + 1)
                        at_least(dve, s.moe_out, t * M + n - 2)
                        nc.vector.tensor_tensor(hm[:, slot(n + 2 * par), :], hr[:, slot(n + 2 * par), :], ps[:, 3 + e % 2, :],
                                                ALU.mult).then_inc(s.moe_masked, 1)
                    dve.wait_ge(s.moe_out, t * M + M)
                    nc.vector.tensor_copy(k.Y[:, tok(t)], ps[:, 5 + par, :]).then_inc(s.moe_stored, 1)
                for t in range(2):
                    body(t, t)
                with dve.Fori(1, NT // 2) as turn:
                    i = turn * 2
                    for par in range(2):
                        body(i + par, par)


def ternary(k, call, wt):
    nc, s, ps = k.nc, k.s, k.ps
    n = 512
    with ExitStack() as ctx:
        part = ctx.enter_context(nc.sbuf_tensor(f"tern_part{call}", [P, 2], F32))
        lim = ctx.enter_context(nc.sbuf_tensor(f"tern_lim{call}", [P, 3], F32))
        lowt = ctx.enter_context(nc.sbuf_tensor(f"tern_low{call}", [P, n], F32))
        hi = ctx.enter_context(nc.sbuf_tensor(f"tern_hi{call}", [P, n], F32))
        block = ctx.enter_context(nc.Block())

        @block.vector
        def _(dve):
            base = 8 * call

            def then(m, j):
                m.then_inc(s.tern, 1)
                dve.wait_ge(s.tern, base + j)
            then(nc.vector.tensor_reduce(part[:, 0:1], wt, AX.X, ALU.add, apply_absolute_value=True), 1)
            dve.wait_ge(s.tern_mean, call + 1)
            then(nc.vector.tensor_scalar(lim[:, 0:1], ps[:, 0, 0:1], 1.0 / n, 1e-8, ALU.mult, ALU.max), 2)
            then(nc.vector.tensor_scalar(lim[:, 1:2], lim[:, 0:1], 0.5, None, ALU.mult), 3)
            then(nc.vector.tensor_scalar(lim[:, 2:3], lim[:, 0:1], -0.5, None, ALU.mult), 4)
            then(nc.vector.tensor_scalar(hi[:], wt, lim[:, 1:2], None, ALU.is_gt), 5)
            then(nc.vector.tensor_scalar(lowt[:], wt, lim[:, 2:3], None, ALU.is_lt), 6)
            then(nc.vector.tensor_tensor(hi[:], hi[:], lowt[:], ALU.subtract), 7)
            nc.vector.tensor_tensor(lowt[:], hi[:], wt, ALU.subtract).then_inc(s.tern_step, 1)
            dve.wait_ge(s.tern_step, 2 * call + 1)
            nc.vector.tensor_tensor(wt, wt, lowt[:], ALU.add).then_inc(s.tern_step, 1)
            nc.vector.sem_inc(s.tern, 1)

        @block.tensor
        def _(pe):
            pe.wait_ge(s.tern, 8 * call + 1)
            nc.tensor.matmul(ps[:, 0, 0:1], k.cf("mean"), part[:, 0:1], start=True, stop=True).then_inc(s.tern_mean, 1)


def fold_products(k, sem, jobs):
    nc, ps = k.nc, k.ps
    done = k.folds
    k.folds += len(jobs)
    with nc.Block() as block:
        @block.tensor
        def _(pe):
            for j, (out, pairs) in enumerate(jobs):
                m, n = out.shape[0], out.shape[-1]
                for e, (a, b) in enumerate(pairs):
                    mm = nc.tensor.matmul(ps[0:m, j, 0:n], a, b, start=(e == 0), stop=(e == len(pairs) - 1))
                mm.then_inc(k.s.fold, 1)

        @block.vector
        def _(dve):
            for j, (out, pairs) in enumerate(jobs):
                m, n = out.shape[0], out.shape[-1]
                dve.wait_ge(k.s.fold, done + j + 1)
                nc.vector.tensor_copy(out, ps[0:m, j, 0:n]).then_inc(k.s.folded, 1)


def linear(k, weight, bias, src, dst):
    nc, s, ps = k.nc, k.s, k.ps
    with nc.Block() as block:
        @block.tensor
        def _(pe):
            for t in range(NT):
                nc.tensor.matmul(ps[:, t, :], weight, src[:, t * TILE:(t + 1) * TILE], start=True, stop=True
                                 ).then_inc(s.lin_product, 1)

        @block.vector
        def _(dve):
            for t in range(NT):
                dve.wait_ge(s.lin_product, t + 1)
                nc.vector.tensor_scalar(dst[:, t * TILE:(t + 1) * TILE], ps[:, t, :], bias, None, ALU.add
                                        ).then_inc(s.lin_done, 1)


def gated_residual(k, call, out=None):
    nc, s = k.nc, k.s
    W = 2 * TILE
    NC = N // W
    with nc.Block() as block:
        @block.scalar
        def _(act):
            for c in range(NC):
                cols = slice(c * W, (c + 1) * W)
                nc.scalar.activation(k.Y[:, cols], k.Y[:, cols], ACT.Silu).then_inc(s.silu, 1)

        @block.vector
        def _(dve):
            for c in range(NC):
                cols = slice(c * W, (c + 1) * W)
                dve.wait_ge(s.silu, call * NC + c + 1)
                nc.vector.tensor_tensor(k.Y[:, cols], k.S[:, cols], k.Y[:, cols], ALU.mult).then_inc(s.gate_times, 1)
                dve.wait_ge(s.gate_times, call * NC + c + 1)
                nc.vector.tensor_tensor(k.X[:, cols], k.X[:, cols], k.Y[:, cols], ALU.add).then_inc(s.gate_added, 1)

        if out is not None:
            @block.sync
            def _(sp):
                for c in range(NC):
                    cols = slice(c * W, (c + 1) * W)
                    sp.wait_ge(s.gate_added, call * NC + c + 1)
                    sp.dma_start(out[:, cols], k.X[:, cols]).then_inc(s.out_stored, 16)
                sp.wait_ge(s.out_stored, 16 * NC)


class Signals:

    def __init__(self, new):
        self.load_x = new("load_x")
        self.load_const = new("load_const")
        self.load_l0a = new("load_l0a")
        self.load_l0f = new("load_l0f")
        self.load_l1 = new("load_l1")
        self.load_moe = new("load_moe")
        self.load_l2 = new("load_l2")
        self.load_l3 = new("load_l3")
        self.cast = new("cast")
        self.credit = new("credit")
        self.ln_free = new("ln_free")
        self.ln_zero = new("ln_zero")
        self.ln_shifted = new("ln_shifted")
        self.ln_centred = new("ln_centred")
        self.ln_squared = new("ln_squared")
        self.ln_var = new("ln_var")
        self.ln_rstd = new("ln_rstd")
        self.ln_rstd2 = new("ln_rstd2")
        self.ln_vy2 = new("ln_vy2")
        self.ln_exact = new("ln_exact")
        self.ln_affine = new("ln_affine")
        self.rms_free = new("rms_free")
        self.rms_product = new("rms_product")
        self.rms_squared = new("rms_squared")
        self.rms_mean = new("rms_mean")
        self.rms_rstd = new("rms_rstd")
        self.rms_rstd2 = new("rms_rstd2")
        self.rms_vy2 = new("rms_vy2")
        self.rms_exact = new("rms_exact")
        self.rms_weight = new("rms_weight")
        self.ff_gelu = new("ff_gelu")
        self.ff_value = new("ff_value")
        self.ff_value_used = new("ff_value_used")
        self.ff_gate = new("ff_gate")
        self.ff_hid_used = new("ff_hid_used")
        self.ff_out_used = new("ff_out_used")
        self.mix_used = new("mix_used")
        self.mix_product = new("mix_product")
        self.mix_sigmoid = new("mix_sigmoid")
        self.gate_product = new("gate_product")
        self.gate_ready = new("gate_ready")
        self.sp_step = new("sp_step")
        self.sp_max = new("sp_max")
        self.sp_coef = new("sp_coef")
        self.decay = new("decay")
        self.decay2 = new("decay2")
        self.keep = new("keep")
        self.scaled = new("scaled")
        self.reset = new("reset")
        self.scanned = new("scanned")
        self.gated = new("gated")
        self.hs2 = new("hs2")
        self.la_init = new("la_init")
        self.la_shifted = new("la_shifted")
        self.la_vprod = new("la_vprod")
        self.la_rot = new("la_rot")
        self.la_rotated = new("la_rotated")
        self.la_qk = new("la_qk")
        self.la_stored = new("la_stored")
        self.la_squared = new("la_squared")
        self.la_product = new("la_product")
        self.la_rnorm = new("la_rnorm")
        self.la_rnorm2 = new("la_rnorm2")
        self.la_vy2 = new("la_vy2")
        self.la_exact = new("la_exact")
        self.la_clamped = new("la_clamped")
        self.la_vread = new("la_vread")
        self.la_norm = new("la_norm")
        self.la_max = new("la_max")
        self.la_score = new("la_score")
        self.la_m2 = new("la_m2")
        self.la_shift = new("la_shift")
        self.la_mt = new("la_mt")
        self.la_prob = new("la_prob")
        self.la_keyed = new("la_keyed")
        self.la_divided = new("la_divided")
        self.la_attended = new("la_attended")
        self.la_turn = new("la_turn")
        self.la_turned = new("la_turned")
        self.la_out = new("la_out")
        self.la_table = new("la_table")
        self.la_rec = new("la_rec")
        self.at_parts = new("at_parts")
        self.at_stacked = new("at_stacked")
        self.at_scratch = new("at_scratch")
        self.at_keyed = new("at_keyed")
        self.at_init = new("at_init")
        self.at_vprod = new("at_vprod")
        self.at_fetched = new("at_fetched")
        self.at_used = new("at_used")
        self.at_product = new("at_product")
        self.at_vread = new("at_vread")
        self.at_max = new("at_max")
        self.at_score = new("at_score")
        self.at_m2 = new("at_m2")
        self.at_shift = new("at_shift")
        self.at_mt = new("at_mt")
        self.at_prob = new("at_prob")
        self.at_divided = new("at_divided")
        self.at_attended = new("at_attended")
        self.at_turn = new("at_turn")
        self.at_turned = new("at_turned")
        self.at_stored = new("at_stored")
        self.at_out = new("at_out")
        self.at_rec = new("at_rec")
        self.at_hi = new("at_hi")
        self.at_res = new("at_res")
        self.at_mid = new("at_mid")
        self.at_sum = new("at_sum")
        self.at_content = new("at_content")
        self.at_kv = new("at_kv")
        self.alibi_loaded = new("alibi_loaded")
        self.alibi_cast = new("alibi_cast")
        self.alibi_rows = new("alibi_rows")
        self.moe_iota = new("moe_iota")
        self.moe_scores = new("moe_scores")
        self.moe_fetched = new("moe_fetched")
        self.moe_hot = new("moe_hot")
        self.moe_turn = new("moe_turn")
        self.moe_turned = new("moe_turned")
        self.moe_pick = new("moe_pick")
        self.moe_masked = new("moe_masked")
        self.moe_stored = new("moe_stored")
        self.moe_out = new("moe_out")
        self.moe_relu = new("moe_relu")
        self.moe_hidden = new("moe_hidden")
        self.tern = new("tern")
        self.tern_mean = new("tern_mean")
        self.tern_step = new("tern_step")
        self.fold = new("fold")
        self.folded = new("folded")
        self.lin_product = new("lin_product")
        self.lin_done = new("lin_done")
        self.silu = new("silu")
        self.gate_times = new("gate_times")
        self.gate_added = new("gate_added")
        self.out_stored = new("out_stored")


def program(nc, x, cast, conf, rope0, alibi_q, alibi_k, l0a, l0f0, l0f1, l1, moe, l2, l3, out, stop=99):
    with ExitStack() as ctx:
        k = Core()
        s = Signals(lambda name: ctx.enter_context(nc.semaphore(name)))
        k.nc, k.s = nc, s
        sb = lambda n, shape, dt=F32: ctx.enter_context(nc.sbuf_tensor(n, shape, dt))
        k.X, k.XN, k.S, k.Y = (sb(n, [P, N]) for n in ("x", "xn", "s", "y"))
        castt = sb("cast", [P, CAST[1]], BF16)
        conft = sb("conf", [P, CONF[1]])
        k.eps5, k.eps6 = sb("eps5", [P, 1]), sb("eps6", [P, 1])
        k.cb, k.cf = pack(castt, CAST[0]), pack(conft, CONF[0])
        k.ps = ctx.enter_context(nc.psum_tensor("ps", [P, 8, TILE], F32))
        k.shifts = k.rounds = k.stack_dmas = k.folds = 0
        raw = k.Y[:, 0:CAST[1]]

        def dump(buf):
            with nc.Block() as block:
                @block.sync
                def _(sp):
                    sp.dma_start(out, buf[:]).then_inc(s.out_stored, 16)
                    sp.wait_ge(s.out_stored, 16)

        stack = ExitStack()
        with stack:
            new = lambda n, shape, dt=F32: stack.enter_context(nc.sbuf_tensor(n, shape, dt))
            f0, f1, r0 = new("w_l0f0", [P, W_L0F[1]]), new("w_l0f1", [P, W_L0F[1]]), new("w_l0t", [P, W_L0T[1]])
            with nc.sbuf_tensor("w_l0a", [P, W_L0A[1]], F32) as a0:
                with nc.Block() as block:
                    @block.sync
                    def _(sp):
                        sp.dma_start(conft[:], conf).then_inc(s.load_const, 16)
                        for t in range(4):
                            cols = slice(t * N // 4, (t + 1) * N // 4)
                            sp.dma_start(k.X[:, cols], x[:, cols]).then_inc(s.load_x, 16)
                        sp.dma_start(raw, cast).then_inc(s.load_const, 16)
                        sp.dma_start(a0[:], l0a).then_inc(s.load_l0a, 16)
                        sp.dma_start(r0[:], rope0).then_inc(s.load_l0f, 16)
                        sp.dma_start(f0[:], l0f0).then_inc(s.load_l0f, 16)
                        sp.dma_start(f1[:], l0f1).then_inc(s.load_l0f, 16)
                        sp.wait_ge(s.load_x, 64)
                        sp.wait_ge(s.load_l0a, 16)
                        sp.wait_ge(s.load_l0f, 48)

                    @block.vector
                    def _(dve):
                        nc.vector.memset(k.eps5[:], 1e-5).then_inc(s.credit, 1)
                        nc.vector.memset(k.eps6[:], 1e-6).then_inc(s.credit, 1)
                        nc.vector.sem_inc(s.ln_free, U)
                        nc.vector.sem_inc(s.rms_free, U)
                        nc.vector.sem_inc(s.ff_gelu, CREDIT)
                        nc.vector.sem_inc(s.ff_value_used, CREDIT)
                        nc.vector.sem_inc(s.ff_hid_used, CREDIT)
                        nc.vector.sem_inc(s.ff_out_used, 2)
                        nc.vector.sem_inc(s.mix_used, 2)
                        dve.wait_ge(s.load_const, 32)
                        nc.vector.tensor_copy(castt[:], raw).then_inc(s.cast, 1)

                layer_norm(k, 0, k.X, k.XN)
                if stop == 1:
                    return dump(k.XN)
                w = pack(a0, W_L0A[0])
                with ExitStack() as inner:
                    work = [inner.enter_context(nc.sbuf_tensor(n, [P, N], F32)) for n in ("mix_h", "mix_gate")]
                    recurrent_mixer(k, w, work)
            if stop == 2:
                return dump(k.S)
            rope = pack(r0, W_L0T[0])
            hid = k.XN
            for layer, t in enumerate((f0, f1)):
                w = pack(t, W_L0F[0])
                src = k.XN if layer == 0 else k.Y
                local_attention(k, layer, w, rope, src, k.Y)
                if stop == 3 + 2 * layer:
                    return dump(k.Y)
                layer_norm(k, 1 + layer, k.Y, hid, shift=True, affine=(w("lg"), w("lb")))
                feed_forward(k, 1 + layer, NT * 3 * (1 + layer), hid, HCH,
                             lambda lo, n: w("w1", HID + lo, n), lambda c, n: w("b1g", c, 1, rows=n),
                             lambda lo, n: w("w1", lo, n), lambda c, n: w("b1a", c, 1, rows=n),
                             lambda c, n: w("w2", c * P, P, rows=n), w("b2"), k.Y, k.Y)
                if stop == 4 + 2 * layer:
                    return dump(k.Y)
            gated_residual(k, 0)
        if stop == 7:
            return dump(k.X)

        with ExitStack() as inner:
            t1 = inner.enter_context(nc.sbuf_tensor("w_l1", [P, W_L1[1]], F32))
            tm = inner.enter_context(nc.sbuf_tensor("w_moe", [P, W_MOE[1]], F32))
            with nc.Block() as block:
                @block.sync
                def _(sp):
                    sp.dma_start(t1[:], l1).then_inc(s.load_l1, 16)
                    sp.dma_start(tm[:], moe).then_inc(s.load_moe, 16)
                    sp.wait_ge(s.load_l1, 16)
            layer_norm(k, 3, k.X, k.XN)
            alibi_attention(k, pack(t1, W_L1[0]), (alibi_q, alibi_k))
            if stop == 8:
                return dump(k.S)
            with nc.Block() as block:
                @block.sync
                def _(sp):
                    sp.wait_ge(s.load_moe, 16)
            experts(k, pack(tm, W_MOE[0]))
            if stop == 9:
                return dump(k.Y)
            gated_residual(k, 1)
        if stop == 10:
            return dump(k.X)

        with ExitStack() as inner:
            t2 = inner.enter_context(nc.sbuf_tensor("w_l2", [P, W_L2[1]], F32))
            fold = inner.enter_context(nc.sbuf_tensor("l2_fold", [P, 5, P], F32))
            w2 = pack(t2, W_L2[0])
            with nc.Block() as block:
                @block.sync
                def _(sp):
                    sp.dma_start(t2[:], l2).then_inc(s.load_l2, 16)
                    sp.wait_ge(s.load_l2, 16)
            layer_norm(k, 4, k.X, k.XN)
            qa, kva = w2("qaT", rows=64), w2("kvaT", rows=32)
            fold_products(k, None, [(fold[:, 0, :], [(qa, w2("qb", rows=64))]), (fold[:, 1, :], [(qa, w2("qbr", rows=64))]),
                                    (fold[:, 2, :], [(kva, w2("kb", rows=32))]), (fold[:, 3, :], [(kva, w2("kbr", rows=32))]),
                                    (fold[:, 4, :], [(kva, w2("vb", rows=32))])])
            rope8_attention(k, w2, fold)
            if stop == 11:
                return dump(k.S)
            ternary(k, 0, w2("f1"))
            ternary(k, 1, w2("f2"))
            feed_forward(k, 3, NT * 9, k.XN, [(c * P, P) for c in range(4)], lambda lo, n: w2("f1", lo, n),
                         lambda c, n: w2("f1b", c, 1), None, None, lambda c, n: w2("f2", c * P, P), w2("f2b"), None, k.Y)
            if stop == 12:
                return dump(k.Y)
            gated_residual(k, 2)
        if stop == 13:
            return dump(k.X)

        with ExitStack() as inner:
            t3 = inner.enter_context(nc.sbuf_tensor("w_l3", [P, W_L3[1]], F32))
            fold = inner.enter_context(nc.sbuf_tensor("l3_fold", [P, 5 * P], F32))
            w3 = pack(t3, W_L3[0])
            with nc.Block() as block:
                @block.sync
                def _(sp):
                    sp.dma_start(t3[:], l3).then_inc(s.load_l3, 16)
                    sp.wait_ge(s.load_l3, 16)
            layer_norm(k, 5, k.X, k.XN)
            qa = w3("qT", rows=64)
            fold_products(k, None, [(fold[:, 0:P], [(qa, w3("qd", rows=64))]), (fold[:, P:5 * P], [(qa, w3("qr", rows=64))])])
            rms_norm(k, 2, None, k.Y, w3("gkv", rows=32), rows=32, mean="mean32", before=(w3("wkv"), k.XN))
            latent_attention(k, w3, fold, k.Y)
            if stop == 14:
                return dump(k.S)
            with ExitStack() as dft:
                AT = dft.enter_context(nc.sbuf_tensor("dft_at", [P, 2, P], F32))
                M = dft.enter_context(nc.sbuf_tensor("dft_m", [P, P], F32))
                fold_products(k, None, [(AT[:, 0, :], [(w3("fr"), w3("dc")), (w3("fi"), w3("ds"))]),
                                        (AT[:, 1, :], [(w3("fi"), w3("dc")), (w3("fr"), w3("dsn"))])])
                fold_products(k, None, [(M[:], [(AT[:, 0, :], w3("dcm")), (AT[:, 1, :], w3("dsm"))])])
                linear(k, M[:], w3("fb"), k.XN, k.Y)
                if stop == 15:
                    return dump(k.Y)
                gated_residual(k, 3, out)


def lay(where, **parts):
    packed = np.zeros((P, where[1]), np.float32)
    for name, a in parts.items():
        at, n = where[0][name]
        a = np.asarray(a)
        a = a.reshape(a.shape[0], -1)
        assert a.shape[1] == n, (name, a.shape, n)
        packed[:a.shape[0], at:at + n] = a
    return packed


def chunked(a, rows=P):
    return a.reshape(-1, rows, a.shape[1]).transpose(1, 0, 2).reshape(rows, -1)


def columns(v):
    return v.reshape(-1, P).T


def padded(a, sizes):
    out, at = [], 0
    for n in sizes:
        out.append(np.concatenate([a[at:at + n], np.zeros((P - n, a.shape[1]), a.dtype)], 0))
        at += n
    return np.concatenate(out, 1)


def kernel(**inputs):
    import concourse.bacc as bacc
    from concourse.bass_utils import run_bass_kernel_spmd
    v = {n: np.asarray(a) for n, a in inputs.items()}
    g = lambda layer: {n[len(layer):]: a for n, a in v.items() if n.startswith(layer)}
    packs = {}
    packs["x"] = np.ascontiguousarray(v["L0_attn_hidden_states"].reshape(N, P).T)
    packs["cast"] = np.concatenate([a for _, a in const_cast()], 1).astype(np.float32)
    packs["conf"] = np.concatenate([a for _, a in const_f32()], 1).astype(np.float32)
    packs["rope0"] = np.concatenate([a for _, a in const_local_rope()], 1).astype(np.float32)
    packs["alibi_q"], packs["alibi_k"] = const_alibi()
    a = g("L0_attn_")
    col = lambda x: x.reshape(-1, 1)
    packs["l0a"] = lay(W_L0A, fc=a["fc_w"].T, fr=a["fc_r_w"].T, fi=a["fc_i_w"].T, gate=a["fc_gate_w"].T,
                       mg=a["mlp_gate_w"].T, mf=a["mlp_fc_w"].T, mo=chunked(a["out_w"].T), fc_b=col(a["fc_b"]),
                       fr_b=col(a["fc_r_b"]), fi_b=col(a["fc_i_b"]), gate_b=col(a["fc_gate_b"]), norm=col(a["norm_w"]),
                       norm2=col(a["norm2_w"]), alpha=col(a["alpha"]), mo_b=col(a["out_b"]),
                       mg_b=columns(a["mlp_gate_b"]), mf_b=columns(a["mlp_fc_b"]))
    a = g("L0_ffn_")
    rot = np.arange(512) // 64 * 64 + (np.arange(512) % 64 + 32) % 64
    half = (np.arange(64) + 32) % 64
    two = lambda x: col(np.concatenate([x, x]))
    sizes = [n for _, n in HCH]
    for l in range(2):
        wq, wk, wv = np.split(a["wqkv"][l], 3, 1)
        b1 = a["b1"][l].reshape(-1, 1)
        packs[f"l0f{l}"] = lay(W_L0F, wq=wq, wqr=wq[:, rot], wk=wk, wkr=wk[:, rot], wv=wv, wo=chunked(a["wo"][l]),
                               w1=a["w1"][l], w2=padded(a["w2"][l], sizes), qs=two(a["q_scale"][l]),
                               qsr=two(a["q_scale"][l][half]), ks=two(a["k_scale"][l]), ksr=two(a["k_scale"][l][half]),
                               lg=col(a["ln_g"][l]), lb=col(a["ln_b"][l]), b1a=padded(b1[:HID], sizes),
                               b1g=padded(b1[HID:], sizes), b2=col(a["b2"][l]))
    a = g("L1_attn_")
    wq, wk, wv = np.split(a["w_attn"], 3, 0)
    packs["l1"] = lay(W_L1, wq=wq.T[:, DH], wk=wk.T[:, DH], wv=wv.T, wo=a["w_proj"].T)
    a = g("L1_ffn_")
    packs["moe"] = lay(W_MOE, wg=a["Wg"], bg=a["bg"].reshape(1, -1), w1=a["W1"].transpose(1, 0, 2),
                       w2=chunked(a["W2"].reshape(-1, P)), b1=columns(a["b1"]), b2=a["b2"])
    a, f = g("L2_attn_"), g("L2_ffn_")
    kv = a["Wkvb"].reshape(-1, 4, D8, 2)
    kb = np.repeat(kv[..., 0], 4, 1).reshape(-1, P)
    vb = np.repeat(kv[..., 1], 4, 1).reshape(-1, P)
    swap = [h * D8 + (d ^ 1) for d in range(D8) for h in range(H16)]
    packs["l2"] = lay(W_L2, qaT=a["Wqa"].T, qb=a["Wqb"][:, DH], qbr=a["Wqb"][:, swap], kvaT=a["Wkva"].T, kb=kb[:, DH],
                      kbr=kb[:, swap], vb=vb, wo=a["Wout"], bo=col(a["bout"]),
                      cos=dict(const_rope8())["cos"], sin=dict(const_rope8())["sin"],
                      f1=f["W1"].T, f1b=columns(f["b1"]), f2=chunked(f["W2"].T), f2b=col(f["b2"]))
    a, f = g("L3_attn_"), g("L3_ffn_")
    dh32 = [h * 32 + d for d in range(32) for h in range(H16)]
    packs["l3"] = lay(W_L3, wkv=a["W_kv"], gkv=col(a["g_kv"]), kd=a["W_kdec"][:, DH], vd=a["W_vdec"], qT=a["W_q"].T,
                      qd=a["W_qdec"][:, DH], qr=a["W_qrope"][:, dh32], kr=a["W_krope"][:, dh32], wo=a["W_o"],
                      fr=f["w_freq_real"], fi=f["w_freq_imag"], fb=col(f["bias"]),
                      **dict(const_rope32()), **dict(const_dft()))
    nc = bacc.Bacc("TRN2", target_bir_lowering=False, num_devices=1)
    args = [nc.dram_tensor(f"in_{n}", p.shape, F32, kind="ExternalInput").ap() for n, p in packs.items()]
    out = nc.dram_tensor("out_0", (P, N), F32, kind="ExternalOutput").ap()
    program(nc, *args, out)
    r = run_bass_kernel_spmd(nc, [{f"in_{n}": np.ascontiguousarray(p) for n, p in packs.items()}], core_ids=[0])
    return np.ascontiguousarray(r.results[0]["out_0"].T).reshape(B, L, P)
```

```python
from contextlib import ExitStack

import numpy as np

import concourse.bass as bass
from concourse import mybir

ALU = mybir.AluOpType
ACT = mybir.ActivationFunctionType
AX = mybir.AxisListType
F32 = mybir.dt.float32
BF16 = mybir.dt.bfloat16

P = 128
B, L = 16, 256
N = B * L
TILE = 512
NT = N // TILE
U = 4
H16, D8 = 16, 8
GW = 64
KEY_LAG, VALUE_LAG = 4, 6
ROUND = 3
RING = 4
H8, D64 = 8, 64
HID = 341
HCH = [(0, 128), (128, 128), (256, HID - 256)]
FCH = [(0, 128), (128, 128), (256, 128)]
NEXP, EH = 8, 512
BIG = -1e30
CREDIT = 3


def const_cast():
    i = np.arange(P)
    ident = np.eye(P)
    causal = np.where(i[None, :] <= i[:, None], 0.0, BIG)
    band = lambda q, k: np.where((q - k >= 0) & (q - k <= 64), 0.0, BIG)
    q, k, j = i[:, None], i[None, :], np.arange(192)[None, :]
    local_q0 = band(q, k)
    local_q1 = band(q + 128, j + 64)
    local_k0 = band(j, i[:, None])
    sel = np.zeros((P, H16, P))
    for h in range(H16):
        sel[h, h] = sel[32 + h, h] = 1.0
    parts = [("ident", ident), ("causal_q", causal), ("causal_k", causal.T), ("local_q0", local_q0),
             ("local_q1", local_q1), ("local_k0", local_k0), ("sel", sel.reshape(P, -1))]
    return parts


def const_f32():
    c = np.arange(P)
    blk = (c[:, None] // 32 == c[None, :] // 32).astype(np.float64)
    return [("centre", np.eye(P) - 1.0 / P), ("mean", np.full((P, P), 1.0 / P)), ("block32", blk), ("identf", np.eye(P)),
            ("mean32", np.full((P, 32), 1.0 / 32)), ("ones", np.ones((P, P)))]


def const_local_rope():
    half = np.arange(0, D64, 2, dtype=np.float32)
    inv = np.float32(1.0) / np.float32(10000.0) ** (half / np.float32(D64))
    t = np.arange(L, dtype=np.float32)
    fr = (t[:, None] * inv[None, :]).astype(np.float32).astype(np.float64).T
    base = (half.astype(np.float64) + 0.4 * D64) / (1.4 * D64)
    power = (t.astype(np.float64) - L // 2) / 32.0
    sc = (base[None, :] ** power[:, None]).T
    four = lambda a: -0.5 * np.concatenate([a] * 4, 0)
    return [("qc", four(np.cos(fr) * sc)), ("qs", four(np.sin(fr) * sc)),
            ("kc", four(np.cos(fr) / sc)), ("ks", four(np.sin(fr) / sc))]


def const_rope8():
    inv = np.float32(1.0) / np.float32(10000.0) ** (np.arange(0, D8, 2, dtype=np.float32) / np.float32(D8))
    fr = np.outer(np.arange(L, dtype=np.float32), inv).astype(np.float32).astype(np.float64)
    d = np.arange(P) // H16
    cos, sin = np.cos(fr)[:, d // 2].T, np.sin(fr)[:, d // 2].T
    return [("cos", cos), ("sin", np.where(d % 2 == 0, -1.0, 1.0)[:, None] * sin)]


def const_rope32():
    inv = np.float32(1.0) / np.float32(10000.0) ** (np.arange(0, 32, 2, dtype=np.float32) / np.float32(32))
    fr = np.outer(np.arange(L, dtype=np.float32), inv).astype(np.float32).astype(np.float64)
    cos, sin = [], []
    for c in range(2):
        d = 8 * c + np.arange(P) // H16
        cos += [np.cos(fr)[:, d].T] * 2
        sin += [-np.sin(fr)[:, d].T, np.sin(fr)[:, d].T]
    return [("cos", np.concatenate(cos, 1)), ("sin", np.concatenate(sin, 1))]


def const_dft():
    a = 2 * np.pi * (np.outer(np.arange(P), np.arange(P)) % P) / P
    return [("dc", np.cos(a)), ("ds", np.sin(a)), ("dsn", -np.sin(a)), ("dcm", np.cos(a) / P), ("dsm", -np.sin(a) / P)]


def const_alibi():
    slopes = np.array([(2.0 ** -0.5) ** (h + 1) for h in range(H16)])
    v = (slopes[:, None] * np.sqrt(8.0) * np.arange(L)[None, :]).astype(np.float32)

    def bf(a):
        u = a.astype(np.float32).view(np.uint32)
        u = (u + 0x7FFF + ((u >> 16) & 1)) & np.uint32(0xFFFF0000)
        return u.view(np.float32)

    hi = bf(v)
    mid = bf(v - hi)
    lo = v - hi - mid
    rows = np.stack([hi, mid, lo]).reshape(3, -1)
    ones = np.ones_like(rows)
    return np.concatenate([ones, -rows], 0), np.concatenate([rows, ones], 0)


def widths(parts):
    at, where = 0, {}
    for name, n in parts:
        where[name] = (at, n)
        at += n
    return where, at


CAST = widths([(n, a.shape[1]) for n, a in const_cast()])
CONF = widths([(n, a.shape[1]) for n, a in const_f32()])
DH = [d * 1 + h * D8 for d in range(D8) for h in range(H16)]
W_L0A = widths([("fc", P), ("fr", P), ("fi", P), ("gate", P), ("mg", 3 * P), ("mf", 3 * P), ("mo", 3 * P), ("fc_b", 1),
                ("fr_b", 1), ("fi_b", 1), ("gate_b", 1), ("norm", 1), ("norm2", 1), ("alpha", 1), ("mo_b", 1),
                ("mg_b", 3), ("mf_b", 3)])
W_L0F = widths([("wq", 512), ("wk", 512), ("wv", 512), ("wo", 512), ("w1", 2 * HID),
                ("w2", 3 * P), ("q1", 1), ("q2", 1), ("k1", 1), ("k2", 1), ("lg", 1), ("lb", 1), ("b1a", 3),
                ("b1g", 3), ("b2", 1)])
W_L0T = widths([("qc", L), ("qs", L), ("kc", L), ("ks", L)])
W_L1 = widths([("wq", P), ("wk", P), ("wv", P), ("wo", P)])
W_MOE = widths([("wg", NEXP), ("bg", NEXP), ("w1", NEXP * EH), ("w2", NEXP * EH), ("b1", NEXP * 4), ("b2", P)])
W_L2 = widths([("qaT", P), ("qb", P), ("qbr", P), ("kvaT", P), ("kb", P), ("kbr", P), ("vb", P), ("wo", P), ("bo", 1),
               ("cos", L), ("sin", L), ("f1", 512), ("f1b", 4), ("f2", 512), ("f2b", 1)])
W_L3 = widths([("wkv", 32), ("gkv", 1), ("kd", P), ("vd", P), ("qT", P), ("qd", P), ("qr", 512), ("kr", 512), ("wo", P),
               ("cos", 4 * L), ("sin", 4 * L), ("dc", P), ("ds", P), ("dsn", P), ("dcm", P), ("dsm", P), ("fr", P),
               ("fi", P), ("fb", 1)])


def pack(tile, where):
    def part(name, lo=0, n=None, rows=P):
        at, width = where[name]
        n = width - lo if n is None else n
        return tile[0:rows, at + lo:at + lo + n]
    return part


class Core:
    pass


def at_least(eng, sem, value):
    if isinstance(value, int) and value <= 0:
        return
    eng.wait_ge(sem, value)


def tok(t, n=TILE):
    return bass.ds(t * n, n)


def norm_steps(eng, *stages):
    for i in range(NT + max(lag for lag, _ in stages)):
        for lag, stage in stages:
            if 0 <= i - lag < NT:
                stage(i - lag)


def layer_norm(k, call, src, dst, shift=False, affine=None, gate=None):
    nc, s = k.nc, k.s
    base = call * NT
    cols = lambda t: slice(t * TILE, (t + 1) * TILE)
    with ExitStack() as ctx:
        sq = ctx.enter_context(nc.sbuf_tensor(f"ln_sq{call}", [P, U, TILE], F32))
        rs = ctx.enter_context(nc.sbuf_tensor(f"ln_rs{call}", [P, U, TILE], F32))
        y2 = ctx.enter_context(nc.sbuf_tensor(f"ln_y2{call}", [P, U, TILE], F32))
        hs = ctx.enter_context(nc.sbuf_tensor(f"ln_hs{call}", [P, U, TILE], F32)) if shift else None
        block = ctx.enter_context(nc.Block())

        if shift or gate is not None:
            @block.gpsimd
            def _(pool):
                if shift:
                    rows = hs[64:128, :, :].rearrange("p u (b l) -> p (u b) l", l=L)
                    nc.gpsimd.memset(rows[:, :, 0:1], 0.0).then_inc(s.ln_zero, 1)
                    pool.wait_ge(s.ln_zero, k.shifts + 1)
                for t in range(NT):
                    if shift:
                        pool.wait_ge(s.ln_free, base + t + 1)
                        nc.gpsimd.tensor_copy(hs[0:64, t % U, :], src[0:64, cols(t)]).then_inc(s.ln_copied, 1)
                    else:
                        pool.wait_ge(s.gate_times, gate * NT + t + 1)
                        nc.gpsimd.tensor_tensor(src[:, cols(t)], src[:, cols(t)], k.Y[:, cols(t)], ALU.add
                                                ).then_inc(s.gate_added, 1)

        @block.tensor
        def _(pe):
            def centre(t):
                pe.wait_ge(s.ln_free, base + t + 1)
                if shift:
                    pe.wait_ge(s.ln_zero, k.shifts + 1)
                    pe.wait_ge(s.ln_copied, k.shifts * NT + t + 1)
                    pe.wait_ge(s.ln_shifted, k.shifts * NT + t + 1)
                if gate is not None:
                    pe.wait_ge(s.gate_added, gate * NT + t + 1)
                x = hs[:, t % U, :] if shift else src[:, cols(t)]
                nc.tensor.matmul(k.ps[:, t % U, :], k.cf("centre"), x, start=True, stop=True).then_inc(s.ln_centred, 1)

            def variance(t):
                pe.wait_ge(s.ln_squared, base + t + 1)
                nc.tensor.matmul(k.ps[:, U + t % U, :], k.cf("mean"), sq[:, t % U, :], start=True, stop=True
                                 ).then_inc(s.ln_var, 1)
            norm_steps(pe, (0, centre), (1, variance))

        @block.scalar
        def _(act):
            if gate is not None:
                for t in range(NT):
                    nc.scalar.activation(k.Y[:, cols(t)], k.Y[:, cols(t)], ACT.Silu).then_inc(s.silu, 1)

            def square(t):
                act.wait_ge(s.ln_centred, base + t + 1)
                nc.scalar.activation(sq[:, t % U, :], k.ps[:, t % U, :], ACT.Square).then_inc(s.ln_squared, 1)

            def rsqrt(t):
                act.wait_ge(s.ln_var, base + t + 1)
                nc.scalar.activation(rs[:, t % U, :], k.ps[:, U + t % U, :], ACT.Abs_reciprocal_sqrt, bias=k.eps5[:, 0:1]
                                     ).then_inc(s.ln_rstd, 1)

            def square_root(t):
                act.wait_ge(s.ln_rstd, base + t + 1)
                nc.scalar.activation(y2[:, t % U, :], rs[:, t % U, :], ACT.Square).then_inc(s.ln_rstd2, 1)
            norm_steps(act, (0, square), (2, rsqrt), (2, square_root))

        @block.vector
        def _(dve):
            if shift:
                dve.wait_ge(s.ln_zero, k.shifts + 1)

            def gated(t):
                if gate is not None:
                    dve.wait_ge(s.silu, gate * NT + t + 1)
                    nc.vector.tensor_tensor(k.Y[:, cols(t)], k.S[:, cols(t)], k.Y[:, cols(t)], ALU.mult
                                            ).then_inc(s.gate_times, 1)

            def shifted(t):
                if shift:
                    dve.wait_ge(s.ln_free, base + t + 1)
                    by_row = lambda v: v.rearrange("p (b l) -> p b l", l=L)
                    nc.vector.tensor_copy(by_row(hs[64:128, t % U, :])[:, :, 1:L], by_row(src[64:128, cols(t)])[:, :, 0:L - 1]
                                          ).then_inc(s.ln_shifted, 1)

            def exact(t):
                u = t % U
                dve.wait_ge(s.ln_rstd2, base + t + 1)
                nc.vector.scalar_tensor_tensor(out=y2[:, u, :], in0=k.ps[:, U + u, :], scalar=1e-5, in1=y2[:, u, :],
                                               op0=ALU.add, op1=ALU.mult).then_inc(s.ln_vy2, 1)
                dve.wait_ge(s.ln_vy2, base + t + 1)
                nc.vector.scalar_tensor_tensor(out=rs[:, u, :], in0=y2[:, u, :], scalar=-3.0, in1=rs[:, u, :],
                                               op0=ALU.add, op1=ALU.mult).then_inc(s.ln_exact, 1)
                dve.wait_ge(s.ln_exact, base + t + 1)
                nc.vector.scalar_tensor_tensor(out=dst[:, cols(t)], in0=rs[:, u, :], scalar=-0.5, in1=k.ps[:, u, :],
                                               op0=ALU.mult, op1=ALU.mult).then_inc(s.ln_free, 1)
                if affine:
                    dve.wait_ge(s.ln_free, base + U + t + 1)
                    nc.vector.tensor_scalar(dst[:, cols(t)], dst[:, cols(t)], affine[0], affine[1], ALU.mult, ALU.add
                                            ).then_inc(s.ln_affine, 1)
            norm_steps(dve, (0, gated), (0, shifted), (3, exact))
    if shift:
        k.shifts += 1


def rms_norm(k, call, src, dst, weight, rows=P, mean="mean", before=None):
    nc, s = k.nc, k.s
    base = call * NT
    cols = lambda t: slice(t * TILE, (t + 1) * TILE)
    with ExitStack() as ctx:
        sq = ctx.enter_context(nc.sbuf_tensor(f"rms_sq{call}", [P, U, TILE], F32))
        rs = ctx.enter_context(nc.sbuf_tensor(f"rms_rs{call}", [P, U, TILE], F32))
        y2 = ctx.enter_context(nc.sbuf_tensor(f"rms_y2{call}", [P, U, TILE], F32))
        wh = ctx.enter_context(nc.sbuf_tensor(f"rms_wh{call}", [P, 1], F32))
        block = ctx.enter_context(nc.Block())
        x = lambda t: k.ps[0:rows, t % U, :] if before else src[:, cols(t)]

        @block.tensor
        def _(pe):
            def product(t):
                if before:
                    pe.wait_ge(s.rms_free, base + t + 1)
                    nc.tensor.matmul(k.ps[0:rows, t % U, :], before[0], before[1][:, cols(t)], start=True, stop=True
                                     ).then_inc(s.rms_product, 1)

            def square_mean(t):
                pe.wait_ge(s.rms_squared, base + t + 1)
                nc.tensor.matmul(k.ps[0:rows, U + t % U, :], k.cf(mean, rows=rows, n=rows), sq[0:rows, t % U, :],
                                 start=True, stop=True).then_inc(s.rms_mean, 1)
            norm_steps(pe, (0, product), (1, square_mean))

        @block.scalar
        def _(act):
            def square(t):
                act.wait_ge(s.rms_free, base + t + 1)
                if before:
                    act.wait_ge(s.rms_product, t + 1)
                nc.scalar.activation(sq[0:rows, t % U, :], x(t), ACT.Square).then_inc(s.rms_squared, 1)

            def rsqrt(t):
                act.wait_ge(s.rms_mean, base + t + 1)
                nc.scalar.activation(rs[0:rows, t % U, :], k.ps[0:rows, U + t % U, :], ACT.Abs_reciprocal_sqrt,
                                     bias=k.eps6[0:rows, 0:1]).then_inc(s.rms_rstd, 1)

            def square_root(t):
                act.wait_ge(s.rms_rstd, base + t + 1)
                nc.scalar.activation(y2[0:rows, t % U, :], rs[0:rows, t % U, :], ACT.Square).then_inc(s.rms_rstd2, 1)
            norm_steps(act, (0, square), (2, rsqrt), (2, square_root))

        @block.vector
        def _(dve):
            nc.vector.tensor_scalar(wh[0:rows, :], weight, -0.5, None, ALU.mult).then_inc(s.rms_weight, 1)
            dve.wait_ge(s.rms_weight, call + 1)

            def exact(t):
                u = t % U
                dve.wait_ge(s.rms_rstd2, base + t + 1)
                nc.vector.scalar_tensor_tensor(out=y2[0:rows, u, :], in0=k.ps[0:rows, U + u, :], scalar=1e-6,
                                               in1=y2[0:rows, u, :], op0=ALU.add, op1=ALU.mult).then_inc(s.rms_vy2, 1)
                dve.wait_ge(s.rms_vy2, base + t + 1)
                nc.vector.scalar_tensor_tensor(out=rs[0:rows, u, :], in0=y2[0:rows, u, :], scalar=-3.0,
                                               in1=rs[0:rows, u, :], op0=ALU.add, op1=ALU.mult).then_inc(s.rms_exact, 1)
                dve.wait_ge(s.rms_exact, base + t + 1)
                nc.vector.scalar_tensor_tensor(out=dst[0:rows, cols(t)], in0=x(t), scalar=wh[0:rows, :],
                                               in1=rs[0:rows, u, :], op0=ALU.mult, op1=ALU.mult).then_inc(s.rms_free, 1)
            norm_steps(dve, (0, exact))


def feed_forward(k, call, units, src, chunks, gate_w, gate_b, value_w, value_b, out_w, out_b, resid, dst):
    nc, s = k.nc, k.s
    nch = len(chunks)
    base = call * NT
    RH = 3 if value_w else 4
    with ExitStack() as ctx:
        gl = ctx.enter_context(nc.sbuf_tensor(f"ff_gl{call}", [P, RH, TILE], F32))
        hid = ctx.enter_context(nc.sbuf_tensor(f"ff_hid{call}", [P, RH, TILE], F32))
        block = ctx.enter_context(nc.Block())
        seq = [(u, c) for u in range(U) for c in range(nch)]

        @block.tensor
        def _(pe):
            with pe.Fori(0, NT // U) as turn:
                i = turn * U
                def outs(n):
                    u, c = seq[n]
                    unit = units + i * nch + n
                    pe.wait_ge(s.ff_value_used if value_w else s.ff_gelu, unit + 1 + CREDIT)
                    if c == 0:
                        pe.wait_ge(s.ff_out_used, base + i + u + 1)
                    lo, w = chunks[c]
                    m = nc.tensor.matmul(k.ps[:, 6 + u % 2, :], out_w(c, w), hid[0:w, n % RH, :],
                                         start=(c == 0), stop=(c == nch - 1))
                    m.then_inc(s.ff_hid_used, 1)
                for n, (u, c) in enumerate(seq):
                    lo, w = chunks[c]
                    unit = units + i * nch + n
                    pe.wait_ge(s.ff_gelu, unit + 1)
                    x = src[:, tok(i + u)]
                    nc.tensor.matmul(k.ps[0:w, n % RH, :], gate_w(lo, w), x, start=True, stop=True
                                     ).then_inc(s.ff_gate, 1)
                    if value_w:
                        pe.wait_ge(s.ff_value_used, unit + 1)
                        nc.tensor.matmul(k.ps[0:w, 3 + n % RH, :], value_w(lo, w), x, start=True, stop=True
                                         ).then_inc(s.ff_value, 1)
                    if n >= 2:
                        outs(n - 2)
                outs(len(seq) - 2)
                outs(len(seq) - 1)

        @block.scalar
        def _(act):
            with act.Fori(0, NT // U) as turn:
                i = turn * U
                for n, (u, c) in enumerate(seq):
                    lo, w = chunks[c]
                    unit = units + i * nch + n
                    act.wait_ge(s.ff_gate, unit + 1)
                    if value_w:
                        act.wait_ge(s.ff_value_used, unit + 1)
                        to = gl[0:w, n % RH, :]
                    else:
                        act.wait_ge(s.ff_hid_used, unit + 1)
                        to = hid[0:w, n % RH, :]
                    g = nc.scalar.activation(to, k.ps[0:w, n % RH, :], ACT.Gelu, bias=gate_b(c, w))
                    g.then_inc(s.ff_gelu, 1)

        @block.vector
        def _(dve):
            with dve.Fori(0, NT // U) as turn:
                i = turn * U
                def finish(u):
                    t = i + u
                    dve.wait_ge(s.ff_hid_used, units + (t + 1) * nch + CREDIT)
                    if resid is None:
                        m = nc.vector.tensor_scalar(dst[:, tok(t)], k.ps[:, 6 + u % 2, :], out_b, None, ALU.add)
                    else:
                        m = nc.vector.scalar_tensor_tensor(out=dst[:, tok(t)], in0=k.ps[:, 6 + u % 2, :], scalar=out_b,
                                                           in1=resid[:, tok(t)], op0=ALU.add, op1=ALU.add)
                    m.then_inc(s.ff_out_used, 1)
                for n, (u, c) in enumerate(seq):
                    lo, w = chunks[c]
                    unit = units + i * nch + n
                    if value_w:
                        dve.wait_ge(s.ff_gelu, unit + 1 + CREDIT)
                        dve.wait_ge(s.ff_value, unit + 1)
                        dve.wait_ge(s.ff_hid_used, unit + 1)
                        nc.vector.scalar_tensor_tensor(out=hid[0:w, n % RH, :], in0=k.ps[0:w, 3 + n % RH, :],
                                                       scalar=value_b(c, w), in1=gl[0:w, n % RH, :],
                                                       op0=ALU.add, op1=ALU.mult).then_inc(s.ff_value_used, 1)
                    if c == nch - 1 and u >= 1:
                        finish(u - 1)
                finish(U - 1)


def recurrent_mixer(k, w, work):
    nc, s = k.nc, k.s
    XN, S, Y = k.XN, k.S, k.Y
    Hb, GT = work
    R, Uv = Y, S
    rms_norm(k, 0, XN, Hb, w("norm"))

    outer = ExitStack()
    sp = outer.enter_context(nc.sbuf_tensor("mix_sp", [P, 6], F32))
    with ExitStack() as ctx:
        ig = ctx.enter_context(nc.sbuf_tensor("mix_i", [P, 2, TILE], F32))
        block = ctx.enter_context(nc.Block())

        @block.tensor
        def _(pe):
            with pe.Fori(0, NT // 2) as turn:
                i = turn * 2
                for u in range(2):
                    pe.wait_ge(s.mix_used, i + u + 1)
                    for n, name in enumerate(("fr", "fi", "fc")):
                        nc.tensor.matmul(k.ps[:, 2 * n + u, :], w(name), Hb[:, tok(i + u)], start=True, stop=True
                                         ).then_inc(s.mix_product, 1)

        @block.scalar
        def _(act):
            nc.scalar.activation(sp[:, 0:1], w("alpha"), ACT.Abs).then_inc(s.sp_step, 1)
            act.wait_ge(s.sp_step, 1)
            nc.scalar.activation(sp[:, 1:2], sp[:, 0:1], ACT.Exp, scale=-1.0).then_inc(s.sp_step, 1)
            act.wait_ge(s.sp_step, 2)
            nc.scalar.activation(sp[:, 2:3], sp[:, 1:2], ACT.Ln, bias=k.cf("ones", n=1)).then_inc(s.sp_step, 1)
            with act.Fori(0, NT // 2) as turn:
                i = turn * 2
                for u in range(2):
                    act.wait_ge(s.mix_product, 3 * (i + u) + 2)
                    nc.scalar.activation(R[:, tok(i + u)], k.ps[:, u, :], ACT.Sigmoid, bias=w("fr_b"))
                    nc.scalar.activation(ig[:, u, :], k.ps[:, 2 + u, :], ACT.Sigmoid, bias=w("fi_b")
                                         ).then_inc(s.mix_sigmoid, 1)

        @block.vector
        def _(dve):
            nc.vector.tensor_scalar(sp[:, 3:4], w("alpha"), 0.0, None, ALU.max).then_inc(s.sp_max, 1)
            dve.wait_ge(s.sp_max, 1)
            dve.wait_ge(s.sp_step, 3)
            nc.vector.tensor_tensor(sp[:, 5:6], sp[:, 3:4], sp[:, 2:3], ALU.add).then_inc(s.sp_max, 1)
            dve.wait_ge(s.sp_max, 2)
            nc.vector.tensor_scalar(sp[:, 4:5], sp[:, 5:6], -8.0, None, ALU.mult).then_inc(s.sp_coef, 1)
            with dve.Fori(0, NT // 2) as turn:
                i = turn * 2
                for u in range(2):
                    dve.wait_ge(s.mix_sigmoid, i + u + 1)
                    dve.wait_ge(s.mix_product, 3 * (i + u) + 3)
                    nc.vector.scalar_tensor_tensor(out=Uv[:, tok(i + u)], in0=k.ps[:, 4 + u, :], scalar=w("fc_b"),
                                                   in1=ig[:, u, :], op0=ALU.add, op1=ALU.mult).then_inc(s.mix_used, 1)

    with outer as ctx:
        NC = N // (2 * TILE)
        a2 = ctx.enter_context(nc.sbuf_tensor("mix_a2", [P, NC, 2 * TILE], F32))
        block = ctx.enter_context(nc.Block())

        @block.tensor
        def _(pe):
            for t in range(NT):
                nc.tensor.matmul(k.ps[:, t, :], w("gate"), Hb[:, t * TILE:(t + 1) * TILE], start=True, stop=True
                                 ).then_inc(s.gate_product, 1)

        @block.scalar
        def _(act):
            act.wait_ge(s.sp_coef, 1)
            for c in range(NC):
                cols = slice(c * 2 * TILE, (c + 1) * 2 * TILE)
                nc.scalar.activation(R[:, cols], R[:, cols], ACT.Exp, scale=sp[:, 4:5]).then_inc(s.decay, 1)
            for c in range(NC):
                act.wait_ge(s.decay2, c + 1)
                nc.scalar.activation(a2[:, c, :], a2[:, c, :], ACT.Sqrt, scale=-1.0, bias=k.cf("ones", n=1)
                                     ).then_inc(s.keep, 1)
            for t in range(NT):
                act.wait_ge(s.gate_product, t + 1)
                nc.scalar.activation(GT[:, t * TILE:(t + 1) * TILE], k.ps[:, t, :], ACT.Gelu, bias=w("gate_b")
                                     ).then_inc(s.gate_ready, 1)

        @block.gpsimd
        def _(pool):
            for c in range(NC):
                cols = slice(c * 2 * TILE, (c + 1) * 2 * TILE)
                pool.wait_ge(s.decay, c + 1)
                nc.gpsimd.tensor_tensor(a2[:, c, :], R[:, cols], R[:, cols], ALU.mult).then_inc(s.decay2, 1)
            for t in range(NT):
                cols = slice(t * TILE, (t + 1) * TILE)
                pool.wait_ge(s.gated, t + 1)
                nc.gpsimd.tensor_tensor(Uv[:, cols], Uv[:, cols], XN[:, cols], ALU.add).then_inc(s.hs2, 1)

        @block.vector
        def _(dve):
            for c in range(NC):
                cols = slice(c * 2 * TILE, (c + 1) * 2 * TILE)
                dve.wait_ge(s.decay2, c + 1)
                nc.vector.memset(R[:, cols].rearrange("p (b l) -> p b l", l=L)[:, :, 0:1], 0.0).then_inc(s.reset, 1)
                dve.wait_ge(s.keep, c + 1)
                nc.vector.tensor_tensor(Uv[:, cols], Uv[:, cols], a2[:, c, :], ALU.mult).then_inc(s.scaled, 1)
                dve.wait_ge(s.scaled, c + 1)
                dve.wait_ge(s.reset, c + 1)
                nc.vector.tensor_tensor_scan(Uv[:, cols], R[:, cols], Uv[:, cols], 0.0, ALU.mult, ALU.add
                                             ).then_inc(s.scanned, 1)
            for t in range(NT):
                cols = slice(t * TILE, (t + 1) * TILE)
                dve.wait_ge(s.scanned, t // 2 + 1)
                dve.wait_ge(s.gate_ready, t + 1)
                nc.vector.tensor_tensor(Uv[:, cols], Uv[:, cols], GT[:, cols], ALU.mult).then_inc(s.gated, 1)

    rms_norm(k, 1, Uv, Hb, w("norm2"))
    feed_forward(k, 0, 0, Hb, FCH, lambda lo, n: w("mg", lo, n), lambda c, n: w("mg_b", c, 1),
                 lambda lo, n: w("mf", lo, n), lambda c, n: w("mf_b", c, 1),
                 lambda c, n: w("mo", c * P, P), w("mo_b"), S, S)


def rows_pipeline(eng, step, tail, slots):
    first = 6
    last = first + (B - 1 - first) // slots * slots
    for i in range(first):
        step(i, i % slots)
    with eng.Fori(first // slots, last // slots) as turn:
        for n in range(slots):
            step(turn * slots + n, n)
    for i in range(last, B + tail):
        step(i, i % slots)


def done(i, lag):
    return min(max(i - lag + 1, 0), B) if isinstance(i, int) else i - lag + 1


def live(i, lag):
    return not isinstance(i, int) or 0 <= i - lag < B


def placed(j, e):
    return 64 * (j // 2) + 32 * e, j % 2


LA_PRODUCTS = {3: 0, 4: 1, 5: 2, 6: 3}
LA_VALUE_LAG, LA_RING = 1, 2
LA_SCALED_FIRST = 2
LA_MAX_AT = 6
POOL_SCALED = [(1, 0, 0), (1, 1, 1), (1, 2, 0), (1, 3, 1), (0, 0, 0), (0, 1, 1)]


def local_attention(k, layer, w, rope, X0, Yd):
    nc, s, ps = k.nc, k.s, k.ps
    row0 = layer * B
    W65 = D64 + 1
    NS = 3
    NPOOL = len(POOL_SCALED)
    with ExitStack() as ctx:
        sb = lambda n, shape, dt=F32: ctx.enter_context(nc.sbuf_tensor(f"la{layer}_{n}", shape, dt))
        hs = sb("hs", [P, NS, L])
        tab = sb("tab", [P, 2, 4, L])
        QK = sb("qk", [P, NS, 2, 4, L])
        V = sb("v", [P, NS, 2, H8, W65])
        sq = sb("sq", [P, 2, 2 * L])
        sqs = sb("sqs", [P, 2, L])
        vc = sb("vc", [P, 4, L])
        rn = sb("rn", [P, 4, L])
        y2 = sb("y2", [P, 4, L])
        ta = sb("ta", [P, 2, 2 * L])
        tb = sb("tb", [P, 2, 2 * L])
        tc = sb("tc", [P, 2, 2, 2, L])
        nm = sb("nm", [P, 2, H8])
        nb = sb("nb", [P, 2, H8], BF16)
        m2 = sb("m2", [P, 2, P])
        mT = sb("mt", [P, NS, L], BF16)
        pr = sb("pr", [P, LA_RING, 320])
        rec = sb("rec", [P, 2, 2])
        ot = sb("ot", [P, 2, 4, P])
        oT = sb("oT", [P, 4, L])
        block = ctx.enter_context(nc.Block())

        def scaled(n, g, j, e):
            part, chunk = placed(j, e)
            src = slice(32 * j, 32 * j + 32)
            to = QK[part:part + 32, n, g, :, :].rearrange("p (c a) t -> p c a t", a=2)[:, :, chunk, :]
            return to, rn[src, 2 * g:2 * g + 2, :], tc[src, g, :, e, :]

        @block.gpsimd
        def _(pool):
            nc.gpsimd.memset(V[:, :, :, :, D64:W65], 1.0).then_inc(s.la_init, 1)
            nc.gpsimd.memset(m2[:], 0.0).then_inc(s.la_init, 1)
            pool.wait_ge(s.la_init, 3 * layer + 2)
            nc.gpsimd.memset(hs[64:128, :, 0:1], 0.0).then_inc(s.la_init, 1)
            pool.wait_ge(s.la_init, 3 * layer + 3)

            def step(i, n):
                b = row0 + i
                for x in range(H8):
                    if live(i, 0) and x == 0:
                        at_least(pool, s.la_vprod, 2 * (b - NS + 1) if live(i, NS) else 0)
                        nc.gpsimd.tensor_copy(hs[0:64, n, :], X0[0:64, bass.ds(i * L, L)]).then_inc(s.la_shifted, 1)
                        pool.wait_ge(s.la_shifted, 2 * b + 1)
                        nc.gpsimd.tensor_copy(hs[64:128, n, 1:L], X0[64:128, bass.ds(i * L, L - 1)]
                                              ).then_inc(s.la_shifted, 1)
                        pool.wait_ge(s.la_shifted, 2 * b + 2)
                    if live(i, 0) and x in LA_PRODUCTS:
                        p = LA_PRODUCTS[x]
                        pool.wait_ge(s.la_squared, 4 * b + p + 1)
                        at_least(pool, s.la_norm, 4 * b + p - 1)
                        nc.gpsimd.tensor_tensor(sqs[:, p % 2, :], sq[:, p % 2, 0:L], sq[:, p % 2, L:2 * L], ALU.add
                                                ).then_inc(s.la_sqsum, 1)
                        pool.wait_ge(s.la_sqsum, 4 * b + p + 1)
                    if live(i, 1) and x in (2, 3):
                        if x == 2:
                            pool.wait_ge(s.la_exact, b)
                            pool.wait_ge(s.la_rotated, 4 * b)
                            if live(i, 1 + NS):
                                at_least(pool, s.la_keyed, H8 * (b - NS))
                        first = (x - 2) * (NPOOL // 2)
                        for m in range(first, first + NPOOL // 2):
                            to, norm, src = scaled((n - 1) % NS, *POOL_SCALED[m])
                            nc.gpsimd.tensor_tensor(to, norm, src, ALU.mult).then_inc(s.la_qkp, 1)
                            pool.wait_ge(s.la_qkp, NPOOL * (b - 1) + m + 1)
                    if live(i, 0) and x in LA_PRODUCTS:
                        p = LA_PRODUCTS[x]
                        pool.wait_ge(s.la_rot, 4 * b + p + 1)
                        if p == 0:
                            at_least(pool, s.la_qk, b)
                        nc.gpsimd.tensor_tensor(tc[:, p // 2, p % 2, :, :].rearrange("p e t -> p (e t)"), ta[:, p % 2, :],
                                                tb[:, p % 2, :], ALU.add).then_inc(s.la_rotated, 1)
            rows_pipeline(pool, step, 4, NS)

        @block.tensor
        def _(pe):
            pe.wait_ge(s.la_init, 3 * (layer + 1))

            def product(i, n, p):
                u = 4 * (row0 + i) + p
                if p == 0:
                    pe.wait_ge(s.la_shifted, 2 * (row0 + i + 1))
                at_least(pe, s.la_rot, u - 1)
                weights = w("wq" if p < 2 else "wk", p % 2 * 2 * P, 2 * P)
                for e in range(2):
                    m = nc.tensor.matmul(ps[:, p % 2, e * L:(e + 1) * L], weights[:, e * P:(e + 1) * P], hs[:, n, :],
                                         start=True, stop=True)
                m.then_inc(s.la_product, 1)

            def norms(i, p):
                if p == 0:
                    at_least(pe, s.la_clamped, row0 + i)
                    at_least(pe, s.la_vread, 2 * (row0 + done(i, 1)))
                pe.wait_ge(s.la_sqsum, 4 * (row0 + i) + p + 1)
                nc.tensor.matmul(ps[:, 2 + p // 2, p % 2 * L:(p % 2 + 1) * L], k.cf("block32"), sqs[:, p % 2, :],
                                 start=True, stop=True).then_inc(s.la_norm, 1)

            def head(n, h):
                part, chunk = placed(h % 4, 0)
                at = h // 4 * 2 + chunk
                return QK[part:part + 64, n, 0, at, :], QK[part:part + 64, n, 1, at, :]

            def maxima(i, n, h):
                u = H8 * (row0 + i) + h
                if h == 0:
                    pe.wait_ge(s.la_qk, row0 + i + 1)
                    pe.wait_ge(s.la_qkp, NPOOL * (row0 + i + 1))
                at_least(pe, s.la_max, u)
                q, kk = head(n, h)
                nc.tensor.matmul(ps[:, 4, 0:128], q[:, 0:128], kk[:, 0:128], start=True, stop=False)
                nc.tensor.matmul(ps[:, 4, 0:128], k.cb("ident"), k.cb("local_q0"), start=False, stop=True)
                nc.tensor.matmul(ps[:, 4, 128:320], q[:, 128:256], kk[:, 64:256], start=True, stop=False)
                nc.tensor.matmul(ps[:, 4, 128:320], k.cb("ident"), k.cb("local_q1"), start=False, stop=True
                                 ).then_inc(s.la_score, 1)

            def keyed(i, n, h):
                u = H8 * (row0 + i) + h
                if h == 0:
                    pe.wait_ge(s.la_mt, row0 + i + 1)
                at_least(pe, s.la_prob, u)
                q, kk = head(n, h)
                sel = k.cb("sel", h * P, P)
                nc.tensor.matmul(ps[:, 5, 0:192], kk[:, 0:128], q[:, 0:192], start=True, stop=False)
                nc.tensor.matmul(ps[:, 5, 0:192], k.cb("ident"), k.cb("local_k0"), start=False, stop=False)
                nc.tensor.matmul(ps[:, 5, 0:192], sel, mT[:, n, 0:192], start=False, stop=True)
                nc.tensor.matmul(ps[:, 5, 192:320], kk[:, 128:256], q[:, 128:256], start=True, stop=False)
                nc.tensor.matmul(ps[:, 5, 192:320], k.cb("ident"), k.cb("local_k0", 0, P), start=False, stop=False)
                nc.tensor.matmul(ps[:, 5, 192:320], sel, mT[:, n, 128:256], start=False, stop=True).then_inc(s.la_keyed, 1)

            def values(i, n, h):
                u = H8 * (row0 + i) + h
                pe.wait_ge(s.la_prob, u + 1)
                if h == 0:
                    pe.wait_ge(s.la_vread, 2 * (row0 + i + 1))
                if h % 2 == 0:
                    at_least(pe, s.la_divided, 4 * (row0 + i) + h // 2)
                o0, o1 = (h % 2) * W65, (2 + h % 2) * W65
                p = pr[:, h % LA_RING, :]
                nc.tensor.matmul(ps[:, 7, o0:o0 + W65], p[:, 0:128], V[:, n, 0, h, :], start=True, stop=True)
                nc.tensor.matmul(ps[:, 7, o1:o1 + W65], p[:, 192:320], V[:, n, 1, h, :], start=True, stop=True)
                nc.tensor.matmul(ps[0:64, 7, o1:o1 + W65], p[:, 128:192], V[:, n, 0, h, :], start=False, stop=True,
                                 skip_group_check=True).then_inc(s.la_attended, 1)

            def bank6_read(i):
                at_least(pe, s.la_mt, row0 + done(i - 1, 2))
                at_least(pe, s.la_stored, row0 + done(i - 1, 4))

            def project_values(i, n):
                pe.wait_ge(s.la_clamped, row0 + i)
                for q in range(2):
                    nc.tensor.matmul(ps[:, 2 + q, :], hs[:, n, q * P:(q + 1) * P], w("wv"), start=True, stop=True
                                     ).then_inc(s.la_vprod, 1)

            def turn(i, half):
                b = row0 + i - 4
                pe.wait_ge(s.la_divided, 4 * b + 2 * (half + 1))
                bank6_read(i)
                at_least(pe, s.la_turned, 2 * b + half)
                pe.nop(nofuse=True)
                for c in range(2):
                    for q in range(2):
                        at = c * L + q * P
                        m = nc.tensor.transpose(ps[:, 6, at:at + P], ot[:, q, 2 * half + c, :], k.cf("identf"))
                m.then_inc(s.la_turn, 1)

            def output(i):
                pe.wait_ge(s.la_turned, 2 * (row0 + i - 3))
                for c in range(4):
                    m = nc.tensor.matmul(ps[:, 6, 0:L], w("wo", c * P, P), oT[:, c, :], start=(c == 0), stop=(c == 3))
                m.then_inc(s.la_out, 1)

            def shifts(i):
                pe.wait_ge(s.la_m2, 3 * (row0 + i - 1))
                at_least(pe, s.la_stored, row0 + done(i, 4))
                pe.nop(nofuse=True)
                for q in range(2):
                    m = nc.tensor.transpose(ps[:, 6, q * P:(q + 1) * P], m2[:, q, :], k.cf("identf"))
                m.then_inc(s.la_shift, 1)

            def step(i, n):
                for x in range(H8):
                    if live(i, 0) and x in LA_PRODUCTS:
                        product(i, n, LA_PRODUCTS[x])
                    row = 1 if x >= LA_MAX_AT else 2
                    if live(i, row):
                        maxima(i - row, (n - row) % NS, (x - LA_MAX_AT) % H8)
                    if live(i, 4) and x == 2:
                        turn(i, 0)
                    if live(i, 3):
                        keyed(i - 3, n, x)
                    row = 3 if x >= LA_VALUE_LAG else 4
                    if live(i, row):
                        values(i - row, (n - row) % NS, (x - LA_VALUE_LAG) % H8)
                    if live(i, 1) and x == 0:
                        project_values(i, (n - 1) % NS)
                    if live(i, 4) and x == 3:
                        turn(i, 1)
                    if live(i, 4) and x == 4:
                        output(i)
                    if live(i, 2) and x == 6:
                        shifts(i)
                    if live(i, 0) and x - 1 in LA_PRODUCTS:
                        norms(i, LA_PRODUCTS[x - 1])
            rows_pipeline(pe, step, 4, NS)

        @block.scalar
        def _(act):
            act.wait_ge(s.la_init, 3 * (layer + 1))

            def step(i, n):
                b = row0 + i
                for x in range(H8):
                    if live(i, 0) and x in LA_PRODUCTS:
                        p = LA_PRODUCTS[x]
                        act.wait_ge(s.la_product, 4 * b + p + 1)
                        at_least(act, s.la_sqsum, 4 * b + p - 1)
                        nc.scalar.activation(sq[:, p % 2, :], ps[:, p % 2, :], ACT.Square).then_inc(s.la_squared, 1)
                    if live(i, 3):
                        u = H8 * (b - 3) + x
                        act.wait_ge(s.la_keyed, u + 1)
                        at_least(act, s.la_attended, u - LA_RING + 1)
                        nc.scalar.activation(pr[:, x % LA_RING, :], ps[:, 5, 0:320], ACT.Exp, scale=8.0
                                             ).then_inc(s.la_prob, 1)
                    if live(i, 2) and x == 6:
                        act.wait_ge(s.la_shift, b - 1)
                        if live(i, 2 + NS):
                            at_least(act, s.la_keyed, H8 * (b - 1 - NS))
                        nc.scalar.copy(mT[:, (n - 2) % NS, :], ps[:, 6, 0:L]).then_inc(s.la_mt, 1)
                    if live(i, 1) and x == 0:
                        act.wait_ge(s.la_clamped, b)
                        at_least(act, s.la_qk, b - 1)
                        at_least(act, s.la_qkp, NPOOL * (b - 1))
                        nc.scalar.activation(rn[:], vc[:], ACT.Abs_reciprocal_sqrt).then_inc(s.la_rnorm, 1)
                        act.wait_ge(s.la_rnorm, b)
                        nc.scalar.activation(y2[:], rn[:], ACT.Square).then_inc(s.la_rnorm2, 1)
                    if live(i, 1) and x in (1, 2):
                        act.wait_ge(s.la_vprod, 2 * (b - 1) + x)
                        if live(i, 1 + NS):
                            at_least(act, s.la_attended, H8 * (b - NS))
                        nc.scalar.copy(V[:, (n - 1) % NS, x - 1, :, 0:D64], ps[:, 1 + x, :].rearrange("p (h d) -> p h d", d=D64)
                                       ).then_inc(s.la_vread, 1)
                    if live(i, 4) and x in (2, 3):
                        c = 2 * (x - 2)
                        act.wait_ge(s.la_turn, 2 * (b - 4) + x - 1)
                        at_least(act, s.la_out, b - 4)
                        nc.scalar.copy(oT[:, c:c + 2, :].rearrange("p c t -> p (c t)"), ps[:, 6, :]
                                       ).then_inc(s.la_turned, 1)
            rows_pipeline(act, step, 4, NS)

        @block.vector
        def _(dve):
            for g, (c, si, one, two) in enumerate((("qc", "qs", "q1", "q2"), ("kc", "ks", "k1", "k2"))):
                nc.vector.tensor_scalar(tab[:, g, 0, :], rope(c), w(one), None, ALU.mult)
                nc.vector.tensor_scalar(tab[:, g, 1, :], rope(c), w(two), None, ALU.mult)
                nc.vector.tensor_scalar(tab[:, g, 2, :], rope(si), w(two), -1.0, ALU.mult, ALU.mult)
                nc.vector.tensor_scalar(tab[:, g, 3, :], rope(si), w(one), None, ALU.mult).then_inc(s.la_table, 1)
            dve.wait_ge(s.la_table, 2 * (layer + 1))
            dve.wait_ge(s.la_init, 3 * (layer + 1))

            flat = lambda v: v.rearrange("p c t -> p (c t)")

            def rotate(i, p):
                u = 4 * (row0 + i) + p
                g = p // 2
                dve.wait_ge(s.la_squared, u + 1)
                at_least(dve, s.la_rotated, u - 1)
                nc.vector.tensor_tensor(ta[:, p % 2, :], ps[:, p % 2, :], flat(tab[:, g, 0:2, :]), ALU.mult)
                nc.vector.tensor_tensor(tb[:, p % 2, 0:L], ps[:, p % 2, L:2 * L], tab[:, g, 2, :], ALU.mult)
                nc.vector.tensor_tensor(tb[:, p % 2, L:2 * L], ps[:, p % 2, 0:L], tab[:, g, 3, :], ALU.mult
                                        ).then_inc(s.la_rot, 1)

            def divide(i, g):
                b = row0 + i
                dve.wait_ge(s.la_attended, H8 * b + 2 * (g + 1))
                out = ps[:, 7, 0:4 * W65].rearrange("p (q h c) -> p q h c", q=2, c=W65)
                nc.vector.reciprocal(rec[:], out[:, :, :, D64]).then_inc(s.la_rec, 1)
                at_least(dve, s.la_turn, 2 * b - 1 + g // 2)
                dve.wait_ge(s.la_rec, 4 * b + g + 1)
                nc.vector.tensor_tensor(ot[:, :, g, :].rearrange("p q (h d) -> p q h d", d=D64), out[:, :, :, 0:D64],
                                        rec[:].unsqueeze(3).to_broadcast([P, 2, 2, D64]), ALU.mult
                                        ).then_inc(s.la_divided, 1)

            own = [(g, j, e) for g in range(2) for j in range(4) for e in range(2) if (g, j, e) not in POOL_SCALED]

            def step(i, n):
                b = row0 + i
                for x in range(H8):
                    if live(i, 1) and x == 0:
                        dve.wait_ge(s.la_norm, 4 * b)
                        at_least(dve, s.la_vy2, b - 1)
                        nc.vector.tensor_scalar(flat(vc[:]), ps[:, 2:4, :].rearrange("p a t -> p (a t)"), 1e-24, None,
                                                ALU.max).then_inc(s.la_clamped, 1)
                    if live(i, 3) and x in (3, 5, 7):
                        divide(i - 3, (x - 3) // 2)
                    if live(i, 4) and x == 1:
                        divide(i - 4, 3)
                    if live(i, 4) and x == 5:
                        dve.wait_ge(s.la_out, b - 3)
                        nc.vector.tensor_tensor(Yd[:, bass.ds((i - 4) * L, L)], ps[:, 6, 0:L], X0[:, bass.ds((i - 4) * L, L)],
                                                ALU.add).then_inc(s.la_stored, 1)
                    row = 1 if x >= LA_MAX_AT else 2
                    h = (x - LA_MAX_AT) % H8
                    if live(i, row):
                        r = b - row
                        dve.wait_ge(s.la_score, H8 * r + h + 1)
                        if h == 0:
                            at_least(dve, s.la_m2, 3 * r)
                        nc.vector.tensor_reduce(nm[:, 0, h:h + 1], ps[:, 4, 0:128], AX.X, ALU.max, negate=True)
                        nc.vector.tensor_reduce(nm[:, 1, h:h + 1], ps[:, 4, 128:320], AX.X, ALU.max, negate=True
                                                ).then_inc(s.la_max, 1)
                        if h == H8 - 1:
                            dve.wait_ge(s.la_max, H8 * (r + 1))
                            nc.vector.tensor_copy(nb[:], nm[:]).then_inc(s.la_m2, 1)
                            dve.wait_ge(s.la_m2, 3 * r + 1)
                            at_least(dve, s.la_shift, r)
                            nc.vector.tensor_copy(m2[:, :, 0:H8], nb[:]).then_inc(s.la_m2, 1)
                            nc.vector.tensor_tensor(m2[:, :, 32:32 + H8], nm[:], nb[:], ALU.subtract).then_inc(s.la_m2, 1)
                    if live(i, 0) and x in LA_PRODUCTS:
                        rotate(i, LA_PRODUCTS[x])
                    if live(i, 1) and x == 1:
                        dve.wait_ge(s.la_rnorm2, b)
                        nc.vector.tensor_tensor(flat(y2[:]), flat(vc[:]), flat(y2[:]), ALU.mult).then_inc(s.la_vy2, 1)
                        dve.wait_ge(s.la_vy2, b)
                        nc.vector.scalar_tensor_tensor(out=flat(rn[:]), in0=flat(y2[:]), scalar=-3.0, in1=flat(rn[:]),
                                                       op0=ALU.add, op1=ALU.mult).then_inc(s.la_exact, 1)
                    if live(i, 1) and x in (2, 3):
                        half = own[:LA_SCALED_FIRST] if x == 2 else own[LA_SCALED_FIRST:]
                        if x == 2:
                            dve.wait_ge(s.la_exact, b)
                            dve.wait_ge(s.la_rotated, 4 * b)
                            if live(i, 1 + NS):
                                at_least(dve, s.la_keyed, H8 * (b - NS))
                        for g, j, e in half:
                            to, norm, src = scaled((n - 1) % NS, g, j, e)
                            m = nc.vector.tensor_tensor(to, norm, src, ALU.mult)
                        if x == 3:
                            m.then_inc(s.la_qk, 1)
            rows_pipeline(dve, step, 4, NS)


def attention(k, call, slots, stack_dt, scale, rounds, value_from, value_w, out_w, out_b, make):
    nc, s, ps = k.nc, k.s, k.ps
    row0 = call * B
    rd0 = k.rounds
    sd0 = k.stack_dmas
    with ExitStack() as ctx:
        sb = lambda n, shape, dt=F32: ctx.enter_context(nc.sbuf_tensor(f"at{call}_{n}", shape, dt))
        a = Core()
        a.value_from = value_from
        a.row0, a.rd0, a.slots = row0, rd0, slots
        a.value_row = 1 if slots > 2 else 2
        xv = sb("xv", [a.value_from[0], slots, L])
        a.Qs = sb("qs", [P, slots, H16 * L], stack_dt)
        a.Ks = sb("ks", [P, slots, H16 * L], stack_dt)
        V = sb("v", [P, slots, 2, 2, 8 * GW + GW])
        nm = sb("nm", [P, 2, H16])
        nb = sb("nb", [P, 2, H16], BF16)
        m2 = sb("m2", [P, 2, P])
        mT = sb("mt", [P, slots, L], BF16)
        pr = sb("pr", [P, RING, 384])
        raw = sb("raw", [P, 2 * L])
        sums = sb("sums", [P, L])
        oT = sb("oT", [P, L])

        def heads(n, q, parity, half):
            lo = 4 * GW * parity + GW // 2 * half
            return V[:, n, q, :, lo:lo + 4 * (GW + D8)].rearrange("p g (j c) -> p g j c", c=GW + D8)[:, :, :, 0:D8]
        make(a, sb)
        quarters = a.load_groups
        hq = H16 // quarters
        nst = len(a.stack_loads(0, 0)) * quarters
        k.rounds += rounds * B
        k.stack_dmas += nst * B
        block = ctx.enter_context(nc.Block())

        @block.sync
        def _(sp):
            sp.wait_ge(s.at_zeroed, 2 * (call + 1))
            a.fill_constant_rows(sp)

            def step(i, n):
                def load(g):
                    r, nr = i - a.load_row, (n - a.load_row) % slots
                    b = row0 + r
                    if not live(i, a.load_row):
                        return
                    if g == 0:
                        sp.wait_ge(s.at_scratch, 32 * (b + 1))
                        sp.nop(nofuse=True)
                    at_least(sp, s.at_stacked, 16 * (sd0 + nst * r + nst // quarters * g))
                    sp.nop(nofuse=True)
                    if live(i, a.load_row + slots):
                        at_least(sp, s.at_keyed, H16 * (b - slots) + hq * (g + 1))
                        sp.nop(nofuse=True)
                    for dst, src in a.stack_loads(nr, g):
                        sp.dma_start(dst, src).then_inc(s.at_stacked, 16)

                for g in range(quarters // 2):
                    load(g)
                if live(i, 0):
                    a.wait_parts(sp, i)
                    sp.nop(nofuse=True)
                    if live(i, slots):
                        at_least(sp, s.at_stacked, 16 * (sd0 + nst * (i - slots + 1)))
                        sp.nop(nofuse=True)
                    for dst, src in a.scratch_stores(n):
                        sp.dma_start(dst, src).then_inc(s.at_scratch, 16)
                for g in range(quarters // 2, quarters):
                    load(g)
            rows_pipeline(sp, step, 4, slots)

        @block.gpsimd
        def _(pool):
            nc.gpsimd.memset(V[:], 0.0).then_inc(s.at_init, 1)
            nc.gpsimd.memset(m2[:], 0.0).then_inc(s.at_init, 1)
            pool.wait_ge(s.at_init, 3 * call + 2)
            for n in range(slots):
                for q in range(2):
                    for parity in range(2):
                        m = nc.gpsimd.memset(heads(n, q, parity, 1 - parity), 1.0)
            m.then_inc(s.at_init, 1)

            def step(i, n):
                b = row0 + i
                for x in range(H16):
                    if live(i, 0):
                        a.pool_round(pool, i, n, x)
                    if live(i, 4) and x == VALUE_LAG + 4:
                        pool.wait_ge(s.at_rec, b - 3)
                        at_least(pool, s.at_out, b - 4)
                        for g in range(4):
                            r = slice(32 * g, 32 * g + 32)
                            nc.gpsimd.tensor_tensor(oT[r, :], raw[r, g % 2 * L:(g % 2 + 1) * L], sums[r, :], ALU.mult
                                                    ).then_inc(s.at_divided, 1)
                            pool.wait_ge(s.at_divided, 4 * (b - 4) + g + 1)
                r = i + 1 - a.value_row
                if live(i, a.value_row - 1):
                    if live(i, a.value_row - 1 + slots):
                        at_least(pool, s.at_vprod, row0 + r - slots + 1)
                    nc.gpsimd.tensor_copy(xv[:, (n + 1 - a.value_row) % slots, :],
                                          value_from[1][0:value_from[0], bass.ds(r * L, L)]).then_inc(s.at_fetched, 1)
            rows_pipeline(pool, step, 4, slots)

        @block.tensor
        def _(pe):
            pe.wait_ge(s.at_init, 3 * (call + 1))

            def product(i, n, r):
                at_least(pe, s.at_used, rd0 + rounds * i + r)
                a.product(i, n, r).then_inc(s.at_product, 1)

            def shifts(i):
                pe.wait_ge(s.at_m2, 3 * (row0 + i - 2))
                at_least(pe, s.at_vread, row0 + done(i - 1, a.value_row))
                at_least(pe, s.at_stored, row0 + done(i - 1, 4))
                pe.nop(nofuse=True)
                for q in range(2):
                    m = nc.tensor.transpose(ps[:, 1, q * P:(q + 1) * P], m2[:, q, :], k.cf("identf"))
                m.then_inc(s.at_shift, 1)

            def value_rows(i, n):
                pe.wait_ge(s.at_fetched, row0 + done(i, a.value_row))
                at_least(pe, s.at_mt, row0 + done(i, 3))
                pe.nop(nofuse=True)
                for q in range(2):
                    m = nc.tensor.matmul(ps[:, 1, q * P:(q + 1) * P], xv[:, n, q * P:(q + 1) * P], value_w,
                                         start=True, stop=True)
                m.then_inc(s.at_vprod, 1)

            def output(i):
                pe.wait_ge(s.at_divided, 4 * (row0 + i - 3))
                at_least(pe, s.at_vread, row0 + done(i, a.value_row))
                at_least(pe, s.at_mt, row0 + done(i, 3))
                at_least(pe, s.at_stored, row0 + done(i - 1, 4))
                nc.tensor.matmul(ps[:, 1, 0:L], out_w, oT[:], start=True, stop=True).then_inc(s.at_out, 1)

            def maxima(i, n, h):
                u = H16 * (row0 + i) + h
                if h % hq == 0:
                    pe.wait_ge(s.at_stacked, 16 * (sd0 + nst * i + nst // quarters * (h // hq + 1)))
                at_least(pe, s.at_max, u - 1)
                q, kk = a.Qs[:, n, h * L:(h + 1) * L], a.Ks[:, n, h * L:(h + 1) * L]
                o = ps[:, 2 + h % 2, :]
                nc.tensor.matmul(o[:, 0:128], q[:, 0:128], kk[:, 0:128], start=True, stop=False)
                nc.tensor.matmul(o[:, 0:128], k.cb("ident"), k.cb("causal_q"), start=False, stop=True)
                nc.tensor.matmul(o[:, 128:384], q[:, 128:256], kk[:, 0:256], start=True, stop=False)
                nc.tensor.matmul(o[:, 256:384], k.cb("ident"), k.cb("causal_q"), start=False, stop=True
                                 ).then_inc(s.at_score, 1)

            def keyed(i, n, h):
                u = H16 * (row0 + i) + h
                if h == 0:
                    pe.wait_ge(s.at_mt, row0 + i + 1)
                at_least(pe, s.at_prob, u - 1)
                q, kk = a.Qs[:, n, h * L:(h + 1) * L], a.Ks[:, n, h * L:(h + 1) * L]
                o = ps[:, 4 + h % 2, :]
                sel = k.cb("sel", h * P, P)
                nc.tensor.matmul(o[:, 0:256], kk[:, 0:128], q[:, 0:256], start=True, stop=False)
                nc.tensor.matmul(o[:, 0:128], k.cb("ident"), k.cb("causal_k"), start=False, stop=False)
                nc.tensor.matmul(o[:, 0:256], sel, mT[:, n, 0:256], start=False, stop=True)
                nc.tensor.matmul(o[:, 256:384], kk[:, 128:256], q[:, 128:256], start=True, stop=False)
                nc.tensor.matmul(o[:, 256:384], k.cb("ident"), k.cb("causal_k"), start=False, stop=False)
                nc.tensor.matmul(o[:, 256:384], sel, mT[:, n, 128:256], start=False, stop=True).then_inc(s.at_keyed, 1)

            def values(i, n, h):
                pe.wait_ge(s.at_prob, H16 * (row0 + i) + h + 1)
                if h == 0:
                    at_least(pe, s.at_raw, row0 + i)
                    pe.wait_ge(s.at_vread, row0 + i + 1)
                g, j = h // 4, h % 4
                lo, row = 4 * GW * (g % 2) + GW * j, GW * (g // 2)
                o = ps[row:row + GW, 7, g % 2 * L:(g % 2 + 1) * L]
                w = pr[:, h % RING, :]
                nc.tensor.matmul(o, V[:, n, 0, g // 2, lo:lo + GW], w[:, 0:L], start=(j == 0), stop=False)
                nc.tensor.matmul(o[:, P:L], V[:, n, 1, g // 2, lo:lo + GW], w[:, L:L + P], start=False, stop=(j == 3)
                                 ).then_inc(s.at_attended, 1)

            def step(i, n):
                for x in range(H16):
                    if live(i, 0) and x % ROUND == 0 and x // ROUND < rounds:
                        product(i, n, x // ROUND)
                    if live(i, 3) and x == 1:
                        shifts(i)
                    if live(i, 2):
                        maxima(i - 2, (n - 2) % slots, x)
                    for stage, lag in ((keyed, KEY_LAG), (values, VALUE_LAG)):
                        row = 3 + (x < lag)
                        if live(i, row):
                            stage(i - row, (n - row) % slots, (x - lag) % H16)
                    if live(i, a.value_row) and x == 7:
                        value_rows(i, (n - a.value_row) % slots)
                    if live(i, 4) and x == 14:
                        output(i)
            rows_pipeline(pe, step, 4, slots)

        @block.scalar
        def _(act):
            act.wait_ge(s.at_init, 3 * (call + 1))

            def step(i, n):
                b = row0 + i
                for x in range(H16):
                    if live(i, 4) and x == VALUE_LAG:
                        act.wait_ge(s.at_attended, H16 * (b - 3))
                        at_least(act, s.at_divided, 4 * (b - 4))
                        nc.scalar.copy(raw[:], ps[:, 7, :]).then_inc(s.at_raw, 1)
                    row = 3 + (x < KEY_LAG)
                    if live(i, row):
                        h = (x - KEY_LAG) % H16
                        u = H16 * (b - row) + h
                        act.wait_ge(s.at_keyed, u + 1)
                        at_least(act, s.at_attended, u - RING + 1)
                        nc.scalar.activation(pr[:, h % RING, :], ps[:, 4 + h % 2, 0:384], ACT.Exp, scale=scale
                                             ).then_inc(s.at_prob, 1)
                    if live(i, 0):
                        a.act_round(act, i, n, x)
                    if live(i, 3) and x == 1:
                        act.wait_ge(s.at_shift, b - 2)
                        if live(i, 3 + slots):
                            at_least(act, s.at_keyed, H16 * (b - 2 - slots))
                        nc.scalar.copy(mT[:, (n - 3) % slots, :], ps[:, 1, 0:L]).then_inc(s.at_mt, 1)
                    if live(i, 4) and x == VALUE_LAG + 1:
                        act.wait_ge(s.at_raw, b - 3)
                        for g in range(4):
                            r = g // 2 * GW + GW // 2 * (1 - g % 2)
                            m = nc.scalar.copy(sums[32 * g:32 * g + 32, :], raw[r:r + 32, g % 2 * L:(g % 2 + 1) * L])
                        m.then_inc(s.at_sums, 1)
                    if live(i, a.value_row) and x == 9:
                        act.wait_ge(s.at_vprod, b + 1 - a.value_row)
                        if live(i, a.value_row + slots):
                            at_least(act, s.at_attended, H16 * (b + 1 - a.value_row - slots))
                        for q in range(2):
                            made = ps[:, 1, q * P:(q + 1) * P].rearrange("p (g r j d) -> p g r j d", r=2, j=4, d=D8)
                            for parity in range(2):
                                m = nc.scalar.copy(heads((n - a.value_row) % slots, q, parity, parity), made[:, :, parity])
                        m.then_inc(s.at_vread, 1)
            rows_pipeline(act, step, 4, slots)

        @block.vector
        def _(dve):
            for st in (a.Qs, a.Ks):
                nc.vector.memset(st[:], 0.0).then_inc(s.at_zeroed, 1)
            a.vector_init(dve)
            dve.wait_ge(s.at_init, 3 * (call + 1))

            def step(i, n):
                b = row0 + i
                for x in range(H16):
                    if live(i, 2):
                        dve.wait_ge(s.at_score, H16 * (b - 2) + x + 1)
                        if x == 0:
                            at_least(dve, s.at_m2, 3 * (b - 2))
                        nc.vector.tensor_reduce(nm[:, 0, x:x + 1], ps[:, 2 + x % 2, 0:128], AX.X, ALU.max, negate=True)
                        nc.vector.tensor_reduce(nm[:, 1, x:x + 1], ps[:, 2 + x % 2, 128:384], AX.X, ALU.max,
                                                negate=True).then_inc(s.at_max, 1)
                    if live(i, 0):
                        a.vector_round(dve, i, n, x)
                    if live(i, 4) and x == VALUE_LAG + 3:
                        dve.wait_ge(s.at_sums, b - 3)
                        nc.vector.reciprocal(sums[:], sums[:]).then_inc(s.at_rec, 1)
                    if live(i, 4) and x == 15:
                        dve.wait_ge(s.at_out, b - 3)
                        to = k.S[:, bass.ds((i - 4) * L, L)]
                        if out_b is None:
                            m = nc.vector.tensor_copy(to, ps[:, 1, 0:L])
                        else:
                            m = nc.vector.tensor_scalar(to, ps[:, 1, 0:L], out_b, None, ALU.add)
                        m.then_inc(s.at_stored, 1)
                if live(i, 2):
                    c = 3 * (b - 2)
                    dve.wait_ge(s.at_max, H16 * (b - 1))
                    nc.vector.tensor_copy(nb[:], nm[:]).then_inc(s.at_m2, 1)
                    dve.wait_ge(s.at_m2, c + 1)
                    at_least(dve, s.at_shift, b - 2)
                    nc.vector.tensor_copy(m2[:, :, 0:H16], nb[:]).then_inc(s.at_m2, 1)
                    nc.vector.tensor_tensor(m2[:, :, 32:48], nm[:], nb[:], ALU.subtract).then_inc(s.at_m2, 1)
            rows_pipeline(dve, step, 4, slots)


def nothing(*_):
    pass


def split_stacks(k, a, sb, name):
    nc, s = k.nc, k.s
    a.parts = sb("parts", [P, 3, 2 * L], BF16)
    a.res = sb("res", [P, 2 * L])
    scr = nc.dram_tensor(f"scratch_{name}", (a.slots, 2, 3, P, L), BF16)
    a.load_groups, a.load_row = 1, 0

    def scratch_stores(n):
        return [(scr[n, j].rearrange("s p t -> p s t"), a.parts[:, :, j * L:(j + 1) * L]) for j in range(2)]

    def stack_loads(n, g):
        q, kk = (scr[n, j].rearrange("s (d h) t -> (s d) (h t)", h=H16) for j in range(2))
        return ([(a.Qs[0:24, n, :], q[0:24]), (a.Qs[24:40, n, :], q[0:16]), (a.Qs[40:48, n, :], q[0:8])]
                + [(a.Ks[8 * j:8 * j + 8, n, :], kk[0:8]) for j in range(3)]
                + [(a.Ks[24 + 8 * j:32 + 8 * j, n, :], kk[8:16]) for j in range(2)]
                + [(a.Ks[40:48, n, :], kk[16:24])])
    a.scratch_stores, a.stack_loads = scratch_stores, stack_loads
    a.wait_parts = lambda sp, i: sp.wait_ge(s.at_parts, a.row0 + i + 1)

    def leading(act, i, src):
        at_least(act, s.at_scratch, 32 * (a.row0 + i))
        nc.scalar.copy(a.parts[:, 0, :], src).then_inc(s.at_hi, 1)

    def rest(dve, i, src):
        dve.wait_ge(s.at_hi, a.row0 + i + 1)
        at_least(dve, s.at_parts, a.row0 + i)
        return nc.vector.tensor_tensor(a.res[:], src, a.parts[:, 0, :], ALU.subtract)

    def middle(act, i):
        act.wait_ge(s.at_res, a.row0 + i + 1)
        nc.scalar.copy(a.parts[:, 1, :], a.res[:]).then_inc(s.at_mid, 1)

    def last(pool, i):
        pool.wait_ge(s.at_mid, a.row0 + i + 1)
        nc.gpsimd.tensor_tensor(a.parts[:, 2, :], a.res[:], a.parts[:, 1, :], ALU.subtract).then_inc(s.at_parts, 1)
    a.leading, a.rest, a.middle, a.last = leading, rest, middle, last


def alibi_attention(k, w, alibi):
    nc, s, ps = k.nc, k.s, k.ps

    def make(a, sb):
        split_stacks(k, a, sb, "alibi")
        half = H16 * L // 2
        rows16 = sb("alibi", [64, half], BF16)
        a.pool_round = lambda pool, i, n, x: a.last(pool, i) if x == 6 else None

        def fill(sp):
            for j in range(2):
                sp.dma_start(k.Y[32 * j:32 * j + 6, :], alibi[j]).then_inc(s.alibi_loaded, 16)
            for c in range(2):
                sp.wait_ge(s.alibi_cast, 2 * (c + 1))
                for n in range(a.slots):
                    for st, r in ((a.Qs, 0), (a.Ks, 32)):
                        sp.dma_start(st[48:54, n, c * half:(c + 1) * half], rows16[r:r + 6, :]).then_inc(s.alibi_rows, 16)
                sp.wait_ge(s.alibi_rows, 32 * a.slots * (c + 1))
        a.fill_constant_rows = fill

        def init(dve):
            dve.wait_ge(s.alibi_loaded, 32)
            for c in range(2):
                at_least(dve, s.alibi_rows, 32 * a.slots * c)
                for j in range(2):
                    r = slice(32 * j, 32 * j + 6)
                    nc.vector.tensor_copy(rows16[r, :], k.Y[r, c * half:(c + 1) * half]).then_inc(s.alibi_cast, 1)
        a.vector_init = init

        def product(i, n, r):
            nc.tensor.matmul(ps[:, 0, 0:L], w("wq"), k.XN[:, bass.ds(i * L, L)], start=True, stop=True)
            return nc.tensor.matmul(ps[:, 0, L:2 * L], w("wk"), k.XN[:, bass.ds(i * L, L)], start=True, stop=True)
        a.product = product

        def act_round(act, i, n, x):
            if x == 2:
                act.wait_ge(s.at_product, a.rd0 + i + 1)
                a.leading(act, i, ps[:, 0, :])
            if x == 5:
                a.middle(act, i)
        a.act_round = act_round

        def vector_round(dve, i, n, x):
            if x == 3:
                a.rest(dve, i, ps[:, 0, :]).then_inc(s.at_res, 1)
                dve.wait_ge(s.at_res, a.row0 + i + 1)
                nc.vector.sem_inc(s.at_used, 1)
        a.vector_round = vector_round

    attention(k, 0, 3, BF16, float(1 / np.sqrt(8.0)), 1, (P, k.XN), w("wv"), w("wo"), None, make)


def rope8_attention(k, w, fold):
    nc, s, ps = k.nc, k.s, k.ps

    def make(a, sb):
        split_stacks(k, a, sb, "rope8")
        ta, tb, tq = sb("ta", [P, 2, L]), sb("tb", [P, 2, L]), sb("tq", [P, 2, L])
        a.fill_constant_rows = a.vector_init = nothing

        def product(i, n, r):
            nc.tensor.matmul(ps[:, 0, 0:L], fold[:, 2 * r, :], k.XN[:, bass.ds(i * L, L)], start=True, stop=True)
            return nc.tensor.matmul(ps[:, 0, L:2 * L], fold[:, 2 * r + 1, :], k.XN[:, bass.ds(i * L, L)], start=True, stop=True)
        a.product = product

        def vector_round(dve, i, n, x):
            if x in (1, ROUND + 1):
                r = x // ROUND
                dve.wait_ge(s.at_product, a.rd0 + 2 * i + r + 1)
                at_least(dve, s.at_sum, 2 * i + r - 1)
                nc.vector.tensor_tensor(ta[:, r, :], ps[:, 0, 0:L], w("cos"), ALU.mult)
                nc.vector.tensor_tensor(tb[:, r, :], ps[:, 0, L:2 * L], w("sin"), ALU.mult).then_inc(s.at_used, 1)
            if x == 9:
                a.rest(dve, i, tq[:].rearrange("p a t -> p (a t)")).then_inc(s.at_res, 1)
        a.vector_round = vector_round

        def pool_round(pool, i, n, x):
            if x in (2, ROUND + 2):
                r = x // ROUND
                pool.wait_ge(s.at_used, a.rd0 + 2 * i + r + 1)
                at_least(pool, s.at_res, a.row0 + i)
                nc.gpsimd.tensor_tensor(tq[:, r, :], ta[:, r, :], tb[:, r, :], ALU.add).then_inc(s.at_sum, 1)
            if x == 11:
                a.last(pool, i)
        a.pool_round = pool_round

        def act_round(act, i, n, x):
            if x == 8:
                act.wait_ge(s.at_sum, 2 * i + 2)
                a.leading(act, i, tq[:].rearrange("p a t -> p (a t)"))
            if x == 11:
                a.middle(act, i)
        a.act_round = act_round

    attention(k, 1, 3, BF16, float(D8 ** -0.5), 2, (P, k.XN), fold[:, 4, :], w("wo"), w("bo"), make)


def latent_attention(k, w, fold, kvn):
    nc, s, ps = k.nc, k.s, k.ps

    def make(a, sb):
        ta, tb = sb("ta", [P, 2, 2 * L]), sb("tb", [P, 2, 2 * L])
        qk = sb("parts", [P, 2, 5, L])
        scr = nc.dram_tensor("scratch_latent", (a.slots, 2, 5 * P, L), F32)
        a.load_groups, a.load_row = 4, 1

        def scratch_stores(n):
            return [(scr[n, j].rearrange("(c p) t -> p c t", p=P), qk[:, j, :, :]) for j in range(2)]

        def stack_loads(n, g):
            cols = slice(g * H16 // a.load_groups * L, (g + 1) * H16 // a.load_groups * L)
            return [(st[0:5 * P // H16, n, cols], scr[n, j].rearrange("(d h) t -> d (h t)", h=H16)[:, cols])
                    for j, st in enumerate((a.Qs, a.Ks))]
        a.scratch_stores, a.stack_loads = scratch_stores, stack_loads
        a.fill_constant_rows = a.vector_init = nothing

        def wait_parts(sp, i):
            sp.wait_ge(s.at_content, i + 1)
            sp.nop(nofuse=True)
            sp.wait_ge(s.at_sum, 2 * B + 4 * (i + 1))
        a.wait_parts = wait_parts

        def product(i, n, r):
            x = k.XN[:, bass.ds(i * L, L)]
            if r == 0:
                nc.tensor.matmul(ps[:, 0, 0:L], fold[:, 0:P], x, start=True, stop=True)
                return nc.tensor.matmul(ps[:, 0, L:2 * L], w("kd", rows=32), kvn[0:32, bass.ds(i * L, L)], start=True, stop=True)
            c = (r - 1) % 2
            src = fold[:, P:5 * P] if r < 3 else w("kr")
            nc.tensor.matmul(ps[:, 0, 0:L], src[:, c * P:(c + 1) * P], x, start=True, stop=True)
            return nc.tensor.matmul(ps[:, 0, L:2 * L], src[:, (c + 2) * P:(c + 3) * P], x, start=True, stop=True)
        a.product = product

        def act_round(act, i, n, x):
            if x == 1:
                act.wait_ge(s.at_product, a.rd0 + 5 * i + 1)
                at_least(act, s.at_scratch, 32 * (a.row0 + i))
                nc.scalar.copy(qk[:, :, 0, :], ps[:, 0, :].rearrange("p (a t) -> p a t", a=2)).then_inc(s.at_content, 1)
                act.wait_ge(s.at_content, i + 1)
                nc.scalar.sem_inc(s.at_used, 1)
        a.act_round = act_round

        def vector_round(dve, i, n, x):
            p = x // ROUND
            if x % ROUND == 1 and 1 <= p < 5:
                c, e = (p - 1) % 2, p % 2
                dve.wait_ge(s.at_product, a.rd0 + 5 * i + p + 1)
                at_least(dve, s.at_sum, 2 * B + 4 * i + p - 2)
                two = ps[:, 0, :].rearrange("p (a t) -> p a t", a=2)
                sin = w("sin", c * 2 * L, 2 * L)
                nc.vector.tensor_tensor(ta[:, e, :], ps[:, 0, :], w("cos", c * 2 * L, 2 * L), ALU.mult)
                nc.vector.tensor_tensor(tb[:, e, 0:L], two[:, 1, :], sin[:, 0:L], ALU.mult)
                nc.vector.tensor_tensor(tb[:, e, L:2 * L], two[:, 0, :], sin[:, L:2 * L], ALU.mult).then_inc(s.at_used, 1)
        a.vector_round = vector_round

        def pool_round(pool, i, n, x):
            p = x // ROUND
            if x % ROUND == 2 and 1 <= p < 5:
                c, e = (p - 1) % 2, p % 2
                pool.wait_ge(s.at_used, a.rd0 + 5 * i + p + 1)
                if p == 1:
                    at_least(pool, s.at_scratch, 32 * (a.row0 + i))
                nc.gpsimd.tensor_tensor(qk[:, (p - 1) // 2, 1 + c:4 + c:2, :], ta[:, e, :].rearrange("p (a t) -> p a t", a=2),
                                        tb[:, e, :].rearrange("p (a t) -> p a t", a=2), ALU.add).then_inc(s.at_sum, 1)
        a.pool_round = pool_round

    attention(k, 2, 2, F32, float(40.0 ** -0.5), 5, (32, kvn), w("vd", rows=32), w("wo"), None, make)


def experts(k, w):
    nc, s, ps = k.nc, k.s, k.ps
    with ExitStack() as ctx:
        sb = lambda n, shape, dt=F32: ctx.enter_context(nc.sbuf_tensor(f"moe_{n}", shape, dt))
        gs = sb("gs", [P, N // P, NEXP])
        best = sb("best", [P, N // P])
        pick = sb("pick", [P, N // P])
        at = sb("at", [P, N // P, NEXP])
        hot = sb("hot", [P, N // P, NEXP])
        io = sb("io", [P, NEXP])
        hotT = sb("hott", [NEXP, N])
        hotb = sb("hotb", [NEXP, N], BF16)
        hr = sb("hr", [P, 3, TILE])
        hm = sb("hm", [P, 3, TILE])

        with nc.Block() as block:
            @block.gpsimd
            def _(pool):
                for e in range(NEXP):
                    m = nc.gpsimd.memset(io[:, e:e + 1], float(e))
                m.then_inc(s.moe_iota, 1)

            @block.tensor
            def _(pe):
                for t in range(NT):
                    for q in range(4):
                        o = ps[:, t, q * NEXP:(q + 1) * NEXP]
                        nc.tensor.matmul(o, k.XN[:, t * TILE + q * P:t * TILE + (q + 1) * P], w("wg"), start=True, stop=False)
                        m = nc.tensor.matmul(o, k.cf("ones", rows=1), w("bg", rows=1), start=False, stop=True)
                    m.then_inc(s.moe_scores, 1)
                pe.wait_ge(s.moe_hot, 5)
                for t in range(NT):
                    for q in range(4):
                        m = nc.tensor.transpose(ps[0:NEXP, t, q * P:(q + 1) * P], hot[:, 4 * t + q, :], k.cf("identf"))
                    m.then_inc(s.moe_turn, 1)

            @block.vector
            def _(dve):
                dve.wait_ge(s.moe_scores, NT)
                dve.wait_ge(s.moe_iota, 1)
                flat = gs[:].rearrange("p (t q) e -> p t (q e)", q=4)
                nc.vector.tensor_copy(flat, ps[:, :, 0:4 * NEXP]).then_inc(s.moe_hot, 1)
                dve.wait_ge(s.moe_hot, 1)
                nc.vector.tensor_reduce(best[:], gs[:], AX.X, ALU.max).then_inc(s.moe_hot, 1)
                dve.wait_ge(s.moe_hot, 2)
                wide = [P, N // P, NEXP]
                iota = io[:].unsqueeze(1).to_broadcast(wide)
                nc.vector.tensor_tensor(at[:], gs[:], best[:].unsqueeze(2).to_broadcast(wide), ALU.is_equal
                                        ).then_inc(s.moe_hot, 1)
                dve.wait_ge(s.moe_hot, 3)
                nc.vector.scalar_tensor_tensor(out=hot[:], in0=at[:], scalar=-16.0, in1=iota, op0=ALU.mult, op1=ALU.add
                                               ).then_inc(s.moe_hot, 1)
                dve.wait_ge(s.moe_hot, 4)
                nc.vector.tensor_reduce(pick[:], hot[:], AX.X, ALU.min).then_inc(s.moe_pick, 1)
                dve.wait_ge(s.moe_pick, 1)
                nc.vector.tensor_tensor(hot[:], hot[:], pick[:].unsqueeze(2).to_broadcast(wide), ALU.is_equal
                                        ).then_inc(s.moe_hot, 1)
                for t in range(NT):
                    dve.wait_ge(s.moe_turn, t + 1)
                    nc.vector.tensor_copy(hotT[:, t * TILE:(t + 1) * TILE], ps[0:NEXP, t, :]).then_inc(s.moe_turned, 1)

            @block.scalar
            def _(act):
                for t in range(NT):
                    act.wait_ge(s.moe_turned, t + 1)
                    nc.scalar.copy(hotb[:, t * TILE:(t + 1) * TILE], hotT[:, t * TILE:(t + 1) * TILE])

        with nc.Block() as block:
            units = [(e, c) for e in range(NEXP) for c in range(EH // P)]
            M = len(units)

            def slot(n):
                return n % 3

            @block.tensor
            def _(pe):
                pe.wait_ge(s.load_moe, 16)

                def body(t, par):
                    def out(n):
                        e, c = units[n]
                        pe.wait_ge(s.moe_masked, t * M + n + 1)
                        if n == 0:
                            at_least(pe, s.moe_stored, t - 1)
                            pe.nop(nofuse=True)
                            nc.tensor.matmul(ps[:, 5 + par, :], w("b2", rows=NEXP), hotT[:, tok(t)], start=True, stop=False)
                        nc.tensor.matmul(ps[:, 5 + par, :], w("w2", n * P, P), hm[:, slot(n + 2 * par), :],
                                         start=False, stop=(n == M - 1)).then_inc(s.moe_out, 1)
                    for n, (e, c) in enumerate(units):
                        if c == 0:
                            at_least(pe, s.moe_masked, t * M + n - 4)
                            pe.nop(nofuse=True)
                            nc.tensor.matmul(ps[:, 3 + e % 2, :], k.cb("sel", e * P, P, rows=NEXP), hotb[:, tok(t)],
                                             start=True, stop=True)
                        at_least(pe, s.moe_relu, t * M + n - 2)
                        nc.tensor.matmul(ps[:, slot(n + 2 * par), :], w("w1", n * P, P), k.XN[:, tok(t)],
                                         start=True, stop=True).then_inc(s.moe_hidden, 1)
                        if n >= 2:
                            out(n - 2)
                    out(M - 2)
                    out(M - 1)
                for t in range(2):
                    body(t, t)
                with pe.Fori(1, NT // 2) as turn:
                    i = turn * 2
                    for par in range(2):
                        body(i + par, par)

            @block.scalar
            def _(act):
                def body(t, par):
                    for n in range(M):
                        act.wait_ge(s.moe_hidden, t * M + n + 1)
                        at_least(act, s.moe_masked, t * M + n - 2)
                        nc.scalar.activation(hr[:, slot(n + 2 * par), :], ps[:, slot(n + 2 * par), :], ACT.Relu,
                                             bias=w("b1", n, 1)).then_inc(s.moe_relu, 1)
                for t in range(2):
                    body(t, t)
                with act.Fori(1, NT // 2) as turn:
                    i = turn * 2
                    for par in range(2):
                        body(i + par, par)

            @block.vector
            def _(dve):
                def body(t, par):
                    for n, (e, c) in enumerate(units):
                        dve.wait_ge(s.moe_relu, t * M + n + 1)
                        at_least(dve, s.moe_out, t * M + n - 2)
                        nc.vector.tensor_tensor(hm[:, slot(n + 2 * par), :], hr[:, slot(n + 2 * par), :], ps[:, 3 + e % 2, :],
                                                ALU.mult).then_inc(s.moe_masked, 1)
                    dve.wait_ge(s.moe_out, t * M + M)
                    nc.vector.tensor_copy(k.Y[:, tok(t)], ps[:, 5 + par, :]).then_inc(s.moe_stored, 1)
                for t in range(2):
                    body(t, t)
                with dve.Fori(1, NT // 2) as turn:
                    i = turn * 2
                    for par in range(2):
                        body(i + par, par)


def ternary(k, call, wt):
    nc, s, ps = k.nc, k.s, k.ps
    n = 512
    with ExitStack() as ctx:
        part = ctx.enter_context(nc.sbuf_tensor(f"tern_part{call}", [P, 2], F32))
        lim = ctx.enter_context(nc.sbuf_tensor(f"tern_lim{call}", [P, 3], F32))
        lowt = ctx.enter_context(nc.sbuf_tensor(f"tern_low{call}", [P, n], F32))
        hi = ctx.enter_context(nc.sbuf_tensor(f"tern_hi{call}", [P, n], F32))
        block = ctx.enter_context(nc.Block())

        @block.vector
        def _(dve):
            base = 8 * call

            def then(m, j):
                m.then_inc(s.tern, 1)
                dve.wait_ge(s.tern, base + j)
            then(nc.vector.tensor_reduce(part[:, 0:1], wt, AX.X, ALU.add, apply_absolute_value=True), 1)
            dve.wait_ge(s.tern_mean, call + 1)
            then(nc.vector.tensor_scalar(lim[:, 0:1], ps[:, 0, 0:1], 1.0 / n, 1e-8, ALU.mult, ALU.max), 2)
            then(nc.vector.tensor_scalar(lim[:, 1:2], lim[:, 0:1], 0.5, None, ALU.mult), 3)
            then(nc.vector.tensor_scalar(lim[:, 2:3], lim[:, 0:1], -0.5, None, ALU.mult), 4)
            then(nc.vector.tensor_scalar(hi[:], wt, lim[:, 1:2], None, ALU.is_gt), 5)
            then(nc.vector.tensor_scalar(lowt[:], wt, lim[:, 2:3], None, ALU.is_lt), 6)
            then(nc.vector.tensor_tensor(hi[:], hi[:], lowt[:], ALU.subtract), 7)
            nc.vector.tensor_tensor(lowt[:], hi[:], wt, ALU.subtract).then_inc(s.tern_step, 1)
            dve.wait_ge(s.tern_step, 2 * call + 1)
            nc.vector.tensor_tensor(wt, wt, lowt[:], ALU.add).then_inc(s.tern_step, 1)
            nc.vector.sem_inc(s.tern, 1)

        @block.tensor
        def _(pe):
            pe.wait_ge(s.tern, 8 * call + 1)
            nc.tensor.matmul(ps[:, 0, 0:1], k.cf("mean"), part[:, 0:1], start=True, stop=True).then_inc(s.tern_mean, 1)


def fold_products(k, sem, jobs):
    nc, ps = k.nc, k.ps
    done = k.folds
    k.folds += len(jobs)
    with nc.Block() as block:
        @block.tensor
        def _(pe):
            for j, (out, pairs) in enumerate(jobs):
                m, n = out.shape[0], out.shape[-1]
                for e, (a, b) in enumerate(pairs):
                    mm = nc.tensor.matmul(ps[0:m, j, 0:n], a, b, start=(e == 0), stop=(e == len(pairs) - 1))
                mm.then_inc(k.s.fold, 1)

        @block.vector
        def _(dve):
            for j, (out, pairs) in enumerate(jobs):
                m, n = out.shape[0], out.shape[-1]
                dve.wait_ge(k.s.fold, done + j + 1)
                nc.vector.tensor_copy(out, ps[0:m, j, 0:n]).then_inc(k.s.folded, 1)


def gated_linear(k, call, weight, bias, src, out):
    nc, s, ps = k.nc, k.s, k.ps
    base = call * NT
    cols = lambda t: slice(t * TILE, (t + 1) * TILE)
    with nc.Block() as block:
        @block.tensor
        def _(pe):
            for t in range(NT):
                nc.tensor.matmul(ps[:, t, :], weight, src[:, cols(t)], start=True, stop=True).then_inc(s.lin_product, 1)

        @block.scalar
        def _(act):
            for t in range(NT):
                act.wait_ge(s.lin_product, t + 1)
                nc.scalar.activation(k.Y[:, cols(t)], ps[:, t, :], ACT.Silu, bias=bias).then_inc(s.silu, 1)

        @block.vector
        def _(dve):
            for t in range(NT):
                dve.wait_ge(s.silu, base + t + 1)
                nc.vector.tensor_tensor(k.Y[:, cols(t)], k.S[:, cols(t)], k.Y[:, cols(t)], ALU.mult).then_inc(s.gate_times, 1)
                dve.wait_ge(s.gate_times, base + t + 1)
                nc.vector.tensor_tensor(k.X[:, cols(t)], k.X[:, cols(t)], k.Y[:, cols(t)], ALU.add).then_inc(s.gate_added, 1)

        @block.sync
        def _(sp):
            for t in range(NT):
                sp.wait_ge(s.gate_added, base + t + 1)
                sp.dma_start(out[:, cols(t)], k.X[:, cols(t)]).then_inc(s.out_stored, 16)
            sp.wait_ge(s.out_stored, 16 * NT)


class Signals:

    def __init__(self, new):
        self.load_x = new("load_x")
        self.load_const = new("load_const")
        self.load_l0a = new("load_l0a")
        self.load_l0f = new("load_l0f")
        self.load_l1 = new("load_l1")
        self.load_moe = new("load_moe")
        self.load_l2 = new("load_l2")
        self.load_l3 = new("load_l3")
        self.cast = new("cast")
        self.credit = new("credit")
        self.ln_free = new("ln_free")
        self.ln_zero = new("ln_zero")
        self.ln_shifted = new("ln_shifted")
        self.ln_copied = new("ln_copied")
        self.ln_centred = new("ln_centred")
        self.ln_squared = new("ln_squared")
        self.ln_var = new("ln_var")
        self.ln_rstd = new("ln_rstd")
        self.ln_rstd2 = new("ln_rstd2")
        self.ln_vy2 = new("ln_vy2")
        self.ln_exact = new("ln_exact")
        self.ln_affine = new("ln_affine")
        self.rms_free = new("rms_free")
        self.rms_product = new("rms_product")
        self.rms_squared = new("rms_squared")
        self.rms_mean = new("rms_mean")
        self.rms_rstd = new("rms_rstd")
        self.rms_rstd2 = new("rms_rstd2")
        self.rms_vy2 = new("rms_vy2")
        self.rms_exact = new("rms_exact")
        self.rms_weight = new("rms_weight")
        self.ff_gelu = new("ff_gelu")
        self.ff_value = new("ff_value")
        self.ff_value_used = new("ff_value_used")
        self.ff_gate = new("ff_gate")
        self.ff_hid_used = new("ff_hid_used")
        self.ff_out_used = new("ff_out_used")
        self.mix_used = new("mix_used")
        self.mix_product = new("mix_product")
        self.mix_sigmoid = new("mix_sigmoid")
        self.gate_product = new("gate_product")
        self.gate_ready = new("gate_ready")
        self.sp_step = new("sp_step")
        self.sp_max = new("sp_max")
        self.sp_coef = new("sp_coef")
        self.decay = new("decay")
        self.decay2 = new("decay2")
        self.keep = new("keep")
        self.scaled = new("scaled")
        self.reset = new("reset")
        self.scanned = new("scanned")
        self.gated = new("gated")
        self.hs2 = new("hs2")
        self.la_init = new("la_init")
        self.la_shifted = new("la_shifted")
        self.la_vprod = new("la_vprod")
        self.la_rot = new("la_rot")
        self.la_rotated = new("la_rotated")
        self.la_qk = new("la_qk")
        self.la_stored = new("la_stored")
        self.la_squared = new("la_squared")
        self.la_product = new("la_product")
        self.la_rnorm = new("la_rnorm")
        self.la_rnorm2 = new("la_rnorm2")
        self.la_vy2 = new("la_vy2")
        self.la_exact = new("la_exact")
        self.la_clamped = new("la_clamped")
        self.la_vread = new("la_vread")
        self.la_norm = new("la_norm")
        self.la_max = new("la_max")
        self.la_score = new("la_score")
        self.la_m2 = new("la_m2")
        self.la_shift = new("la_shift")
        self.la_mt = new("la_mt")
        self.la_prob = new("la_prob")
        self.la_keyed = new("la_keyed")
        self.la_divided = new("la_divided")
        self.la_attended = new("la_attended")
        self.la_turn = new("la_turn")
        self.la_turned = new("la_turned")
        self.la_out = new("la_out")
        self.la_table = new("la_table")
        self.la_rec = new("la_rec")
        self.la_sqsum = new("la_sqsum")
        self.la_qkp = new("la_qkp")
        self.at_parts = new("at_parts")
        self.at_stacked = new("at_stacked")
        self.at_scratch = new("at_scratch")
        self.at_keyed = new("at_keyed")
        self.at_init = new("at_init")
        self.at_vprod = new("at_vprod")
        self.at_fetched = new("at_fetched")
        self.at_used = new("at_used")
        self.at_product = new("at_product")
        self.at_vread = new("at_vread")
        self.at_max = new("at_max")
        self.at_score = new("at_score")
        self.at_m2 = new("at_m2")
        self.at_shift = new("at_shift")
        self.at_mt = new("at_mt")
        self.at_prob = new("at_prob")
        self.at_divided = new("at_divided")
        self.at_attended = new("at_attended")
        self.at_sums = new("at_sums")
        self.at_raw = new("at_raw")
        self.at_zeroed = new("at_zeroed")
        self.at_stored = new("at_stored")
        self.at_out = new("at_out")
        self.at_rec = new("at_rec")
        self.at_hi = new("at_hi")
        self.at_res = new("at_res")
        self.at_mid = new("at_mid")
        self.at_sum = new("at_sum")
        self.at_content = new("at_content")
        self.alibi_loaded = new("alibi_loaded")
        self.alibi_cast = new("alibi_cast")
        self.alibi_rows = new("alibi_rows")
        self.moe_iota = new("moe_iota")
        self.moe_scores = new("moe_scores")
        self.moe_hot = new("moe_hot")
        self.moe_turn = new("moe_turn")
        self.moe_turned = new("moe_turned")
        self.moe_pick = new("moe_pick")
        self.moe_masked = new("moe_masked")
        self.moe_stored = new("moe_stored")
        self.moe_out = new("moe_out")
        self.moe_relu = new("moe_relu")
        self.moe_hidden = new("moe_hidden")
        self.tern = new("tern")
        self.tern_mean = new("tern_mean")
        self.tern_step = new("tern_step")
        self.fold = new("fold")
        self.folded = new("folded")
        self.lin_product = new("lin_product")
        self.silu = new("silu")
        self.gate_times = new("gate_times")
        self.gate_added = new("gate_added")
        self.out_stored = new("out_stored")


def program(nc, x, cast, conf, rope0, alibi_q, alibi_k, l0a, l0f0, l0f1, l1, moe, l2, l3, out, stop=99):
    with ExitStack() as ctx:
        k = Core()
        s = Signals(lambda name: ctx.enter_context(nc.semaphore(name)))
        k.nc, k.s = nc, s
        sb = lambda n, shape, dt=F32: ctx.enter_context(nc.sbuf_tensor(n, shape, dt))
        k.X, k.XN, k.S, k.Y = (sb(n, [P, N]) for n in ("x", "xn", "s", "y"))
        castt = sb("cast", [P, CAST[1]], BF16)
        conft = sb("conf", [P, CONF[1]])
        k.eps5, k.eps6 = sb("eps5", [P, 1]), sb("eps6", [P, 1])
        k.cb, k.cf = pack(castt, CAST[0]), pack(conft, CONF[0])
        k.ps = ctx.enter_context(nc.psum_tensor("ps", [P, 8, TILE], F32))
        k.shifts = k.rounds = k.stack_dmas = k.folds = 0
        raw = k.Y[:, 0:CAST[1]]

        def dump(buf):
            with nc.Block() as block:
                @block.sync
                def _(sp):
                    sp.dma_start(out, buf[:]).then_inc(s.out_stored, 16)
                    sp.wait_ge(s.out_stored, 16)

        stack = ExitStack()
        with stack:
            new = lambda n, shape, dt=F32: stack.enter_context(nc.sbuf_tensor(n, shape, dt))
            f0, f1, r0 = new("w_l0f0", [P, W_L0F[1]]), new("w_l0f1", [P, W_L0F[1]]), new("w_l0t", [P, W_L0T[1]])
            with nc.sbuf_tensor("w_l0a", [P, W_L0A[1]], F32) as a0:
                with nc.Block() as block:
                    @block.sync
                    def _(sp):
                        sp.dma_start(conft[:], conf).then_inc(s.load_const, 16)
                        for t in range(4):
                            cols = slice(t * N // 4, (t + 1) * N // 4)
                            sp.dma_start(k.X[:, cols], x[:, cols]).then_inc(s.load_x, 16)
                        sp.dma_start(raw, cast).then_inc(s.load_const, 16)
                        sp.dma_start(a0[:], l0a).then_inc(s.load_l0a, 16)
                        sp.dma_start(r0[:], rope0).then_inc(s.load_l0f, 16)
                        sp.dma_start(f0[:], l0f0).then_inc(s.load_l0f, 16)
                        sp.dma_start(f1[:], l0f1).then_inc(s.load_l0f, 16)
                        sp.wait_ge(s.load_x, 64)

                    @block.vector
                    def _(dve):
                        nc.vector.memset(k.eps5[:], 1e-5).then_inc(s.credit, 1)
                        nc.vector.memset(k.eps6[:], 1e-6).then_inc(s.credit, 1)
                        nc.vector.sem_inc(s.ln_free, U)
                        nc.vector.sem_inc(s.rms_free, U)
                        nc.vector.sem_inc(s.ff_gelu, CREDIT)
                        nc.vector.sem_inc(s.ff_value_used, CREDIT)
                        nc.vector.sem_inc(s.ff_hid_used, CREDIT)
                        nc.vector.sem_inc(s.ff_out_used, 2)
                        nc.vector.sem_inc(s.mix_used, 2)
                        dve.wait_ge(s.load_const, 32)
                        nc.vector.tensor_copy(castt[:], raw).then_inc(s.cast, 1)

                layer_norm(k, 0, k.X, k.XN)
                if stop == 1:
                    return dump(k.XN)
                w = pack(a0, W_L0A[0])
                with nc.Block() as block:
                    @block.sync
                    def _(sp):
                        sp.wait_ge(s.load_l0a, 16)
                with ExitStack() as inner:
                    work = [inner.enter_context(nc.sbuf_tensor(n, [P, N], F32)) for n in ("mix_h", "mix_gate")]
                    recurrent_mixer(k, w, work)
            if stop == 2:
                return dump(k.S)
            rope = pack(r0, W_L0T[0])
            with nc.Block() as block:
                @block.sync
                def _(sp):
                    sp.wait_ge(s.load_l0f, 48)
            hid = k.XN
            for layer, t in enumerate((f0, f1)):
                w = pack(t, W_L0F[0])
                src = k.XN if layer == 0 else k.Y
                local_attention(k, layer, w, rope, src, k.Y)
                if stop == 3 + 2 * layer:
                    return dump(k.Y)
                layer_norm(k, 1 + layer, k.Y, hid, shift=True, affine=(w("lg"), w("lb")))
                feed_forward(k, 1 + layer, NT * 3 * (1 + layer), hid, HCH,
                             lambda lo, n: w("w1", HID + lo, n), lambda c, n: w("b1g", c, 1, rows=n),
                             lambda lo, n: w("w1", lo, n), lambda c, n: w("b1a", c, 1, rows=n),
                             lambda c, n: w("w2", c * P, P, rows=n), w("b2"), k.Y, k.Y)
                if stop == 4 + 2 * layer:
                    return dump(k.Y)

        with ExitStack() as inner:
            t1 = inner.enter_context(nc.sbuf_tensor("w_l1", [P, W_L1[1]], F32))
            tm = inner.enter_context(nc.sbuf_tensor("w_moe", [P, W_MOE[1]], F32))
            with nc.Block() as block:
                @block.sync
                def _(sp):
                    sp.dma_start(t1[:], l1).then_inc(s.load_l1, 16)
                    sp.dma_start(tm[:], moe).then_inc(s.load_moe, 16)
                    sp.wait_ge(s.load_l1, 16)
            layer_norm(k, 3, k.X, k.XN, gate=0)
            alibi_attention(k, pack(t1, W_L1[0]), (alibi_q, alibi_k))
            if stop == 8:
                return dump(k.S)
            with nc.Block() as block:
                @block.sync
                def _(sp):
                    sp.wait_ge(s.load_moe, 16)
            experts(k, pack(tm, W_MOE[0]))
            if stop == 9:
                return dump(k.Y)

        with ExitStack() as inner:
            t2 = inner.enter_context(nc.sbuf_tensor("w_l2", [P, W_L2[1]], F32))
            fold = inner.enter_context(nc.sbuf_tensor("l2_fold", [P, 5, P], F32))
            w2 = pack(t2, W_L2[0])
            with nc.Block() as block:
                @block.sync
                def _(sp):
                    sp.dma_start(t2[:], l2).then_inc(s.load_l2, 16)
                    sp.wait_ge(s.load_l2, 16)
            layer_norm(k, 4, k.X, k.XN, gate=1)
            qa, kva = w2("qaT", rows=64), w2("kvaT", rows=32)
            fold_products(k, None, [(fold[:, 0, :], [(qa, w2("qb", rows=64))]), (fold[:, 1, :], [(qa, w2("qbr", rows=64))]),
                                    (fold[:, 2, :], [(kva, w2("kb", rows=32))]), (fold[:, 3, :], [(kva, w2("kbr", rows=32))]),
                                    (fold[:, 4, :], [(kva, w2("vb", rows=32))])])
            rope8_attention(k, w2, fold)
            if stop == 11:
                return dump(k.S)
            ternary(k, 0, w2("f1"))
            ternary(k, 1, w2("f2"))
            feed_forward(k, 3, NT * 9, k.XN, [(c * P, P) for c in range(4)], lambda lo, n: w2("f1", lo, n),
                         lambda c, n: w2("f1b", c, 1), None, None, lambda c, n: w2("f2", c * P, P), w2("f2b"), None, k.Y)
            if stop == 12:
                return dump(k.Y)

        with ExitStack() as inner:
            t3 = inner.enter_context(nc.sbuf_tensor("w_l3", [P, W_L3[1]], F32))
            fold = inner.enter_context(nc.sbuf_tensor("l3_fold", [P, 5 * P], F32))
            w3 = pack(t3, W_L3[0])
            with nc.Block() as block:
                @block.sync
                def _(sp):
                    sp.dma_start(t3[:], l3).then_inc(s.load_l3, 16)
                    sp.wait_ge(s.load_l3, 16)
            layer_norm(k, 5, k.X, k.XN, gate=2)
            qa = w3("qT", rows=64)
            fold_products(k, None, [(fold[:, 0:P], [(qa, w3("qd", rows=64))]), (fold[:, P:5 * P], [(qa, w3("qr", rows=64))])])
            rms_norm(k, 2, None, k.Y, w3("gkv", rows=32), rows=32, mean="mean32", before=(w3("wkv"), k.XN))
            latent_attention(k, w3, fold, k.Y)
            if stop == 14:
                return dump(k.S)
            with ExitStack() as dft:
                AT = dft.enter_context(nc.sbuf_tensor("dft_at", [P, 2, P], F32))
                M = dft.enter_context(nc.sbuf_tensor("dft_m", [P, P], F32))
                fold_products(k, None, [(AT[:, 0, :], [(w3("fr"), w3("dc")), (w3("fi"), w3("ds"))]),
                                        (AT[:, 1, :], [(w3("fi"), w3("dc")), (w3("fr"), w3("dsn"))])])
                fold_products(k, None, [(M[:], [(AT[:, 0, :], w3("dcm")), (AT[:, 1, :], w3("dsm"))])])
                gated_linear(k, 3, M[:], w3("fb"), k.XN, out)


def lay(where, **parts):
    packed = np.zeros((P, where[1]), np.float32)
    for name, a in parts.items():
        at, n = where[0][name]
        a = np.asarray(a)
        a = a.reshape(a.shape[0], -1)
        assert a.shape[1] == n, (name, a.shape, n)
        packed[:a.shape[0], at:at + n] = a
    return packed


def chunked(a, rows=P):
    return a.reshape(-1, rows, a.shape[1]).transpose(1, 0, 2).reshape(rows, -1)


def columns(v):
    return v.reshape(-1, P).T


def padded(a, sizes):
    out, at = [], 0
    for n in sizes:
        out.append(np.concatenate([a[at:at + n], np.zeros((P - n, a.shape[1]), a.dtype)], 0))
        at += n
    return np.concatenate(out, 1)


def kernel(**inputs):
    import concourse.bacc as bacc
    from concourse.bass_utils import run_bass_kernel_spmd
    v = {n: np.asarray(a) for n, a in inputs.items()}
    g = lambda layer: {n[len(layer):]: a for n, a in v.items() if n.startswith(layer)}
    packs = {}
    packs["x"] = np.ascontiguousarray(v["L0_attn_hidden_states"].reshape(N, P).T)
    packs["cast"] = np.concatenate([a for _, a in const_cast()], 1).astype(np.float32)
    packs["conf"] = np.concatenate([a for _, a in const_f32()], 1).astype(np.float32)
    packs["rope0"] = np.concatenate([a for _, a in const_local_rope()], 1).astype(np.float32)
    packs["alibi_q"], packs["alibi_k"] = const_alibi()
    a = g("L0_attn_")
    col = lambda x: x.reshape(-1, 1)
    packs["l0a"] = lay(W_L0A, fc=a["fc_w"].T, fr=a["fc_r_w"].T, fi=a["fc_i_w"].T, gate=a["fc_gate_w"].T,
                       mg=a["mlp_gate_w"].T, mf=a["mlp_fc_w"].T, mo=chunked(a["out_w"].T), fc_b=col(a["fc_b"]),
                       fr_b=col(a["fc_r_b"]), fi_b=col(a["fc_i_b"]), gate_b=col(a["fc_gate_b"]), norm=col(a["norm_w"]),
                       norm2=col(a["norm2_w"]), alpha=col(a["alpha"]), mo_b=col(a["out_b"]),
                       mg_b=columns(a["mlp_gate_b"]), mf_b=columns(a["mlp_fc_b"]))
    a = g("L0_ffn_")
    halves = np.arange(512).reshape(2, 4, 2, 32).transpose(0, 2, 1, 3).reshape(-1)
    four = lambda x: col(np.concatenate([x] * 4))
    sizes = [n for _, n in HCH]
    for l in range(2):
        wq, wk, wv = np.split(a["wqkv"][l], 3, 1)
        b1 = a["b1"][l].reshape(-1, 1)
        packs[f"l0f{l}"] = lay(W_L0F, wq=wq[:, halves], wk=wk[:, halves], wv=wv, wo=chunked(a["wo"][l]),
                               w1=a["w1"][l], w2=padded(a["w2"][l], sizes), q1=four(a["q_scale"][l][:32]),
                               q2=four(a["q_scale"][l][32:]), k1=four(a["k_scale"][l][:32]), k2=four(a["k_scale"][l][32:]),
                               lg=col(a["ln_g"][l]), lb=col(a["ln_b"][l]), b1a=padded(b1[:HID], sizes),
                               b1g=padded(b1[HID:], sizes), b2=col(a["b2"][l]))
    a = g("L1_attn_")
    wq, wk, wv = np.split(a["w_attn"], 3, 0)
    packs["l1"] = lay(W_L1, wq=wq.T[:, DH], wk=wk.T[:, DH], wv=wv.T, wo=a["w_proj"].T)
    a = g("L1_ffn_")
    packs["moe"] = lay(W_MOE, wg=a["Wg"], bg=a["bg"].reshape(1, -1), w1=a["W1"].transpose(1, 0, 2),
                       w2=chunked(a["W2"].reshape(-1, P)), b1=columns(a["b1"]), b2=a["b2"])
    a, f = g("L2_attn_"), g("L2_ffn_")
    kv = a["Wkvb"].reshape(-1, 4, D8, 2)
    kb = np.repeat(kv[..., 0], 4, 1).reshape(-1, P)
    vb = np.repeat(kv[..., 1], 4, 1).reshape(-1, P)
    swap = [h * D8 + (d ^ 1) for d in range(D8) for h in range(H16)]
    packs["l2"] = lay(W_L2, qaT=a["Wqa"].T, qb=a["Wqb"][:, DH], qbr=a["Wqb"][:, swap], kvaT=a["Wkva"].T, kb=kb[:, DH],
                      kbr=kb[:, swap], vb=vb, wo=a["Wout"], bo=col(a["bout"]),
                      cos=dict(const_rope8())["cos"], sin=dict(const_rope8())["sin"],
                      f1=f["W1"].T, f1b=columns(f["b1"]), f2=chunked(f["W2"].T), f2b=col(f["b2"]))
    a, f = g("L3_attn_"), g("L3_ffn_")
    dh32 = [h * 32 + d for d in range(32) for h in range(H16)]
    packs["l3"] = lay(W_L3, wkv=a["W_kv"], gkv=col(a["g_kv"]), kd=a["W_kdec"][:, DH], vd=a["W_vdec"], qT=a["W_q"].T,
                      qd=a["W_qdec"][:, DH], qr=a["W_qrope"][:, dh32], kr=a["W_krope"][:, dh32], wo=a["W_o"],
                      fr=f["w_freq_real"], fi=f["w_freq_imag"], fb=col(f["bias"]),
                      **dict(const_rope32()), **dict(const_dft()))
    nc = bacc.Bacc("TRN2", target_bir_lowering=False, num_devices=1)
    args = [nc.dram_tensor(f"in_{n}", p.shape, F32, kind="ExternalInput").ap() for n, p in packs.items()]
    out = nc.dram_tensor("out_0", (P, N), F32, kind="ExternalOutput").ap()
    program(nc, *args, out)
    r = run_bass_kernel_spmd(nc, [{f"in_{n}": np.ascontiguousarray(p) for n, p in packs.items()}], core_ids=[0])
    return np.ascontiguousarray(r.results[0]["out_0"].T).reshape(B, L, P)
```

```python
from contextlib import ExitStack

import numpy as np

import concourse.bass as bass
from concourse import mybir

ALU = mybir.AluOpType
ACT = mybir.ActivationFunctionType
AX = mybir.AxisListType
F32 = mybir.dt.float32
BF16 = mybir.dt.bfloat16
I32, U32 = mybir.dt.int32, mybir.dt.uint32

P = 128
B, L = 16, 256
N = B * L
TILE = 512
NT = N // TILE
U = 4
H16, D8 = 16, 8
GW = 64
LAGS, LAGS_WIDE = (3, 5, 4), (4, 6, 4)
ROUND = 3
H8, D64 = 8, 64
HID = 341
HCH = [(0, 128), (128, 128), (256, HID - 256)]
FCH = [(0, 128), (128, 128), (256, 128)]
NEXP, EH = 8, 512
BIG = -1e30
CREDIT = 3


def const_cast():
    i = np.arange(P)
    ident = np.eye(P)
    causal = np.where(i[None, :] <= i[:, None], 0.0, BIG)
    band = lambda q, k: np.where((q - k >= 0) & (q - k <= 64), 0.0, BIG)
    q, k, j = i[:, None], i[None, :], np.arange(192)[None, :]
    local_q0 = band(q, k)
    local_q1 = band(q + 128, j + 64)
    local_k0 = band(j, i[:, None])
    sel = np.zeros((P, H16, P))
    for h in range(H16):
        sel[h, h] = sel[32 + h, h] = 1.0
    parts = [("ident", ident), ("causal_q", causal), ("causal_k", causal.T), ("local_q0", local_q0),
             ("local_q1", local_q1), ("local_k0", local_k0), ("sel", sel.reshape(P, -1))]
    return parts


def const_f32():
    c = np.arange(P)
    blk = (c[:, None] // 32 == c[None, :] // 32).astype(np.float64)
    return [("centre", np.eye(P) - 1.0 / P), ("mean", np.full((P, P), 1.0 / P)), ("block32", blk), ("identf", np.eye(P)),
            ("mean32", np.full((P, 32), 1.0 / 32)), ("ones", np.ones((P, P))),
            ("before", np.triu(np.ones((P, P)), 1))]


def const_local_rope():
    half = np.arange(0, D64, 2, dtype=np.float32)
    inv = np.float32(1.0) / np.float32(10000.0) ** (half / np.float32(D64))
    t = np.arange(L, dtype=np.float32)
    fr = (t[:, None] * inv[None, :]).astype(np.float32).astype(np.float64).T
    base = (half.astype(np.float64) + 0.4 * D64) / (1.4 * D64)
    power = (t.astype(np.float64) - L // 2) / 32.0
    sc = (base[None, :] ** power[:, None]).T
    four = lambda a: -0.5 * np.concatenate([a] * 4, 0)
    return [("qc", four(np.cos(fr) * sc)), ("qs", four(np.sin(fr) * sc)),
            ("kc", four(np.cos(fr) / sc)), ("ks", four(np.sin(fr) / sc))]


def const_rope8():
    inv = np.float32(1.0) / np.float32(10000.0) ** (np.arange(0, D8, 2, dtype=np.float32) / np.float32(D8))
    fr = np.outer(np.arange(L, dtype=np.float32), inv).astype(np.float32).astype(np.float64)
    d = np.arange(P) // H16
    cos, sin = np.cos(fr)[:, d // 2].T, np.sin(fr)[:, d // 2].T
    return [("cos", cos), ("sin", np.where(d % 2 == 0, -1.0, 1.0)[:, None] * sin)]


def const_rope32():
    inv = np.float32(1.0) / np.float32(10000.0) ** (np.arange(0, 32, 2, dtype=np.float32) / np.float32(32))
    fr = np.outer(np.arange(L, dtype=np.float32), inv).astype(np.float32).astype(np.float64)
    cos, sin = [], []
    for c in range(2):
        d = 8 * c + np.arange(P) // H16
        cos += [np.cos(fr)[:, d].T] * 2
        sin += [-np.sin(fr)[:, d].T, np.sin(fr)[:, d].T]
    return [("cos", np.concatenate(cos, 1)), ("sin", np.concatenate(sin, 1))]


def const_dft():
    a = 2 * np.pi * (np.outer(np.arange(P), np.arange(P)) % P) / P
    return [("dc", np.cos(a)), ("ds", np.sin(a)), ("dsn", -np.sin(a)), ("dcm", np.cos(a) / P), ("dsm", -np.sin(a) / P)]


def const_alibi():
    slopes = np.array([(2.0 ** -0.5) ** (h + 1) for h in range(H16)])
    v = (slopes[:, None] * np.sqrt(8.0) * np.arange(L)[None, :]).astype(np.float32)

    def bf(a):
        u = a.astype(np.float32).view(np.uint32)
        u = (u + 0x7FFF + ((u >> 16) & 1)) & np.uint32(0xFFFF0000)
        return u.view(np.float32)

    hi = bf(v)
    mid = bf(v - hi)
    lo = v - hi - mid
    rows = np.stack([hi, mid, lo]).reshape(3, -1)
    ones = np.ones_like(rows)
    return np.concatenate([ones, -rows], 0), np.concatenate([rows, ones], 0)


def widths(parts):
    at, where = 0, {}
    for name, n in parts:
        where[name] = (at, n)
        at += n
    return where, at


CAST = widths([(n, a.shape[1]) for n, a in const_cast()])
CONF = widths([(n, a.shape[1]) for n, a in const_f32()])
DH = [d * 1 + h * D8 for d in range(D8) for h in range(H16)]
W_L0A = widths([("fc", P), ("fr", P), ("fi", P), ("gate", P), ("mg", 3 * P), ("mf", 3 * P), ("mo", 3 * P), ("fc_b", 1),
                ("fr_b", 1), ("fi_b", 1), ("gate_b", 1), ("norm", 1), ("norm2", 1), ("alpha", 1), ("mo_b", 1),
                ("mg_b", 3), ("mf_b", 3)])
W_L0F = widths([("wq", 512), ("wk", 512), ("wv", 512), ("wo", 512), ("w1", 2 * HID),
                ("w2", 3 * P), ("q1", 1), ("q2", 1), ("k1", 1), ("k2", 1), ("lg", 1), ("lb", 1), ("b1a", 3),
                ("b1g", 3), ("b2", 1)])
W_L0T = widths([("qc", L), ("qs", L), ("kc", L), ("ks", L)])
W_L1 = widths([("wq", P), ("wk", P), ("wv", P), ("wo", P), ("wg", NEXP), ("bg", 1)])
W_MOE = widths([("w1", NEXP * EH), ("w2", NEXP * EH)])
W_MOEB = widths([("b1", NEXP * EH), ("b2", NEXP * P)])
W_L2 = widths([("qaT", P), ("qb", P), ("qbr", P), ("kvaT", P), ("kb", P), ("kbr", P), ("vb", P), ("wo", P), ("bo", 1),
               ("cos", L), ("sin", L), ("f1", 512), ("f1b", 4), ("f2", 512), ("f2b", 1)])
W_L3 = widths([("wkv", 32), ("gkv", 1), ("kd", P), ("vd", P), ("qT", P), ("qd", P), ("qr", 512), ("kr", 512), ("wo", P),
               ("cos", 4 * L), ("sin", 4 * L), ("dc", P), ("ds", P), ("dsn", P), ("dcm", P), ("dsm", P), ("fr", P),
               ("fi", P), ("fb", 1)])


def pack(tile, where):
    def part(name, lo=0, n=None, rows=P):
        at, width = where[name]
        n = width - lo if n is None else n
        return tile[0:rows, at + lo:at + lo + n]
    return part


class Core:
    pass


def at_least(eng, sem, value):
    if isinstance(value, int) and value <= 0:
        return
    eng.wait_ge(sem, value)


def tok(t, n=TILE):
    return bass.ds(t * n, n)


def norm_steps(eng, *stages):
    for i in range(NT + max(lag for lag, _ in stages)):
        for lag, stage in stages:
            if 0 <= i - lag < NT:
                stage(i - lag)


def layer_norm(k, call, src, dst, shift=False, affine=None, gate=None, jobs=()):
    nc, s = k.nc, k.s
    base = call * NT
    cols = lambda t: slice(t * TILE, (t + 1) * TILE)
    places, bank, col = [], 6, 0
    for out, a, b in jobs:
        n = out.shape[-1]
        if col + n > TILE:
            bank, col = bank + 1, 0
        places.append(k.ps[0:out.shape[0], bank, col:col + n])
        col += n
    k.folds += len(jobs)
    with ExitStack() as ctx:
        sq = ctx.enter_context(nc.sbuf_tensor(f"ln_sq{call}", [P, U, TILE], F32))
        rs = ctx.enter_context(nc.sbuf_tensor(f"ln_rs{call}", [P, U, TILE], F32))
        y2 = ctx.enter_context(nc.sbuf_tensor(f"ln_y2{call}", [P, U, TILE], F32))
        hs = ctx.enter_context(nc.sbuf_tensor(f"ln_hs{call}", [P, U, TILE], F32)) if shift else None
        block = ctx.enter_context(nc.Block())

        if shift or gate is not None:
            @block.gpsimd
            def _(pool):
                if shift:
                    rows = hs[64:128, :, :].rearrange("p u (b l) -> p (u b) l", l=L)
                    nc.gpsimd.memset(rows[:, :, 0:1], 0.0).then_inc(s.ln_zero, 1)
                    pool.wait_ge(s.ln_zero, k.shifts + 1)
                for t in range(NT):
                    if shift:
                        pool.wait_ge(s.ln_free, base + t + 1)
                        nc.gpsimd.tensor_copy(hs[0:64, t % U, :], src[0:64, cols(t)]).then_inc(s.ln_copied, 1)
                    else:
                        pool.wait_ge(s.gate_times, gate * NT + t + 1)
                        nc.gpsimd.tensor_tensor(src[:, cols(t)], src[:, cols(t)], k.Y[:, cols(t)], ALU.add
                                                ).then_inc(s.gate_added, 1)

        @block.tensor
        def _(pe):
            for (out, a, b), to in zip(jobs, places):
                m = nc.tensor.matmul(to, a, b, start=True, stop=True)
                m.then_inc(s.fold, 1)

            def centre(t):
                pe.wait_ge(s.ln_free, base + t + 1)
                if shift:
                    pe.wait_ge(s.ln_zero, k.shifts + 1)
                    pe.wait_ge(s.ln_copied, k.shifts * NT + t + 1)
                    pe.wait_ge(s.ln_shifted, k.shifts * NT + t + 1)
                if gate is not None:
                    pe.wait_ge(s.gate_added, gate * NT + t + 1)
                x = hs[:, t % U, :] if shift else src[:, cols(t)]
                nc.tensor.matmul(k.ps[:, t % U, :], k.cf("centre"), x, start=True, stop=True).then_inc(s.ln_centred, 1)

            def variance(t):
                pe.wait_ge(s.ln_squared, base + t + 1)
                if jobs and t == 2:
                    pe.wait_ge(s.folded, k.folds)
                nc.tensor.matmul(k.ps[:, U + t % U, :], k.cf("mean"), sq[:, t % U, :], start=True, stop=True
                                 ).then_inc(s.ln_var, 1)
            norm_steps(pe, (0, centre), (1, variance))

        @block.scalar
        def _(act):
            if gate is not None:
                for t in range(NT):
                    nc.scalar.activation(k.Y[:, cols(t)], k.Y[:, cols(t)], ACT.Silu).then_inc(s.silu, 1)

            def square(t):
                act.wait_ge(s.ln_centred, base + t + 1)
                nc.scalar.activation(sq[:, t % U, :], k.ps[:, t % U, :], ACT.Square).then_inc(s.ln_squared, 1)

            def rsqrt(t):
                act.wait_ge(s.ln_var, base + t + 1)
                nc.scalar.activation(rs[:, t % U, :], k.ps[:, U + t % U, :], ACT.Abs_reciprocal_sqrt, bias=k.eps5[:, 0:1]
                                     ).then_inc(s.ln_rstd, 1)

            def square_root(t):
                act.wait_ge(s.ln_rstd, base + t + 1)
                nc.scalar.activation(y2[:, t % U, :], rs[:, t % U, :], ACT.Square).then_inc(s.ln_rstd2, 1)
            norm_steps(act, (0, square), (2, rsqrt), (2, square_root))

        @block.vector
        def _(dve):
            if jobs:
                dve.wait_ge(s.fold, k.folds)
            for (out, a, b), at in zip(jobs, places):
                nc.vector.tensor_copy(out, at).then_inc(s.folded, 1)
            if shift:
                dve.wait_ge(s.ln_zero, k.shifts + 1)

            def gated(t):
                if gate is not None:
                    dve.wait_ge(s.silu, gate * NT + t + 1)
                    nc.vector.tensor_tensor(k.Y[:, cols(t)], k.S[:, cols(t)], k.Y[:, cols(t)], ALU.mult
                                            ).then_inc(s.gate_times, 1)

            def shifted(t):
                if shift:
                    dve.wait_ge(s.ln_free, base + t + 1)
                    by_row = lambda v: v.rearrange("p (b l) -> p b l", l=L)
                    nc.vector.tensor_copy(by_row(hs[64:128, t % U, :])[:, :, 1:L], by_row(src[64:128, cols(t)])[:, :, 0:L - 1]
                                          ).then_inc(s.ln_shifted, 1)

            def exact(t):
                u = t % U
                dve.wait_ge(s.ln_rstd2, base + t + 1)
                nc.vector.scalar_tensor_tensor(out=y2[:, u, :], in0=k.ps[:, U + u, :], scalar=1e-5, in1=y2[:, u, :],
                                               op0=ALU.add, op1=ALU.mult).then_inc(s.ln_vy2, 1)
                dve.wait_ge(s.ln_vy2, base + t + 1)
                nc.vector.scalar_tensor_tensor(out=rs[:, u, :], in0=y2[:, u, :], scalar=-3.0, in1=rs[:, u, :],
                                               op0=ALU.add, op1=ALU.mult).then_inc(s.ln_exact, 1)
                dve.wait_ge(s.ln_exact, base + t + 1)
                nc.vector.scalar_tensor_tensor(out=dst[:, cols(t)], in0=rs[:, u, :], scalar=-0.5, in1=k.ps[:, u, :],
                                               op0=ALU.mult, op1=ALU.mult).then_inc(s.ln_free, 1)
                if affine:
                    dve.wait_ge(s.ln_free, base + U + t + 1)
                    nc.vector.tensor_scalar(dst[:, cols(t)], dst[:, cols(t)], affine[0], affine[1], ALU.mult, ALU.add
                                            ).then_inc(s.ln_affine, 1)
            norm_steps(dve, (0, gated), (0, shifted), (3, exact))
    if shift:
        k.shifts += 1


def rms_norm(k, call, src, dst, weight, rows=P, mean="mean", before=None):
    nc, s = k.nc, k.s
    base = call * NT
    cols = lambda t: slice(t * TILE, (t + 1) * TILE)
    with ExitStack() as ctx:
        sq = ctx.enter_context(nc.sbuf_tensor(f"rms_sq{call}", [P, U, TILE], F32))
        rs = ctx.enter_context(nc.sbuf_tensor(f"rms_rs{call}", [P, U, TILE], F32))
        y2 = ctx.enter_context(nc.sbuf_tensor(f"rms_y2{call}", [P, U, TILE], F32))
        wh = ctx.enter_context(nc.sbuf_tensor(f"rms_wh{call}", [P, 1], F32))
        block = ctx.enter_context(nc.Block())
        x = lambda t: k.ps[0:rows, t % U, :] if before else src[:, cols(t)]

        @block.tensor
        def _(pe):
            def product(t):
                if before:
                    pe.wait_ge(s.rms_free, base + t + 1)
                    nc.tensor.matmul(k.ps[0:rows, t % U, :], before[0], before[1][:, cols(t)], start=True, stop=True
                                     ).then_inc(s.rms_product, 1)

            def square_mean(t):
                pe.wait_ge(s.rms_squared, base + t + 1)
                nc.tensor.matmul(k.ps[0:rows, U + t % U, :], k.cf(mean, rows=rows, n=rows), sq[0:rows, t % U, :],
                                 start=True, stop=True).then_inc(s.rms_mean, 1)
            norm_steps(pe, (0, product), (1, square_mean))

        @block.scalar
        def _(act):
            def square(t):
                act.wait_ge(s.rms_free, base + t + 1)
                if before:
                    act.wait_ge(s.rms_product, t + 1)
                nc.scalar.activation(sq[0:rows, t % U, :], x(t), ACT.Square).then_inc(s.rms_squared, 1)

            def rsqrt(t):
                act.wait_ge(s.rms_mean, base + t + 1)
                nc.scalar.activation(rs[0:rows, t % U, :], k.ps[0:rows, U + t % U, :], ACT.Abs_reciprocal_sqrt,
                                     bias=k.eps6[0:rows, 0:1]).then_inc(s.rms_rstd, 1)

            def square_root(t):
                act.wait_ge(s.rms_rstd, base + t + 1)
                nc.scalar.activation(y2[0:rows, t % U, :], rs[0:rows, t % U, :], ACT.Square).then_inc(s.rms_rstd2, 1)
            norm_steps(act, (0, square), (2, rsqrt), (2, square_root))

        @block.vector
        def _(dve):
            nc.vector.tensor_scalar(wh[0:rows, :], weight, -0.5, None, ALU.mult).then_inc(s.rms_weight, 1)
            dve.wait_ge(s.rms_weight, call + 1)

            def exact(t):
                u = t % U
                dve.wait_ge(s.rms_rstd2, base + t + 1)
                nc.vector.scalar_tensor_tensor(out=y2[0:rows, u, :], in0=k.ps[0:rows, U + u, :], scalar=1e-6,
                                               in1=y2[0:rows, u, :], op0=ALU.add, op1=ALU.mult).then_inc(s.rms_vy2, 1)
                dve.wait_ge(s.rms_vy2, base + t + 1)
                nc.vector.scalar_tensor_tensor(out=rs[0:rows, u, :], in0=y2[0:rows, u, :], scalar=-3.0,
                                               in1=rs[0:rows, u, :], op0=ALU.add, op1=ALU.mult).then_inc(s.rms_exact, 1)
                dve.wait_ge(s.rms_exact, base + t + 1)
                nc.vector.scalar_tensor_tensor(out=dst[0:rows, cols(t)], in0=x(t), scalar=wh[0:rows, :],
                                               in1=rs[0:rows, u, :], op0=ALU.mult, op1=ALU.mult).then_inc(s.rms_free, 1)
            norm_steps(dve, (0, exact))


def feed_forward(k, call, units, src, chunks, gate_w, gate_b, value_w, value_b, out_w, out_b, resid, dst):
    nc, s = k.nc, k.s
    nch = len(chunks)
    base = call * NT
    RH = 3 if value_w else 4
    with ExitStack() as ctx:
        gl = ctx.enter_context(nc.sbuf_tensor(f"ff_gl{call}", [P, RH, TILE], F32))
        hid = ctx.enter_context(nc.sbuf_tensor(f"ff_hid{call}", [P, RH, TILE], F32))
        block = ctx.enter_context(nc.Block())
        seq = [(u, c) for u in range(U) for c in range(nch)]

        @block.tensor
        def _(pe):
            with pe.Fori(0, NT // U) as turn:
                i = turn * U
                def outs(n):
                    u, c = seq[n]
                    unit = units + i * nch + n
                    pe.wait_ge(s.ff_value_used if value_w else s.ff_gelu, unit + 1 + CREDIT)
                    if c == 0:
                        pe.wait_ge(s.ff_out_used, base + i + u + 1)
                    lo, w = chunks[c]
                    m = nc.tensor.matmul(k.ps[:, 6 + u % 2, :], out_w(c, w), hid[0:w, n % RH, :],
                                         start=(c == 0), stop=(c == nch - 1))
                    m.then_inc(s.ff_hid_used, 1)
                for n, (u, c) in enumerate(seq):
                    lo, w = chunks[c]
                    unit = units + i * nch + n
                    pe.wait_ge(s.ff_gelu, unit + 1)
                    x = src[:, tok(i + u)]
                    nc.tensor.matmul(k.ps[0:w, n % RH, :], gate_w(lo, w), x, start=True, stop=True
                                     ).then_inc(s.ff_gate, 1)
                    if value_w:
                        pe.wait_ge(s.ff_value_used, unit + 1)
                        nc.tensor.matmul(k.ps[0:w, 3 + n % RH, :], value_w(lo, w), x, start=True, stop=True
                                         ).then_inc(s.ff_value, 1)
                    if n >= 2:
                        outs(n - 2)
                outs(len(seq) - 2)
                outs(len(seq) - 1)

        @block.scalar
        def _(act):
            with act.Fori(0, NT // U) as turn:
                i = turn * U
                for n, (u, c) in enumerate(seq):
                    lo, w = chunks[c]
                    unit = units + i * nch + n
                    act.wait_ge(s.ff_gate, unit + 1)
                    if value_w:
                        act.wait_ge(s.ff_value_used, unit + 1)
                        to = gl[0:w, n % RH, :]
                    else:
                        act.wait_ge(s.ff_hid_used, unit + 1)
                        to = hid[0:w, n % RH, :]
                    g = nc.scalar.activation(to, k.ps[0:w, n % RH, :], ACT.Gelu, bias=gate_b(c, w))
                    g.then_inc(s.ff_gelu, 1)

        @block.vector
        def _(dve):
            with dve.Fori(0, NT // U) as turn:
                i = turn * U
                def finish(u):
                    t = i + u
                    dve.wait_ge(s.ff_hid_used, units + (t + 1) * nch + CREDIT)
                    if resid is None:
                        m = nc.vector.tensor_scalar(dst[:, tok(t)], k.ps[:, 6 + u % 2, :], out_b, None, ALU.add)
                    else:
                        m = nc.vector.scalar_tensor_tensor(out=dst[:, tok(t)], in0=k.ps[:, 6 + u % 2, :], scalar=out_b,
                                                           in1=resid[:, tok(t)], op0=ALU.add, op1=ALU.add)
                    m.then_inc(s.ff_out_used, 1)
                for n, (u, c) in enumerate(seq):
                    lo, w = chunks[c]
                    unit = units + i * nch + n
                    if value_w:
                        dve.wait_ge(s.ff_gelu, unit + 1 + CREDIT)
                        dve.wait_ge(s.ff_value, unit + 1)
                        dve.wait_ge(s.ff_hid_used, unit + 1)
                        nc.vector.scalar_tensor_tensor(out=hid[0:w, n % RH, :], in0=k.ps[0:w, 3 + n % RH, :],
                                                       scalar=value_b(c, w), in1=gl[0:w, n % RH, :],
                                                       op0=ALU.add, op1=ALU.mult).then_inc(s.ff_value_used, 1)
                    if c == nch - 1 and u >= 1:
                        finish(u - 1)
                finish(U - 1)


def recurrent_mixer(k, w, work):
    nc, s = k.nc, k.s
    XN, S, Y = k.XN, k.S, k.Y
    Hb, GT = work
    R, Uv = Y, S
    rms_norm(k, 0, XN, Hb, w("norm"))

    outer = ExitStack()
    sp = outer.enter_context(nc.sbuf_tensor("mix_sp", [P, 6], F32))
    with ExitStack() as ctx:
        ig = ctx.enter_context(nc.sbuf_tensor("mix_i", [P, 2, TILE], F32))
        block = ctx.enter_context(nc.Block())

        @block.tensor
        def _(pe):
            with pe.Fori(0, NT // 2) as turn:
                i = turn * 2
                for u in range(2):
                    pe.wait_ge(s.mix_used, i + u + 1)
                    for n, name in enumerate(("fr", "fi", "fc")):
                        nc.tensor.matmul(k.ps[:, 2 * n + u, :], w(name), Hb[:, tok(i + u)], start=True, stop=True
                                         ).then_inc(s.mix_product, 1)

        @block.scalar
        def _(act):
            nc.scalar.activation(sp[:, 0:1], w("alpha"), ACT.Abs).then_inc(s.sp_step, 1)
            act.wait_ge(s.sp_step, 1)
            nc.scalar.activation(sp[:, 1:2], sp[:, 0:1], ACT.Exp, scale=-1.0).then_inc(s.sp_step, 1)
            act.wait_ge(s.sp_step, 2)
            nc.scalar.activation(sp[:, 2:3], sp[:, 1:2], ACT.Ln, bias=k.cf("ones", n=1)).then_inc(s.sp_step, 1)
            with act.Fori(0, NT // 2) as turn:
                i = turn * 2
                for u in range(2):
                    act.wait_ge(s.mix_product, 3 * (i + u) + 2)
                    nc.scalar.activation(R[:, tok(i + u)], k.ps[:, u, :], ACT.Sigmoid, bias=w("fr_b"))
                    nc.scalar.activation(ig[:, u, :], k.ps[:, 2 + u, :], ACT.Sigmoid, bias=w("fi_b")
                                         ).then_inc(s.mix_sigmoid, 1)

        @block.vector
        def _(dve):
            nc.vector.tensor_scalar(sp[:, 3:4], w("alpha"), 0.0, None, ALU.max).then_inc(s.sp_max, 1)
            dve.wait_ge(s.sp_max, 1)
            dve.wait_ge(s.sp_step, 3)
            nc.vector.tensor_tensor(sp[:, 5:6], sp[:, 3:4], sp[:, 2:3], ALU.add).then_inc(s.sp_max, 1)
            dve.wait_ge(s.sp_max, 2)
            nc.vector.tensor_scalar(sp[:, 4:5], sp[:, 5:6], -8.0, None, ALU.mult).then_inc(s.sp_coef, 1)
            with dve.Fori(0, NT // 2) as turn:
                i = turn * 2
                for u in range(2):
                    dve.wait_ge(s.mix_sigmoid, i + u + 1)
                    dve.wait_ge(s.mix_product, 3 * (i + u) + 3)
                    nc.vector.scalar_tensor_tensor(out=Uv[:, tok(i + u)], in0=k.ps[:, 4 + u, :], scalar=w("fc_b"),
                                                   in1=ig[:, u, :], op0=ALU.add, op1=ALU.mult).then_inc(s.mix_used, 1)

    with outer as ctx:
        NC = N // (2 * TILE)
        a2 = ctx.enter_context(nc.sbuf_tensor("mix_a2", [P, NC, 2 * TILE], F32))
        block = ctx.enter_context(nc.Block())

        @block.tensor
        def _(pe):
            for t in range(NT):
                nc.tensor.matmul(k.ps[:, t, :], w("gate"), Hb[:, t * TILE:(t + 1) * TILE], start=True, stop=True
                                 ).then_inc(s.gate_product, 1)

        @block.scalar
        def _(act):
            act.wait_ge(s.sp_coef, 1)
            for c in range(NC):
                cols = slice(c * 2 * TILE, (c + 1) * 2 * TILE)
                nc.scalar.activation(R[:, cols], R[:, cols], ACT.Exp, scale=sp[:, 4:5]).then_inc(s.decay, 1)
            for c in range(NC):
                act.wait_ge(s.decay2, c + 1)
                nc.scalar.activation(a2[:, c, :], a2[:, c, :], ACT.Sqrt, scale=-1.0, bias=k.cf("ones", n=1)
                                     ).then_inc(s.keep, 1)
            for t in range(NT):
                act.wait_ge(s.gate_product, t + 1)
                nc.scalar.activation(GT[:, t * TILE:(t + 1) * TILE], k.ps[:, t, :], ACT.Gelu, bias=w("gate_b")
                                     ).then_inc(s.gate_ready, 1)

        @block.gpsimd
        def _(pool):
            for c in range(NC):
                cols = slice(c * 2 * TILE, (c + 1) * 2 * TILE)
                pool.wait_ge(s.decay, c + 1)
                nc.gpsimd.tensor_tensor(a2[:, c, :], R[:, cols], R[:, cols], ALU.mult).then_inc(s.decay2, 1)
            for t in range(NT):
                cols = slice(t * TILE, (t + 1) * TILE)
                pool.wait_ge(s.gated, t + 1)
                nc.gpsimd.tensor_tensor(Uv[:, cols], Uv[:, cols], XN[:, cols], ALU.add).then_inc(s.hs2, 1)

        @block.vector
        def _(dve):
            for c in range(NC):
                cols = slice(c * 2 * TILE, (c + 1) * 2 * TILE)
                dve.wait_ge(s.decay2, c + 1)
                nc.vector.memset(R[:, cols].rearrange("p (b l) -> p b l", l=L)[:, :, 0:1], 0.0).then_inc(s.reset, 1)
                dve.wait_ge(s.keep, c + 1)
                nc.vector.tensor_tensor(Uv[:, cols], Uv[:, cols], a2[:, c, :], ALU.mult).then_inc(s.scaled, 1)
                dve.wait_ge(s.scaled, c + 1)
                dve.wait_ge(s.reset, c + 1)
                nc.vector.tensor_tensor_scan(Uv[:, cols], R[:, cols], Uv[:, cols], 0.0, ALU.mult, ALU.add
                                             ).then_inc(s.scanned, 1)
            for t in range(NT):
                cols = slice(t * TILE, (t + 1) * TILE)
                dve.wait_ge(s.scanned, t // 2 + 1)
                dve.wait_ge(s.gate_ready, t + 1)
                nc.vector.tensor_tensor(Uv[:, cols], Uv[:, cols], GT[:, cols], ALU.mult).then_inc(s.gated, 1)

    rms_norm(k, 1, Uv, Hb, w("norm2"))
    feed_forward(k, 0, 0, Hb, FCH, lambda lo, n: w("mg", lo, n), lambda c, n: w("mg_b", c, 1),
                 lambda lo, n: w("mf", lo, n), lambda c, n: w("mf_b", c, 1),
                 lambda c, n: w("mo", c * P, P), w("mo_b"), S, S)


def rows_pipeline(eng, step, tail, slots):
    first = 6
    last = first + (B - 1 - first) // slots * slots
    for i in range(first):
        step(i, i % slots)
    with eng.Fori(first // slots, last // slots) as turn:
        for n in range(slots):
            step(turn * slots + n, n)
    for i in range(last, B + tail):
        step(i, i % slots)


def done(i, lag):
    return min(max(i - lag + 1, 0), B) if isinstance(i, int) else i - lag + 1


def live(i, lag):
    return not isinstance(i, int) or 0 <= i - lag < B


def placed(j, e):
    return 64 * (j // 2) + 32 * e, j % 2


LA_PRODUCTS = {3: 0, 4: 1, 5: 2, 6: 3}
LA_VALUE_LAG, LA_RING = 1, 2
LA_SCALED_FIRST = 2
LA_MAX_AT = 6
POOL_SCALED = [(1, 0, 0), (1, 1, 1), (1, 2, 0), (1, 3, 1), (0, 0, 0), (0, 1, 1)]


def local_attention(k, layer, w, rope, X0, Yd):
    nc, s, ps = k.nc, k.s, k.ps
    row0 = layer * B
    W65 = D64 + 1
    NS = 3
    NPOOL = len(POOL_SCALED)
    with ExitStack() as ctx:
        sb = lambda n, shape, dt=F32: ctx.enter_context(nc.sbuf_tensor(f"la{layer}_{n}", shape, dt))
        hs = sb("hs", [P, NS, L])
        tab = sb("tab", [P, 2, 4, L])
        QK = sb("qk", [P, NS, 2, 4, L])
        V = sb("v", [P, NS, 2, H8, W65])
        sq = sb("sq", [P, 2, 2 * L])
        sqs = sb("sqs", [P, 2, L])
        vc = sb("vc", [P, 4, L])
        rn = sb("rn", [P, 4, L])
        y2 = sb("y2", [P, 4, L])
        ta = sb("ta", [P, 2, 2 * L])
        tb = sb("tb", [P, 2, 2 * L])
        tc = sb("tc", [P, 2, 2, 2, L])
        nm = sb("nm", [P, 2, H8])
        nb = sb("nb", [P, 2, H8], BF16)
        m2 = sb("m2", [P, 2, P])
        mT = sb("mt", [P, NS, L], BF16)
        pr = sb("pr", [P, LA_RING, 320])
        rec = sb("rec", [P, 2, 2])
        ot = sb("ot", [P, 2, 4, P])
        oT = sb("oT", [P, 4, L])
        block = ctx.enter_context(nc.Block())

        def scaled(n, g, j, e):
            part, chunk = placed(j, e)
            src = slice(32 * j, 32 * j + 32)
            to = QK[part:part + 32, n, g, :, :].rearrange("p (c a) t -> p c a t", a=2)[:, :, chunk, :]
            return to, rn[src, 2 * g:2 * g + 2, :], tc[src, g, :, e, :]

        @block.gpsimd
        def _(pool):
            nc.gpsimd.memset(V[:, :, :, :, D64:W65], 1.0).then_inc(s.la_init, 1)
            nc.gpsimd.memset(m2[:], 0.0).then_inc(s.la_init, 1)
            pool.wait_ge(s.la_init, 3 * layer + 2)
            nc.gpsimd.memset(hs[64:128, :, 0:1], 0.0).then_inc(s.la_init, 1)
            pool.wait_ge(s.la_init, 3 * layer + 3)

            def step(i, n):
                b = row0 + i
                for x in range(H8):
                    if live(i, 0) and x == 0:
                        at_least(pool, s.la_vprod, 2 * (b - NS + 1) if live(i, NS) else 0)
                        nc.gpsimd.tensor_copy(hs[0:64, n, :], X0[0:64, bass.ds(i * L, L)]).then_inc(s.la_shifted, 1)
                        pool.wait_ge(s.la_shifted, 2 * b + 1)
                        nc.gpsimd.tensor_copy(hs[64:128, n, 1:L], X0[64:128, bass.ds(i * L, L - 1)]
                                              ).then_inc(s.la_shifted, 1)
                        pool.wait_ge(s.la_shifted, 2 * b + 2)
                    if live(i, 0) and x in LA_PRODUCTS:
                        p = LA_PRODUCTS[x]
                        pool.wait_ge(s.la_squared, 4 * b + p + 1)
                        at_least(pool, s.la_norm, 4 * b + p - 1)
                        nc.gpsimd.tensor_tensor(sqs[:, p % 2, :], sq[:, p % 2, 0:L], sq[:, p % 2, L:2 * L], ALU.add
                                                ).then_inc(s.la_sqsum, 1)
                        pool.wait_ge(s.la_sqsum, 4 * b + p + 1)
                    if live(i, 1) and x in (2, 3):
                        if x == 2:
                            pool.wait_ge(s.la_exact, b)
                            pool.wait_ge(s.la_rotated, 4 * b)
                            if live(i, 1 + NS):
                                at_least(pool, s.la_keyed, H8 * (b - NS))
                        first = (x - 2) * (NPOOL // 2)
                        for m in range(first, first + NPOOL // 2):
                            to, norm, src = scaled((n - 1) % NS, *POOL_SCALED[m])
                            nc.gpsimd.tensor_tensor(to, norm, src, ALU.mult).then_inc(s.la_qkp, 1)
                            pool.wait_ge(s.la_qkp, NPOOL * (b - 1) + m + 1)
                    if live(i, 0) and x in LA_PRODUCTS:
                        p = LA_PRODUCTS[x]
                        pool.wait_ge(s.la_rot, 4 * b + p + 1)
                        if p == 0:
                            at_least(pool, s.la_qk, b)
                        nc.gpsimd.tensor_tensor(tc[:, p // 2, p % 2, :, :].rearrange("p e t -> p (e t)"), ta[:, p % 2, :],
                                                tb[:, p % 2, :], ALU.add).then_inc(s.la_rotated, 1)
            rows_pipeline(pool, step, 4, NS)

        @block.tensor
        def _(pe):
            pe.wait_ge(s.la_init, 3 * (layer + 1))

            def product(i, n, p):
                u = 4 * (row0 + i) + p
                if p == 0:
                    pe.wait_ge(s.la_shifted, 2 * (row0 + i + 1))
                at_least(pe, s.la_rot, u - 1)
                weights = w("wq" if p < 2 else "wk", p % 2 * 2 * P, 2 * P)
                for e in range(2):
                    m = nc.tensor.matmul(ps[:, p % 2, e * L:(e + 1) * L], weights[:, e * P:(e + 1) * P], hs[:, n, :],
                                         start=True, stop=True)
                m.then_inc(s.la_product, 1)

            def norms(i, p):
                if p == 0:
                    at_least(pe, s.la_clamped, row0 + i)
                    at_least(pe, s.la_vread, 2 * (row0 + done(i, 1)))
                pe.wait_ge(s.la_sqsum, 4 * (row0 + i) + p + 1)
                nc.tensor.matmul(ps[:, 2 + p // 2, p % 2 * L:(p % 2 + 1) * L], k.cf("block32"), sqs[:, p % 2, :],
                                 start=True, stop=True).then_inc(s.la_norm, 1)

            def head(n, h):
                part, chunk = placed(h % 4, 0)
                at = h // 4 * 2 + chunk
                return QK[part:part + 64, n, 0, at, :], QK[part:part + 64, n, 1, at, :]

            def maxima(i, n, h):
                u = H8 * (row0 + i) + h
                if h == 0:
                    pe.wait_ge(s.la_qk, row0 + i + 1)
                    pe.wait_ge(s.la_qkp, NPOOL * (row0 + i + 1))
                at_least(pe, s.la_max, u)
                q, kk = head(n, h)
                nc.tensor.matmul(ps[:, 4, 0:128], q[:, 0:128], kk[:, 0:128], start=True, stop=False)
                nc.tensor.matmul(ps[:, 4, 0:128], k.cb("ident"), k.cb("local_q0"), start=False, stop=True)
                nc.tensor.matmul(ps[:, 4, 128:320], q[:, 128:256], kk[:, 64:256], start=True, stop=False)
                nc.tensor.matmul(ps[:, 4, 128:320], k.cb("ident"), k.cb("local_q1"), start=False, stop=True
                                 ).then_inc(s.la_score, 1)

            def keyed(i, n, h):
                u = H8 * (row0 + i) + h
                if h == 0:
                    pe.wait_ge(s.la_mt, row0 + i + 1)
                at_least(pe, s.la_prob, u)
                q, kk = head(n, h)
                sel = k.cb("sel", h * P, P)
                nc.tensor.matmul(ps[:, 5, 0:192], kk[:, 0:128], q[:, 0:192], start=True, stop=False)
                nc.tensor.matmul(ps[:, 5, 0:192], k.cb("ident"), k.cb("local_k0"), start=False, stop=False)
                nc.tensor.matmul(ps[:, 5, 0:192], sel, mT[:, n, 0:192], start=False, stop=True)
                nc.tensor.matmul(ps[:, 5, 192:320], kk[:, 128:256], q[:, 128:256], start=True, stop=False)
                nc.tensor.matmul(ps[:, 5, 192:320], k.cb("ident"), k.cb("local_k0", 0, P), start=False, stop=False)
                nc.tensor.matmul(ps[:, 5, 192:320], sel, mT[:, n, 128:256], start=False, stop=True).then_inc(s.la_keyed, 1)

            def values(i, n, h):
                u = H8 * (row0 + i) + h
                pe.wait_ge(s.la_prob, u + 1)
                if h == 0:
                    pe.wait_ge(s.la_vread, 2 * (row0 + i + 1))
                if h % 2 == 0:
                    at_least(pe, s.la_divided, 4 * (row0 + i) + h // 2)
                o0, o1 = (h % 2) * W65, (2 + h % 2) * W65
                p = pr[:, h % LA_RING, :]
                nc.tensor.matmul(ps[:, 7, o0:o0 + W65], p[:, 0:128], V[:, n, 0, h, :], start=True, stop=True)
                nc.tensor.matmul(ps[:, 7, o1:o1 + W65], p[:, 192:320], V[:, n, 1, h, :], start=True, stop=True)
                nc.tensor.matmul(ps[0:64, 7, o1:o1 + W65], p[:, 128:192], V[:, n, 0, h, :], start=False, stop=True,
                                 skip_group_check=True).then_inc(s.la_attended, 1)

            def bank6_read(i):
                at_least(pe, s.la_mt, row0 + done(i - 1, 2))
                at_least(pe, s.la_stored, row0 + done(i - 1, 4))

            def project_values(i, n):
                pe.wait_ge(s.la_clamped, row0 + i)
                for q in range(2):
                    nc.tensor.matmul(ps[:, 2 + q, :], hs[:, n, q * P:(q + 1) * P], w("wv"), start=True, stop=True
                                     ).then_inc(s.la_vprod, 1)

            def turn(i, half):
                b = row0 + i - 4
                pe.wait_ge(s.la_divided, 4 * b + 2 * (half + 1))
                bank6_read(i)
                at_least(pe, s.la_turned, 2 * b + half)
                pe.nop(nofuse=True)
                for c in range(2):
                    for q in range(2):
                        at = c * L + q * P
                        m = nc.tensor.transpose(ps[:, 6, at:at + P], ot[:, q, 2 * half + c, :], k.cf("identf"))
                m.then_inc(s.la_turn, 1)

            def output(i):
                pe.wait_ge(s.la_turned, 2 * (row0 + i - 3))
                for c in range(4):
                    m = nc.tensor.matmul(ps[:, 6, 0:L], w("wo", c * P, P), oT[:, c, :], start=(c == 0), stop=(c == 3))
                m.then_inc(s.la_out, 1)

            def shifts(i):
                pe.wait_ge(s.la_m2, 3 * (row0 + i - 1))
                at_least(pe, s.la_stored, row0 + done(i, 4))
                pe.nop(nofuse=True)
                for q in range(2):
                    m = nc.tensor.transpose(ps[:, 6, q * P:(q + 1) * P], m2[:, q, :], k.cf("identf"))
                m.then_inc(s.la_shift, 1)

            def step(i, n):
                for x in range(H8):
                    if live(i, 0) and x in LA_PRODUCTS:
                        product(i, n, LA_PRODUCTS[x])
                    row = 1 if x >= LA_MAX_AT else 2
                    if live(i, row):
                        maxima(i - row, (n - row) % NS, (x - LA_MAX_AT) % H8)
                    if live(i, 4) and x == 2:
                        turn(i, 0)
                    if live(i, 3):
                        keyed(i - 3, n, x)
                    row = 3 if x >= LA_VALUE_LAG else 4
                    if live(i, row):
                        values(i - row, (n - row) % NS, (x - LA_VALUE_LAG) % H8)
                    if live(i, 1) and x == 0:
                        project_values(i, (n - 1) % NS)
                    if live(i, 4) and x == 3:
                        turn(i, 1)
                    if live(i, 4) and x == 4:
                        output(i)
                    if live(i, 2) and x == 6:
                        shifts(i)
                    if live(i, 0) and x - 1 in LA_PRODUCTS:
                        norms(i, LA_PRODUCTS[x - 1])
            rows_pipeline(pe, step, 4, NS)

        @block.scalar
        def _(act):
            act.wait_ge(s.la_init, 3 * (layer + 1))

            def step(i, n):
                b = row0 + i
                for x in range(H8):
                    if live(i, 0) and x in LA_PRODUCTS:
                        p = LA_PRODUCTS[x]
                        act.wait_ge(s.la_product, 4 * b + p + 1)
                        at_least(act, s.la_sqsum, 4 * b + p - 1)
                        nc.scalar.activation(sq[:, p % 2, :], ps[:, p % 2, :], ACT.Square).then_inc(s.la_squared, 1)
                    if live(i, 3):
                        u = H8 * (b - 3) + x
                        act.wait_ge(s.la_keyed, u + 1)
                        at_least(act, s.la_attended, u - LA_RING + 1)
                        nc.scalar.activation(pr[:, x % LA_RING, :], ps[:, 5, 0:320], ACT.Exp, scale=8.0
                                             ).then_inc(s.la_prob, 1)
                    if live(i, 2) and x == 6:
                        act.wait_ge(s.la_shift, b - 1)
                        if live(i, 2 + NS):
                            at_least(act, s.la_keyed, H8 * (b - 1 - NS))
                        nc.scalar.copy(mT[:, (n - 2) % NS, :], ps[:, 6, 0:L]).then_inc(s.la_mt, 1)
                    if live(i, 1) and x == 0:
                        act.wait_ge(s.la_clamped, b)
                        at_least(act, s.la_qk, b - 1)
                        at_least(act, s.la_qkp, NPOOL * (b - 1))
                        nc.scalar.activation(rn[:], vc[:], ACT.Abs_reciprocal_sqrt).then_inc(s.la_rnorm, 1)
                        act.wait_ge(s.la_rnorm, b)
                        nc.scalar.activation(y2[:], rn[:], ACT.Square).then_inc(s.la_rnorm2, 1)
                    if live(i, 1) and x in (1, 2):
                        act.wait_ge(s.la_vprod, 2 * (b - 1) + x)
                        if live(i, 1 + NS):
                            at_least(act, s.la_attended, H8 * (b - NS))
                        nc.scalar.copy(V[:, (n - 1) % NS, x - 1, :, 0:D64], ps[:, 1 + x, :].rearrange("p (h d) -> p h d", d=D64)
                                       ).then_inc(s.la_vread, 1)
                    if live(i, 4) and x in (2, 3):
                        c = 2 * (x - 2)
                        act.wait_ge(s.la_turn, 2 * (b - 4) + x - 1)
                        at_least(act, s.la_out, b - 4)
                        nc.scalar.copy(oT[:, c:c + 2, :].rearrange("p c t -> p (c t)"), ps[:, 6, :]
                                       ).then_inc(s.la_turned, 1)
            rows_pipeline(act, step, 4, NS)

        @block.vector
        def _(dve):
            for g, (c, si, one, two) in enumerate((("qc", "qs", "q1", "q2"), ("kc", "ks", "k1", "k2"))):
                nc.vector.tensor_scalar(tab[:, g, 0, :], rope(c), w(one), None, ALU.mult)
                nc.vector.tensor_scalar(tab[:, g, 1, :], rope(c), w(two), None, ALU.mult)
                nc.vector.tensor_scalar(tab[:, g, 2, :], rope(si), w(two), -1.0, ALU.mult, ALU.mult)
                nc.vector.tensor_scalar(tab[:, g, 3, :], rope(si), w(one), None, ALU.mult).then_inc(s.la_table, 1)
            dve.wait_ge(s.la_table, 2 * (layer + 1))
            dve.wait_ge(s.la_init, 3 * (layer + 1))

            flat = lambda v: v.rearrange("p c t -> p (c t)")

            def rotate(i, p):
                u = 4 * (row0 + i) + p
                g = p // 2
                dve.wait_ge(s.la_squared, u + 1)
                at_least(dve, s.la_rotated, u - 1)
                nc.vector.tensor_tensor(ta[:, p % 2, :], ps[:, p % 2, :], flat(tab[:, g, 0:2, :]), ALU.mult)
                nc.vector.tensor_tensor(tb[:, p % 2, 0:L], ps[:, p % 2, L:2 * L], tab[:, g, 2, :], ALU.mult)
                nc.vector.tensor_tensor(tb[:, p % 2, L:2 * L], ps[:, p % 2, 0:L], tab[:, g, 3, :], ALU.mult
                                        ).then_inc(s.la_rot, 1)

            def divide(i, g):
                b = row0 + i
                dve.wait_ge(s.la_attended, H8 * b + 2 * (g + 1))
                out = ps[:, 7, 0:4 * W65].rearrange("p (q h c) -> p q h c", q=2, c=W65)
                nc.vector.reciprocal(rec[:], out[:, :, :, D64]).then_inc(s.la_rec, 1)
                at_least(dve, s.la_turn, 2 * b - 1 + g // 2)
                dve.wait_ge(s.la_rec, 4 * b + g + 1)
                nc.vector.tensor_tensor(ot[:, :, g, :].rearrange("p q (h d) -> p q h d", d=D64), out[:, :, :, 0:D64],
                                        rec[:].unsqueeze(3).to_broadcast([P, 2, 2, D64]), ALU.mult
                                        ).then_inc(s.la_divided, 1)

            own = [(g, j, e) for g in range(2) for j in range(4) for e in range(2) if (g, j, e) not in POOL_SCALED]

            def step(i, n):
                b = row0 + i
                for x in range(H8):
                    if live(i, 1) and x == 0:
                        dve.wait_ge(s.la_norm, 4 * b)
                        at_least(dve, s.la_vy2, b - 1)
                        nc.vector.tensor_scalar(flat(vc[:]), ps[:, 2:4, :].rearrange("p a t -> p (a t)"), 1e-24, None,
                                                ALU.max).then_inc(s.la_clamped, 1)
                    if live(i, 3) and x in (3, 5, 7):
                        divide(i - 3, (x - 3) // 2)
                    if live(i, 4) and x == 1:
                        divide(i - 4, 3)
                    if live(i, 4) and x == 5:
                        dve.wait_ge(s.la_out, b - 3)
                        nc.vector.tensor_tensor(Yd[:, bass.ds((i - 4) * L, L)], ps[:, 6, 0:L], X0[:, bass.ds((i - 4) * L, L)],
                                                ALU.add).then_inc(s.la_stored, 1)
                    row = 1 if x >= LA_MAX_AT else 2
                    h = (x - LA_MAX_AT) % H8
                    if live(i, row):
                        r = b - row
                        dve.wait_ge(s.la_score, H8 * r + h + 1)
                        if h == 0:
                            at_least(dve, s.la_m2, 3 * r)
                        nc.vector.tensor_reduce(nm[:, 0, h:h + 1], ps[:, 4, 0:128], AX.X, ALU.max, negate=True)
                        nc.vector.tensor_reduce(nm[:, 1, h:h + 1], ps[:, 4, 128:320], AX.X, ALU.max, negate=True
                                                ).then_inc(s.la_max, 1)
                        if h == H8 - 1:
                            dve.wait_ge(s.la_max, H8 * (r + 1))
                            nc.vector.tensor_copy(nb[:], nm[:]).then_inc(s.la_m2, 1)
                            dve.wait_ge(s.la_m2, 3 * r + 1)
                            at_least(dve, s.la_shift, r)
                            nc.vector.tensor_copy(m2[:, :, 0:H8], nb[:]).then_inc(s.la_m2, 1)
                            nc.vector.tensor_tensor(m2[:, :, 32:32 + H8], nm[:], nb[:], ALU.subtract).then_inc(s.la_m2, 1)
                    if live(i, 0) and x in LA_PRODUCTS:
                        rotate(i, LA_PRODUCTS[x])
                    if live(i, 1) and x == 1:
                        dve.wait_ge(s.la_rnorm2, b)
                        nc.vector.tensor_tensor(flat(y2[:]), flat(vc[:]), flat(y2[:]), ALU.mult).then_inc(s.la_vy2, 1)
                        dve.wait_ge(s.la_vy2, b)
                        nc.vector.scalar_tensor_tensor(out=flat(rn[:]), in0=flat(y2[:]), scalar=-3.0, in1=flat(rn[:]),
                                                       op0=ALU.add, op1=ALU.mult).then_inc(s.la_exact, 1)
                    if live(i, 1) and x in (2, 3):
                        half = own[:LA_SCALED_FIRST] if x == 2 else own[LA_SCALED_FIRST:]
                        if x == 2:
                            dve.wait_ge(s.la_exact, b)
                            dve.wait_ge(s.la_rotated, 4 * b)
                            if live(i, 1 + NS):
                                at_least(dve, s.la_keyed, H8 * (b - NS))
                        for g, j, e in half:
                            to, norm, src = scaled((n - 1) % NS, g, j, e)
                            m = nc.vector.tensor_tensor(to, norm, src, ALU.mult)
                        if x == 3:
                            m.then_inc(s.la_qk, 1)
            rows_pipeline(dve, step, 4, NS)


def attention(k, call, slots, stack_dt, scale, rounds, value_from, value_w, out_w, out_b, make):
    nc, s, ps = k.nc, k.s, k.ps
    row0 = call * B
    key_lag, value_lag, ring = LAGS if slots > 2 else LAGS_WIDE
    rd0 = k.rounds
    sd0 = k.stack_dmas
    with ExitStack() as ctx:
        sb = lambda n, shape, dt=F32: ctx.enter_context(nc.sbuf_tensor(f"at{call}_{n}", shape, dt))
        a = Core()
        a.value_from = value_from
        a.row0, a.rd0, a.slots = row0, rd0, slots
        a.value_row = 1 if slots > 2 else 2
        xv = sb("xv", [a.value_from[0], slots, L])
        a.Qs = sb("qs", [P, slots, H16 * L], stack_dt)
        a.Ks = sb("ks", [P, slots, H16 * L], stack_dt)
        V = sb("v", [P, slots, 2, 2, 8 * GW + GW])
        nm = sb("nm", [P, 2, H16])
        nb = sb("nb", [P, 2, H16], BF16)
        m2 = sb("m2", [P, 2, P])
        mT = sb("mt", [P, slots, L], BF16)
        pr = sb("pr", [P, ring, 384])
        raw = sb("raw", [P, 2 * L])
        sums = sb("sums", [P, L])
        oT = sb("oT", [P, L])

        def heads(n, q, parity, half):
            lo = 4 * GW * parity + GW // 2 * half
            return V[:, n, q, :, lo:lo + 4 * (GW + D8)].rearrange("p g (j c) -> p g j c", c=GW + D8)[:, :, :, 0:D8]
        make(a, sb)
        quarters = a.load_groups
        hq = H16 // quarters
        nst = len(a.stack_loads(0, 0)) * quarters
        k.rounds += rounds * B
        k.stack_dmas += nst * B
        block = ctx.enter_context(nc.Block())

        @block.sync
        def _(sp):
            a.load_constant_rows(sp)
            sp.wait_ge(s.at_zeroed, 2 * (call + 1))
            a.fill_constant_rows(sp)

            def step(i, n):
                def load(g):
                    r, nr = i - a.load_row, (n - a.load_row) % slots
                    b = row0 + r
                    if not live(i, a.load_row):
                        return
                    if g == 0:
                        sp.wait_ge(s.at_scratch, 32 * (b + 1))
                        sp.nop(nofuse=True)
                    at_least(sp, s.at_stacked, 16 * (sd0 + nst * r + nst // quarters * g))
                    sp.nop(nofuse=True)
                    if live(i, a.load_row + slots):
                        at_least(sp, s.at_keyed, H16 * (b - slots) + hq * (g + 1))
                        sp.nop(nofuse=True)
                    for dst, src in a.stack_loads(nr, g):
                        sp.dma_start(dst, src).then_inc(s.at_stacked, 16)

                for g in range(quarters // 2):
                    load(g)
                if live(i, 0):
                    a.wait_parts(sp, i)
                    sp.nop(nofuse=True)
                    if live(i, slots):
                        at_least(sp, s.at_stacked, 16 * (sd0 + nst * (i - slots + 1)))
                        sp.nop(nofuse=True)
                    for dst, src in a.scratch_stores(n):
                        sp.dma_start(dst, src).then_inc(s.at_scratch, 16)
                for g in range(quarters // 2, quarters):
                    load(g)
            rows_pipeline(sp, step, 4, slots)

        @block.gpsimd
        def _(pool):
            nc.gpsimd.memset(a.Ks[:], 0.0).then_inc(s.at_zeroed, 1)
            nc.gpsimd.memset(V[:], 0.0).then_inc(s.at_init, 1)
            nc.gpsimd.memset(m2[:], 0.0).then_inc(s.at_init, 1)
            pool.wait_ge(s.at_init, 3 * call + 2)
            for n in range(slots):
                for q in range(2):
                    for parity in range(2):
                        m = nc.gpsimd.memset(heads(n, q, parity, 1 - parity), 1.0)
            m.then_inc(s.at_init, 1)

            def step(i, n):
                b = row0 + i
                for x in range(H16):
                    if live(i, 0):
                        a.pool_round(pool, i, n, x)
                    if live(i, 4) and x == value_lag + 4:
                        pool.wait_ge(s.at_rec, b - 3)
                        at_least(pool, s.at_out, b - 4)
                        for g in range(4):
                            r = slice(32 * g, 32 * g + 32)
                            nc.gpsimd.tensor_tensor(oT[r, :], raw[r, g % 2 * L:(g % 2 + 1) * L], sums[r, :], ALU.mult
                                                    ).then_inc(s.at_divided, 1)
                            pool.wait_ge(s.at_divided, 4 * (b - 4) + g + 1)
                r = i + 1 - a.value_row
                if live(i, a.value_row - 1):
                    if live(i, a.value_row - 1 + slots):
                        at_least(pool, s.at_vprod, row0 + r - slots + 1)
                    nc.gpsimd.tensor_copy(xv[:, (n + 1 - a.value_row) % slots, :],
                                          value_from[1][0:value_from[0], bass.ds(r * L, L)]).then_inc(s.at_fetched, 1)
            rows_pipeline(pool, step, 4, slots)

        @block.tensor
        def _(pe):
            def product(i, n, r):
                before = r - 2 if r >= 2 else rounds - 1 - (rounds - 1 - r) % 2 - rounds
                at_least(pe, s.at_used, rd0 + rounds * i + before + 1)
                a.product(i, n, r).then_inc(s.at_product, 1)

            def shifts(i):
                pe.wait_ge(s.at_m2, 3 * (row0 + i - 2))
                at_least(pe, s.at_vread, row0 + done(i - 1, a.value_row))
                at_least(pe, s.at_stored, row0 + done(i - 1, 4))
                pe.nop(nofuse=True)
                for q in range(2):
                    m = nc.tensor.transpose(ps[:, 1, q * P:(q + 1) * P], m2[:, q, :], k.cf("identf"))
                m.then_inc(s.at_shift, 1)

            def value_rows(i, n):
                pe.wait_ge(s.at_fetched, row0 + done(i, a.value_row))
                at_least(pe, s.at_mt, row0 + done(i, 3))
                pe.nop(nofuse=True)
                for q in range(2):
                    m = nc.tensor.matmul(ps[:, 1, q * P:(q + 1) * P], xv[:, n, q * P:(q + 1) * P], value_w,
                                         start=True, stop=True)
                m.then_inc(s.at_vprod, 1)

            def output(i):
                pe.wait_ge(s.at_divided, 4 * (row0 + i - 3))
                at_least(pe, s.at_vread, row0 + done(i, a.value_row))
                at_least(pe, s.at_mt, row0 + done(i, 3))
                at_least(pe, s.at_stored, row0 + done(i - 1, 4))
                nc.tensor.matmul(ps[:, 1, 0:L], out_w, oT[:], start=True, stop=True).then_inc(s.at_out, 1)

            def maxima(i, n, h):
                u = H16 * (row0 + i) + h
                if h % hq == 0:
                    pe.wait_ge(s.at_stacked, 16 * (sd0 + nst * i + nst // quarters * (h // hq + 1)))
                at_least(pe, s.at_max, u - 1)
                q, kk = a.Qs[:, n, h * L:(h + 1) * L], a.Ks[:, n, h * L:(h + 1) * L]
                o = ps[:, 2 + h % 2, :]
                nc.tensor.matmul(o[:, 0:128], q[:, 0:128], kk[:, 0:128], start=True, stop=False)
                nc.tensor.matmul(o[:, 0:128], k.cb("ident"), k.cb("causal_q"), start=False, stop=True)
                nc.tensor.matmul(o[:, 128:384], q[:, 128:256], kk[:, 0:256], start=True, stop=False)
                nc.tensor.matmul(o[:, 256:384], k.cb("ident"), k.cb("causal_q"), start=False, stop=True
                                 ).then_inc(s.at_score, 1)

            def keyed(i, n, h):
                u = H16 * (row0 + i) + h
                if h == 0:
                    pe.wait_ge(s.at_mt, row0 + i + 1)
                at_least(pe, s.at_prob, u - 1)
                q, kk = a.Qs[:, n, h * L:(h + 1) * L], a.Ks[:, n, h * L:(h + 1) * L]
                o = ps[:, 4 + h % 2, :]
                sel = k.cb("sel", h * P, P)
                nc.tensor.matmul(o[:, 0:256], kk[:, 0:128], q[:, 0:256], start=True, stop=False)
                nc.tensor.matmul(o[:, 0:128], k.cb("ident"), k.cb("causal_k"), start=False, stop=False)
                nc.tensor.matmul(o[:, 0:256], sel, mT[:, n, 0:256], start=False, stop=True)
                nc.tensor.matmul(o[:, 256:384], kk[:, 128:256], q[:, 128:256], start=True, stop=False)
                nc.tensor.matmul(o[:, 256:384], k.cb("ident"), k.cb("causal_k"), start=False, stop=False)
                nc.tensor.matmul(o[:, 256:384], sel, mT[:, n, 128:256], start=False, stop=True).then_inc(s.at_keyed, 1)

            def values(i, n, h):
                pe.wait_ge(s.at_prob, H16 * (row0 + i) + h + 1)
                if h % 8 == 0:
                    at_least(pe, s.at_raw, 2 * (row0 + i) - 1 + h // 8)
                if h == 0:
                    pe.wait_ge(s.at_vread, row0 + i + 1)
                g, j = h // 4, h % 4
                lo, row = 4 * GW * (g % 2) + GW * j, GW * (g // 2)
                o = ps[row:row + GW, 7, g % 2 * L:(g % 2 + 1) * L]
                w = pr[:, h % ring, :]
                nc.tensor.matmul(o, V[:, n, 0, g // 2, lo:lo + GW], w[:, 0:L], start=(j == 0), stop=False)
                nc.tensor.matmul(o[:, P:L], V[:, n, 1, g // 2, lo:lo + GW], w[:, L:L + P], start=False, stop=(j == 3)
                                 ).then_inc(s.at_attended, 1)

            def step(i, n):
                for x in range(H16):
                    if live(i, 0) and x % ROUND == 0 and x // ROUND < rounds:
                        product(i, n, x // ROUND)
                    if live(i, 3) and x == 1:
                        shifts(i)
                    if live(i, 2):
                        maxima(i - 2, (n - 2) % slots, x)
                    for stage, lag in ((keyed, key_lag), (values, value_lag)):
                        row = 3 + (x < lag)
                        if live(i, row):
                            stage(i - row, (n - row) % slots, (x - lag) % H16)
                    if live(i, a.value_row) and x == 7:
                        value_rows(i, (n - a.value_row) % slots)
                    if live(i, 4) and x == 14:
                        output(i)
            rows_pipeline(pe, step, 4, slots)

        @block.scalar
        def _(act):
            a.act_init(act)

            def step(i, n):
                b = row0 + i
                for x in range(H16):
                    for half, at, row in ((0, value_lag + 8, 3), (1, value_lag, 4)):
                        if live(i, row) and x == at:
                            act.wait_ge(s.at_attended, H16 * (b - row) + 8 * (half + 1))
                            at_least(act, s.at_divided, 4 * (b - row))
                            r = slice(64 * half, 64 * half + 64)
                            nc.scalar.copy(raw[r, :], ps[r, 7, :]).then_inc(s.at_raw, 1)
                    row = 3 + (x < key_lag)
                    if live(i, row):
                        h = (x - key_lag) % H16
                        u = H16 * (b - row) + h
                        act.wait_ge(s.at_keyed, u + 1)
                        at_least(act, s.at_attended, u - ring + 1)
                        nc.scalar.activation(pr[:, h % ring, :], ps[:, 4 + h % 2, 0:384], ACT.Exp, scale=scale
                                             ).then_inc(s.at_prob, 1)
                    if live(i, 0):
                        a.act_round(act, i, n, x)
                    if live(i, 3) and x == 1:
                        act.wait_ge(s.at_shift, b - 2)
                        if live(i, 3 + slots):
                            at_least(act, s.at_keyed, H16 * (b - 2 - slots))
                        nc.scalar.copy(mT[:, (n - 3) % slots, :], ps[:, 1, 0:L]).then_inc(s.at_mt, 1)
                    if live(i, 4) and x == value_lag + 1:
                        act.wait_ge(s.at_raw, 2 * (b - 3))
                        for g in range(4):
                            r = g // 2 * GW + GW // 2 * (1 - g % 2)
                            m = nc.scalar.copy(sums[32 * g:32 * g + 32, :], raw[r:r + 32, g % 2 * L:(g % 2 + 1) * L])
                        m.then_inc(s.at_sums, 1)
                    if live(i, a.value_row) and x == 9:
                        if isinstance(i, int) and i == a.value_row:
                            act.wait_ge(s.at_init, 3 * (call + 1))
                        act.wait_ge(s.at_vprod, b + 1 - a.value_row)
                        if live(i, a.value_row + slots):
                            at_least(act, s.at_attended, H16 * (b + 1 - a.value_row - slots))
                        for q in range(2):
                            made = ps[:, 1, q * P:(q + 1) * P].rearrange("p (g r j d) -> p g r j d", r=2, j=4, d=D8)
                            for parity in range(2):
                                m = nc.scalar.copy(heads((n - a.value_row) % slots, q, parity, parity), made[:, :, parity])
                        m.then_inc(s.at_vread, 1)
            rows_pipeline(act, step, 4, slots)

        @block.vector
        def _(dve):
            nc.vector.memset(a.Qs[:], 0.0).then_inc(s.at_zeroed, 1)

            def step(i, n):
                b = row0 + i
                for x in range(H16):
                    if live(i, 2):
                        dve.wait_ge(s.at_score, H16 * (b - 2) + x + 1)
                        if x == 0:
                            at_least(dve, s.at_m2, 3 * (b - 2))
                        nc.vector.tensor_reduce(nm[:, 0, x:x + 1], ps[:, 2 + x % 2, 0:128], AX.X, ALU.max, negate=True)
                        nc.vector.tensor_reduce(nm[:, 1, x:x + 1], ps[:, 2 + x % 2, 128:384], AX.X, ALU.max,
                                                negate=True).then_inc(s.at_max, 1)
                    if live(i, 0):
                        a.vector_round(dve, i, n, x)
                    if live(i, 4) and x == value_lag + 3:
                        dve.wait_ge(s.at_sums, b - 3)
                        nc.vector.reciprocal(sums[:], sums[:]).then_inc(s.at_rec, 1)
                    if live(i, 4) and x == 15:
                        dve.wait_ge(s.at_out, b - 3)
                        to = k.S[:, bass.ds((i - 4) * L, L)]
                        if out_b is None:
                            m = nc.vector.tensor_copy(to, ps[:, 1, 0:L])
                        else:
                            m = nc.vector.tensor_scalar(to, ps[:, 1, 0:L], out_b, None, ALU.add)
                        m.then_inc(s.at_stored, 1)
                if isinstance(i, int) and i == 2:
                    dve.wait_ge(s.at_init, 3 * (call + 1))
                if live(i, 2):
                    c = 3 * (b - 2)
                    dve.wait_ge(s.at_max, H16 * (b - 1))
                    nc.vector.tensor_copy(nb[:], nm[:]).then_inc(s.at_m2, 1)
                    dve.wait_ge(s.at_m2, c + 1)
                    at_least(dve, s.at_shift, b - 2)
                    nc.vector.tensor_copy(m2[:, :, 0:H16], nb[:]).then_inc(s.at_m2, 1)
                    nc.vector.tensor_tensor(m2[:, :, 32:48], nm[:], nb[:], ALU.subtract).then_inc(s.at_m2, 1)
            rows_pipeline(dve, step, 4, slots)


def nothing(*_):
    pass


def split_stacks(k, a, sb, name):
    nc, s = k.nc, k.s
    a.parts = sb("parts", [P, 3, 2 * L], BF16)
    a.res = sb("res", [P, 2 * L])
    scr = nc.dram_tensor(f"scratch_{name}", (a.slots, 2, 3, P, L), BF16)
    a.load_groups, a.load_row = 1, 0

    def scratch_stores(n):
        return [(scr[n, j].rearrange("s p t -> p s t"), a.parts[:, :, j * L:(j + 1) * L]) for j in range(2)]

    def stack_loads(n, g):
        q, kk = (scr[n, j].rearrange("s (d h) t -> (s d) (h t)", h=H16) for j in range(2))
        return ([(a.Qs[0:24, n, :], q[0:24]), (a.Qs[24:40, n, :], q[0:16]), (a.Qs[40:48, n, :], q[0:8])]
                + [(a.Ks[8 * j:8 * j + 8, n, :], kk[0:8]) for j in range(3)]
                + [(a.Ks[24 + 8 * j:32 + 8 * j, n, :], kk[8:16]) for j in range(2)]
                + [(a.Ks[40:48, n, :], kk[16:24])])
    a.scratch_stores, a.stack_loads = scratch_stores, stack_loads
    a.wait_parts = lambda sp, i: sp.wait_ge(s.at_parts, a.row0 + i + 1)

    def leading(act, i, src):
        at_least(act, s.at_scratch, 32 * (a.row0 + i))
        nc.scalar.copy(a.parts[:, 0, :], src).then_inc(s.at_hi, 1)

    def rest(dve, i, src):
        dve.wait_ge(s.at_hi, a.row0 + i + 1)
        at_least(dve, s.at_parts, a.row0 + i)
        return nc.vector.tensor_tensor(a.res[:], src, a.parts[:, 0, :], ALU.subtract)

    def middle(act, i):
        act.wait_ge(s.at_res, a.row0 + i + 1)
        nc.scalar.copy(a.parts[:, 1, :], a.res[:]).then_inc(s.at_mid, 1)

    def last(pool, i):
        pool.wait_ge(s.at_mid, a.row0 + i + 1)
        nc.gpsimd.tensor_tensor(a.parts[:, 2, :], a.res[:], a.parts[:, 1, :], ALU.subtract).then_inc(s.at_parts, 1)
    a.leading, a.rest, a.middle, a.last = leading, rest, middle, last


def alibi_attention(k, w, alibi):
    nc, s, ps = k.nc, k.s, k.ps

    def make(a, sb):
        split_stacks(k, a, sb, "alibi")
        half = H16 * L // 2
        rows16 = sb("alibi", [P, half], BF16)
        parts = [(j, c, slice(32 * j + 64 * c, 32 * j + 64 * c + 6)) for j in range(2) for c in range(2)]
        a.pool_round = lambda pool, i, n, x: a.last(pool, i) if x == 6 else None

        def load(sp):
            for j, c, r in parts:
                sp.dma_start(k.Y[r, 0:half], alibi[j][:, c * half:(c + 1) * half]).then_inc(s.alibi_loaded, 16)
        a.load_constant_rows = load

        def fill(sp):
            sp.wait_ge(s.alibi_cast, 1)
            for j, c, r in parts:
                sp.dma_start((a.Qs, a.Ks)[j][48:54, :, c * half:(c + 1) * half],
                             rows16[r, :].unsqueeze(1).to_broadcast([6, a.slots, half])).then_inc(s.alibi_rows, 16)
            sp.wait_ge(s.alibi_rows, 64)
        a.fill_constant_rows = fill

        def cast(act):
            act.wait_ge(s.alibi_loaded, 64)
            nc.scalar.copy(rows16[:], k.Y[:, 0:half]).then_inc(s.alibi_cast, 1)
        a.act_init = cast

        def product(i, n, r):
            nc.tensor.matmul(ps[:, 0, 0:L], w("wq"), k.XN[:, bass.ds(i * L, L)], start=True, stop=True)
            return nc.tensor.matmul(ps[:, 0, L:2 * L], w("wk"), k.XN[:, bass.ds(i * L, L)], start=True, stop=True)
        a.product = product

        def act_round(act, i, n, x):
            if x == 2:
                act.wait_ge(s.at_product, a.rd0 + i + 1)
                a.leading(act, i, ps[:, 0, :])
            if x == 5:
                a.middle(act, i)
        a.act_round = act_round

        def vector_round(dve, i, n, x):
            if x == 3:
                a.rest(dve, i, ps[:, 0, :]).then_inc(s.at_res, 1)
                dve.wait_ge(s.at_res, a.row0 + i + 1)
                nc.vector.sem_inc(s.at_used, 1)
        a.vector_round = vector_round

    attention(k, 0, 3, BF16, float(1 / np.sqrt(8.0)), 1, (P, k.XN), w("wv"), w("wo"), None, make)


def rope8_attention(k, w, fold):
    nc, s, ps = k.nc, k.s, k.ps

    def make(a, sb):
        split_stacks(k, a, sb, "rope8")
        ta, tb, tq = sb("ta", [P, 2, L]), sb("tb", [P, 2, L]), sb("tq", [P, 2, L])
        a.load_constant_rows = a.fill_constant_rows = a.act_init = nothing

        def product(i, n, r):
            nc.tensor.matmul(ps[:, 6 * r, 0:L], fold[:, 2 * r, :], k.XN[:, bass.ds(i * L, L)], start=True, stop=True)
            return nc.tensor.matmul(ps[:, 6 * r, L:2 * L], fold[:, 2 * r + 1, :], k.XN[:, bass.ds(i * L, L)], start=True, stop=True)
        a.product = product

        def vector_round(dve, i, n, x):
            if x in (1, ROUND + 1):
                r = x // ROUND
                dve.wait_ge(s.at_product, a.rd0 + 2 * i + r + 1)
                at_least(dve, s.at_sum, 2 * i + r - 1)
                nc.vector.tensor_tensor(ta[:, r, :], ps[:, 6 * r, 0:L], w("cos"), ALU.mult)
                nc.vector.tensor_tensor(tb[:, r, :], ps[:, 6 * r, L:2 * L], w("sin"), ALU.mult).then_inc(s.at_used, 1)
            if x == 9:
                a.rest(dve, i, tq[:].rearrange("p a t -> p (a t)")).then_inc(s.at_res, 1)
        a.vector_round = vector_round

        def pool_round(pool, i, n, x):
            if x in (2, ROUND + 2):
                r = x // ROUND
                pool.wait_ge(s.at_used, a.rd0 + 2 * i + r + 1)
                at_least(pool, s.at_res, a.row0 + i)
                nc.gpsimd.tensor_tensor(tq[:, r, :], ta[:, r, :], tb[:, r, :], ALU.add).then_inc(s.at_sum, 1)
            if x == 11:
                a.last(pool, i)
        a.pool_round = pool_round

        def act_round(act, i, n, x):
            if x == 8:
                act.wait_ge(s.at_sum, 2 * i + 2)
                a.leading(act, i, tq[:].rearrange("p a t -> p (a t)"))
            if x == 11:
                a.middle(act, i)
        a.act_round = act_round

    attention(k, 1, 3, BF16, float(D8 ** -0.5), 2, (P, k.XN), fold[:, 4, :], w("wo"), w("bo"), make)


def latent_attention(k, w, fold, kvn):
    nc, s, ps = k.nc, k.s, k.ps

    def make(a, sb):
        ta, tb = sb("ta", [P, 2, 2 * L]), sb("tb", [P, 2, 2 * L])
        qk = sb("parts", [P, 2, 5, L])
        scr = nc.dram_tensor("scratch_latent", (a.slots, 2, 5 * P, L), F32)
        a.load_groups, a.load_row = 4, 1

        def scratch_stores(n):
            return [(scr[n, j].rearrange("(c p) t -> p c t", p=P), qk[:, j, :, :]) for j in range(2)]

        def stack_loads(n, g):
            cols = slice(g * H16 // a.load_groups * L, (g + 1) * H16 // a.load_groups * L)
            return [(st[0:5 * P // H16, n, cols], scr[n, j].rearrange("(d h) t -> d (h t)", h=H16)[:, cols])
                    for j, st in enumerate((a.Qs, a.Ks))]
        a.scratch_stores, a.stack_loads = scratch_stores, stack_loads
        a.load_constant_rows = a.fill_constant_rows = a.act_init = nothing

        def wait_parts(sp, i):
            sp.wait_ge(s.at_content, i + 1)
            sp.nop(nofuse=True)
            sp.wait_ge(s.at_sum, 2 * B + 4 * (i + 1))
        a.wait_parts = wait_parts

        def product(i, n, r):
            x = k.XN[:, bass.ds(i * L, L)]
            if r == 0:
                nc.tensor.matmul(ps[:, 0, 0:L], fold[:, 0:P], x, start=True, stop=True)
                return nc.tensor.matmul(ps[:, 0, L:2 * L], w("kd", rows=32), kvn[0:32, bass.ds(i * L, L)], start=True, stop=True)
            c = (r - 1) % 2
            src = fold[:, P:5 * P] if r < 3 else w("kr")
            nc.tensor.matmul(ps[:, r % 2 * 6, 0:L], src[:, c * P:(c + 1) * P], x, start=True, stop=True)
            return nc.tensor.matmul(ps[:, r % 2 * 6, L:2 * L], src[:, (c + 2) * P:(c + 3) * P], x, start=True, stop=True)
        a.product = product

        def act_round(act, i, n, x):
            if x == 1:
                act.wait_ge(s.at_product, a.rd0 + 5 * i + 1)
                at_least(act, s.at_scratch, 32 * (a.row0 + i))
                nc.scalar.copy(qk[:, :, 0, :], ps[:, 0, :].rearrange("p (a t) -> p a t", a=2)).then_inc(s.at_content, 1)
        a.act_round = act_round

        def vector_round(dve, i, n, x):
            p = x // ROUND
            if x == 2:
                dve.wait_ge(s.at_content, i + 1)
                nc.vector.sem_inc(s.at_used, 1)
            if x % ROUND == 1 and 1 <= p < 5:
                c, e = (p - 1) % 2, p % 2
                dve.wait_ge(s.at_product, a.rd0 + 5 * i + p + 1)
                at_least(dve, s.at_sum, 2 * B + 4 * i + p - 2)
                two = ps[:, 6 * e, :].rearrange("p (a t) -> p a t", a=2)
                sin = w("sin", c * 2 * L, 2 * L)
                nc.vector.tensor_tensor(ta[:, e, :], ps[:, 6 * e, :], w("cos", c * 2 * L, 2 * L), ALU.mult)
                nc.vector.tensor_tensor(tb[:, e, 0:L], two[:, 1, :], sin[:, 0:L], ALU.mult)
                nc.vector.tensor_tensor(tb[:, e, L:2 * L], two[:, 0, :], sin[:, L:2 * L], ALU.mult).then_inc(s.at_used, 1)
        a.vector_round = vector_round

        def pool_round(pool, i, n, x):
            p = x // ROUND
            if x % ROUND == 2 and 1 <= p < 5:
                c, e = (p - 1) % 2, p % 2
                pool.wait_ge(s.at_used, a.rd0 + 5 * i + p + 1)
                if p == 1:
                    at_least(pool, s.at_scratch, 32 * (a.row0 + i))
                nc.gpsimd.tensor_tensor(qk[:, (p - 1) // 2, 1 + c:4 + c:2, :], ta[:, e, :].rearrange("p (a t) -> p a t", a=2),
                                        tb[:, e, :].rearrange("p (a t) -> p a t", a=2), ALU.add).then_inc(s.at_sum, 1)
        a.pool_round = pool_round

    attention(k, 2, 2, F32, float(40.0 ** -0.5), 5, (32, kvn), w("vd", rows=32), w("wo"), None, make)


def experts(k, wgate, weights, both):
    nc, s, ps = k.nc, k.s, k.ps
    NCH = N // P
    XT = NCH + NEXP - 1
    XN = k.XN
    tokens = k.Y
    sorted_in = nc.dram_tensor("experts_in", (XT * P, P), F32).ap()
    sorted_out = nc.dram_tensor("experts_out", (XT * P, P), F32).ap()
    by_tile = lambda dram, lo, hi: dram[lo * P:hi * P, :].rearrange("(t p) d -> p t d", p=P)
    with ExitStack() as ctx:
        sb = lambda n, shape, dt=F32: ctx.enter_context(nc.sbuf_tensor(f"moe_{n}", shape, dt))
        bias = sb("bias", [P, W_MOEB[1]])
        wb = pack(bias, W_MOEB[0])
        both_w = sb("weights", [P, W_MOE[1]])
        w = pack(both_w, W_MOE[0])
        xs = sb("xs", [P, XT, P])
        ys = sb("ys", [P, XT, P])
        scores = sb("scores", [NEXP, N])
        gs = sb("gs", [P, NCH, NEXP])
        best = sb("best", [P, NCH])
        pick = sb("pick", [P, NCH])
        at = sb("at", [P, NCH, NEXP])
        hot = sb("hot", [P, NCH, NEXP])
        io = sb("io", [P, NEXP])
        count_i = sb("counti", [P, XT], I32)
        count = sb("count", [P, XT])
        go_on = sb("goon", [P, NEXP, NCH])
        total = sb("total", [P, NEXP, NCH])
        upto = sb("upto", [P, NEXP, NCH])
        more = sb("more", [P, NEXP, NCH])
        tiles = sb("tiles", [P, NEXP])
        end = sb("end", [P, NEXP])
        begin = sb("begin", [P, NEXP])
        ended = sb("ended", [1, XT, NEXP])
        expert = sb("expert", [1, XT])
        expert_i = sb("experti", [1, XT], I32)
        place = sb("place", [P, NCH, NEXP])
        placed_at = sb("placedat", [P, NCH])
        place_i = sb("placei", [P, NCH], U32)
        xin = sb("xin", [P, 2, P])
        xT = sb("xt", [P, 2, P])
        hr = sb("hr", [P, 2, EH])
        hT = sb("ht", [P, 2, EH])

        with nc.Block() as block:
            @block.sync
            def _(sp):
                sp.wait_ge(s.moe_init, 2)
                sp.dma_start(by_tile(sorted_in, 0, XT), ys[:]).then_inc(s.moe_cleared, 16)
                sp.dma_start(both_w[:], weights).then_inc(s.load_moe, 16)
                sp.dma_start(bias[:], both).then_inc(s.load_moe, 16)
                sp.wait_ge(s.load_moe, 32)

            @block.gpsimd
            def _(pool):
                nc.gpsimd.iota(count_i[:], [[1, XT]], base=0, channel_multiplier=0).then_inc(s.moe_iota, 1)
                for e in range(NEXP):
                    m = nc.gpsimd.memset(io[:, e:e + 1], float(e))
                m.then_inc(s.moe_iota, 1)
                nc.gpsimd.memset(go_on[:], 1.0).then_inc(s.moe_init, 1)
                nc.gpsimd.memset(ys[:], 0.0).then_inc(s.moe_init, 1)
                pool.wait_ge(s.moe_init, 1)
                nc.gpsimd.memset(go_on[:, :, 0:1], 0.0).then_inc(s.moe_iota, 1)
                pool.wait_ge(s.moe_place, 1)
                pool.wait_ge(s.moe_tokens, NT)
                pool.wait_ge(s.moe_cleared, 16)
                for c in range(NCH):
                    nc.gpsimd.indirect_dma_start(sorted_in, bass.IndirectOffsetOnAxis(place_i[:, c:c + 1], 0),
                                                 tokens[:, c * P:(c + 1) * P], None).then_inc(s.moe_scattered, 16)
                pool.wait_ge(s.moe_scattered, 16 * NCH)

            @block.tensor
            def _(pe):
                for t in range(NT):
                    nc.tensor.matmul(ps[0:NEXP, t, :], wgate("wg"), XN[:, t * TILE:(t + 1) * TILE], start=True, stop=True
                                     ).then_inc(s.moe_gate, 1)
                pe.wait_ge(s.moe_scored, NT)
                for c in range(NCH):
                    m = nc.tensor.transpose(ps[:, 0, c * NEXP:(c + 1) * NEXP], scores[:, c * P:(c + 1) * P],
                                            k.cf("identf", n=NEXP, rows=NEXP))
                m.then_inc(s.moe_scores, 1)
                for t in range(NT):
                    if t == 7:
                        pe.wait_ge(s.moe_tokens, 1)
                    for q in range(4):
                        at_ = t * TILE + q * P
                        m = nc.tensor.transpose(ps[:, 1 + t % 7, q * P:(q + 1) * P], XN[:, at_:at_ + P], k.cf("identf"))
                    m.then_inc(s.moe_back, 1)
                pe.wait_ge(s.moe_hot, 5)
                flat = hot[:].rearrange("p c e -> p (c e)")
                n = NCH * NEXP
                nc.tensor.matmul(ps[:, 0, 0:n], k.cf("mean"), flat, start=True, stop=True)
                nc.tensor.matmul(ps[:, 0, n:2 * n], k.cf("before"), flat, start=True, stop=True
                                 ).then_inc(s.moe_prefix, 1)

            @block.scalar
            def _(act):
                for t in range(NT):
                    act.wait_ge(s.moe_gate, t + 1)
                    nc.scalar.activation(scores[:, t * TILE:(t + 1) * TILE], ps[0:NEXP, t, :], ACT.Identity,
                                         bias=wgate("bg", rows=NEXP)).then_inc(s.moe_scored, 1)
                for t in range(NT):
                    act.wait_ge(s.moe_back, t + 1)
                    nc.scalar.copy(tokens[:, t * TILE:(t + 1) * TILE], ps[:, 1 + t % 7, :]).then_inc(s.moe_tokens, 1)

            @block.vector
            def _(dve):
                n = NCH * NEXP
                dve.wait_ge(s.moe_scores, 1)
                dve.wait_ge(s.moe_iota, 3)
                nc.vector.tensor_copy(gs[:].rearrange("p c e -> p (c e)"), ps[:, 0, 0:n]).then_inc(s.moe_hot, 1)
                dve.wait_ge(s.moe_hot, 1)
                nc.vector.tensor_reduce(best[:], gs[:], AX.X, ALU.max).then_inc(s.moe_hot, 1)
                dve.wait_ge(s.moe_hot, 2)
                wide = [P, NCH, NEXP]
                iota = io[:].unsqueeze(1).to_broadcast(wide)
                nc.vector.tensor_tensor(at[:], gs[:], best[:].unsqueeze(2).to_broadcast(wide), ALU.is_equal
                                        ).then_inc(s.moe_hot, 1)
                dve.wait_ge(s.moe_hot, 3)
                nc.vector.scalar_tensor_tensor(out=hot[:], in0=at[:], scalar=-16.0, in1=iota, op0=ALU.mult, op1=ALU.add
                                               ).then_inc(s.moe_hot, 1)
                dve.wait_ge(s.moe_hot, 4)
                nc.vector.tensor_reduce(pick[:], hot[:], AX.X, ALU.min).then_inc(s.moe_pick, 1)
                dve.wait_ge(s.moe_pick, 1)
                nc.vector.tensor_tensor(hot[:], hot[:], pick[:].unsqueeze(2).to_broadcast(wide), ALU.is_equal
                                        ).then_inc(s.moe_hot, 1)

                def then(m, j):
                    m.then_inc(s.moe_order, 1)
                    dve.wait_ge(s.moe_order, j)
                flat = lambda v: v.rearrange("p e c -> p (e c)")
                sums = lambda lo: ps[:, 0, lo:lo + n].rearrange("p (c e) -> p e c", e=NEXP)
                then(nc.vector.tensor_copy(count[:], count_i[:]), 1)
                dve.wait_ge(s.moe_prefix, 1)
                then(nc.vector.tensor_copy(total[:], sums(0)), 2)
                then(nc.vector.tensor_tensor_scan(flat(upto[:]), flat(go_on[:]), flat(total[:]), 0.0, ALU.mult, ALU.add), 3)
                deep = [P, NEXP, NCH]
                then(nc.vector.tensor_tensor(more[:], upto[:, :, NCH - 1:NCH].to_broadcast(deep),
                                             count[:, 0:NCH].unsqueeze(1).to_broadcast(deep), ALU.is_gt), 4)
                then(nc.vector.tensor_reduce(tiles[:], more[:], AX.X, ALU.add), 5)
                then(nc.vector.tensor_tensor_scan(end[:], go_on[:, 0, 1:1 + NEXP], tiles[:], 0.0, ALU.mult, ALU.add), 6)
                then(nc.vector.tensor_tensor(begin[:], end[:], tiles[:], ALU.subtract), 7)
                then(nc.vector.tensor_tensor(upto[:], upto[:], total[:], ALU.subtract), 8)
                then(nc.vector.tensor_tensor(upto[:], upto[:], begin[:].unsqueeze(2).to_broadcast(deep), ALU.add), 9)
                then(nc.vector.scalar_tensor_tensor(out=more[:], in0=upto[:], scalar=float(P), in1=sums(n),
                                                    op0=ALU.mult, op1=ALU.add), 10)
                then(nc.vector.tensor_tensor(place[:], more[:].rearrange("p e c -> p c e"), hot[:], ALU.mult), 11)
                then(nc.vector.tensor_reduce(placed_at[:], place[:], AX.X, ALU.add), 12)
                nc.vector.tensor_copy(place_i[:], placed_at[:]).then_inc(s.moe_place, 1)
                far = [1, XT, NEXP]
                then(nc.vector.tensor_tensor(ended[:], end[0:1, :].unsqueeze(1).to_broadcast(far),
                                             count[0:1, :].unsqueeze(2).to_broadcast(far), ALU.is_le), 13)
                then(nc.vector.tensor_reduce(expert[:], ended[:], AX.X, ALU.add), 14)
                then(nc.vector.tensor_scalar(expert[:], expert[:], float(NEXP - 1), None, ALU.min), 15)
                nc.vector.tensor_copy(expert_i[:], expert[:]).then_inc(s.moe_place, 1)

        first = 4
        cuts = [0, first, XT]

        def tile_pipeline(eng, step):
            last = first + (XT - first) // 2 * 2
            for i in range(first):
                step(i, i % 2)
            with eng.Fori(first // 2, last // 2) as turn:
                for n in range(2):
                    step(turn * 2 + n, n)
            for i in range(last, XT + 3):
                step(i, i % 2)

        def has(i, lag):
            return not isinstance(i, int) or 0 <= i - lag < XT

        def chosen(eng, t):
            return eng.value_load(expert_i[0:1, bass.ds(t, 1)], min_val=0, max_val=NEXP - 1)

        with nc.Block() as block:
            @block.sync
            def _(sp):
                for j in range(2):
                    sp.dma_start(xs[:, cuts[j]:cuts[j + 1], :], by_tile(sorted_in, cuts[j], cuts[j + 1])
                                 ).then_inc(s.moe_sorted, 16)
                    sp.wait_ge(s.moe_sorted, 16 * (j + 1))
                for lo, hi in ((0, XT - 6), (XT - 6, XT)):
                    sp.wait_ge(s.moe_stored, hi)
                    sp.dma_start(by_tile(sorted_out, lo, hi), ys[:, lo:hi, :]).then_inc(s.moe_kept, 16)
                sp.wait_ge(s.moe_kept, 32)

            @block.gpsimd
            def _(pool):
                def step(i, n):
                    if has(i, 0):
                        if isinstance(i, int):
                            pool.wait_ge(s.moe_sorted, 16 if i < first else 32)
                        at_least(pool, s.moe_turned, i - 1)
                        nc.gpsimd.tensor_copy(xin[:, n, :], xs[:, bass.ds(i, 1), :].rearrange("p t d -> p (t d)")
                                              ).then_inc(s.moe_fetched, 1)
                    if isinstance(i, int) and i == first - 1:
                        pool.wait_ge(s.moe_sorted, 32)
                tile_pipeline(pool, step)

            @block.tensor
            def _(pe):
                def step(i, n):
                    e1 = chosen(pe, i - 1) if has(i, 1) else None
                    e2 = chosen(pe, i - 3) if has(i, 3) else None
                    if has(i, 1):
                        t, m = i - 1, 1 - n
                        pe.wait_ge(s.moe_features, t + 1)
                        at_least(pe, s.moe_biased, t - 1)
                        nc.tensor.matmul(ps[:, 2 + m, :], xT[:, m, :], w("w1")[:, bass.ds(e1 * EH, EH)], start=True, stop=True
                                         ).then_inc(s.moe_hidden, 1)
                    if has(i, 2):
                        t = i - 2
                        pe.wait_ge(s.moe_biased, t + 1)
                        at_least(pe, s.moe_relu, t - 1)
                        pe.nop(nofuse=True)
                        for c in range(EH // P):
                            mm = nc.tensor.transpose(ps[:, 4 + n, c * P:(c + 1) * P], hr[:, n, c * P:(c + 1) * P],
                                                     k.cf("identf"))
                        mm.then_inc(s.moe_turn, 1)
                    if has(i, 0):
                        pe.wait_ge(s.moe_fetched, i + 1)
                        at_least(pe, s.moe_features, i - 1)
                        pe.nop(nofuse=True)
                        nc.tensor.transpose(ps[:, n, 0:P], xin[:, n, :], k.cf("identf")).then_inc(s.moe_turned, 1)
                    if has(i, 3):
                        t, m = i - 3, 1 - n
                        pe.wait_ge(s.moe_relu, t + 1)
                        at_least(pe, s.moe_stored, t - 1)
                        pe.nop(nofuse=True)
                        for c in range(EH // P):
                            mm = nc.tensor.matmul(ps[:, 6 + m, 0:P], hT[:, m, c * P:(c + 1) * P],
                                                  w("w2")[:, bass.ds(e2 * EH + c * P, P)], start=(c == 0),
                                                  stop=(c == EH // P - 1))
                        mm.then_inc(s.moe_out, 1)
                tile_pipeline(pe, step)

            @block.scalar
            def _(act):
                def step(i, n):
                    if has(i, 2):
                        t = i - 2
                        act.wait_ge(s.moe_turn, t + 1)
                        at_least(act, s.moe_out, t - 1)
                        nc.scalar.activation(hT[:, n, :], ps[:, 4 + n, :], ACT.Relu).then_inc(s.moe_relu, 1)
                    if has(i, 0):
                        act.wait_ge(s.moe_turned, i + 1)
                        at_least(act, s.moe_hidden, i - 1)
                        nc.scalar.copy(xT[:, n, :], ps[:, n, 0:P]).then_inc(s.moe_features, 1)
                tile_pipeline(act, step)

            @block.vector
            def _(dve):
                def step(i, n):
                    m = 1 - n
                    e1 = chosen(dve, i - 1) if has(i, 1) else None
                    e2 = chosen(dve, i - 3) if has(i, 3) else None
                    if has(i, 1):
                        t = i - 1
                        dve.wait_ge(s.moe_hidden, t + 1)
                        at_least(dve, s.moe_turn, t - 1)
                        nc.vector.tensor_tensor(hr[:, m, :], ps[:, 2 + m, :], wb("b1")[:, bass.ds(e1 * EH, EH)], ALU.add
                                                ).then_inc(s.moe_biased, 1)
                    if has(i, 3):
                        t = i - 3
                        dve.wait_ge(s.moe_out, t + 1)
                        nc.vector.tensor_tensor(ys[:, bass.ds(t, 1), :].rearrange("p t d -> p (t d)"), ps[:, 6 + m, 0:P],
                                                wb("b2")[:, bass.ds(e2 * P, P)], ALU.add).then_inc(s.moe_stored, 1)
                tile_pipeline(dve, step)

        GR = 8
        with nc.Block() as block:
            @block.gpsimd
            def _(pool):
                for c in range(NCH):
                    g = c // GR
                    gathered = (s.moe_gathered0, s.moe_gathered1)[g % 2]
                    if c % GR == 0:
                        at_least(pool, gathered, 16 * GR * (g // 2))
                    nc.gpsimd.indirect_dma_start(xs[:, c, :], None, sorted_out,
                                                 bass.IndirectOffsetOnAxis(place_i[:, c:c + 1], 0)).then_inc(gathered, 16)

            @block.tensor
            def _(pe):
                for t in range(NT):
                    g = 4 * t // GR
                    pe.wait_ge((s.moe_gathered0, s.moe_gathered1)[g % 2], 16 * GR * (g // 2 + 1))
                    for q in range(4):
                        m = nc.tensor.transpose(ps[:, t, q * P:(q + 1) * P], xs[:, 4 * t + q, :], k.cf("identf"))
                    m.then_inc(s.moe_back, 1)

            @block.scalar
            def _(act):
                for t in range(NT):
                    act.wait_ge(s.moe_back, NT + t + 1)
                    nc.scalar.copy(k.Y[:, t * TILE:(t + 1) * TILE], ps[:, t, :])


def ternary(k, call, wt):
    nc, s, ps = k.nc, k.s, k.ps
    n = 512
    with ExitStack() as ctx:
        part = ctx.enter_context(nc.sbuf_tensor(f"tern_part{call}", [P, 2], F32))
        lim = ctx.enter_context(nc.sbuf_tensor(f"tern_lim{call}", [P, 3], F32))
        lowt = ctx.enter_context(nc.sbuf_tensor(f"tern_low{call}", [P, n], F32))
        hi = ctx.enter_context(nc.sbuf_tensor(f"tern_hi{call}", [P, n], F32))
        block = ctx.enter_context(nc.Block())

        @block.vector
        def _(dve):
            base = 8 * call

            def then(m, j):
                m.then_inc(s.tern, 1)
                dve.wait_ge(s.tern, base + j)
            then(nc.vector.tensor_reduce(part[:, 0:1], wt, AX.X, ALU.add, apply_absolute_value=True), 1)
            dve.wait_ge(s.tern_mean, call + 1)
            then(nc.vector.tensor_scalar(lim[:, 0:1], ps[:, 0, 0:1], 1.0 / n, 1e-8, ALU.mult, ALU.max), 2)
            then(nc.vector.tensor_scalar(lim[:, 1:2], lim[:, 0:1], 0.5, None, ALU.mult), 3)
            then(nc.vector.tensor_scalar(lim[:, 2:3], lim[:, 0:1], -0.5, None, ALU.mult), 4)
            then(nc.vector.tensor_scalar(hi[:], wt, lim[:, 1:2], None, ALU.is_gt), 5)
            then(nc.vector.tensor_scalar(lowt[:], wt, lim[:, 2:3], None, ALU.is_lt), 6)
            then(nc.vector.tensor_tensor(hi[:], hi[:], lowt[:], ALU.subtract), 7)
            nc.vector.tensor_tensor(lowt[:], hi[:], wt, ALU.subtract).then_inc(s.tern_step, 1)
            dve.wait_ge(s.tern_step, 2 * call + 1)
            nc.vector.tensor_tensor(wt, wt, lowt[:], ALU.add).then_inc(s.tern_step, 1)
            nc.vector.sem_inc(s.tern, 1)

        @block.tensor
        def _(pe):
            pe.wait_ge(s.tern, 8 * call + 1)
            nc.tensor.matmul(ps[:, 0, 0:1], k.cf("mean"), part[:, 0:1], start=True, stop=True).then_inc(s.tern_mean, 1)


def fold_products(k, sem, jobs):
    nc, ps = k.nc, k.ps
    done = k.folds
    k.folds += len(jobs)
    with nc.Block() as block:
        @block.tensor
        def _(pe):
            for j, (out, pairs) in enumerate(jobs):
                m, n = out.shape[0], out.shape[-1]
                for e, (a, b) in enumerate(pairs):
                    mm = nc.tensor.matmul(ps[0:m, j, 0:n], a, b, start=(e == 0), stop=(e == len(pairs) - 1))
                mm.then_inc(k.s.fold, 1)

        @block.vector
        def _(dve):
            for j, (out, pairs) in enumerate(jobs):
                m, n = out.shape[0], out.shape[-1]
                dve.wait_ge(k.s.fold, done + j + 1)
                nc.vector.tensor_copy(out, ps[0:m, j, 0:n]).then_inc(k.s.folded, 1)


def gated_linear(k, call, weight, bias, src, out):
    nc, s, ps = k.nc, k.s, k.ps
    base = call * NT
    cols = lambda t: slice(t * TILE, (t + 1) * TILE)
    with nc.Block() as block:
        @block.tensor
        def _(pe):
            for t in range(NT):
                nc.tensor.matmul(ps[:, t, :], weight, src[:, cols(t)], start=True, stop=True).then_inc(s.lin_product, 1)

        @block.scalar
        def _(act):
            for t in range(NT):
                act.wait_ge(s.lin_product, t + 1)
                nc.scalar.activation(k.Y[:, cols(t)], ps[:, t, :], ACT.Silu, bias=bias).then_inc(s.silu, 1)

        @block.vector
        def _(dve):
            for t in range(NT):
                dve.wait_ge(s.silu, base + t + 1)
                nc.vector.tensor_tensor(k.Y[:, cols(t)], k.S[:, cols(t)], k.Y[:, cols(t)], ALU.mult).then_inc(s.gate_times, 1)
                dve.wait_ge(s.gate_times, base + t + 1)
                nc.vector.tensor_tensor(k.X[:, cols(t)], k.X[:, cols(t)], k.Y[:, cols(t)], ALU.add).then_inc(s.gate_added, 1)

        @block.sync
        def _(sp):
            for t in range(NT):
                sp.wait_ge(s.gate_added, base + t + 1)
                sp.dma_start(out[:, cols(t)], k.X[:, cols(t)]).then_inc(s.out_stored, 16)
            sp.wait_ge(s.out_stored, 16 * NT)


class Signals:

    def __init__(self, new):
        self.load_x = new("load_x")
        self.load_const = new("load_const")
        self.load_l0a = new("load_l0a")
        self.load_l0f = new("load_l0f")
        self.load_l1 = new("load_l1")
        self.load_moe = new("load_moe")
        self.load_l2 = new("load_l2")
        self.load_l3 = new("load_l3")
        self.cast = new("cast")
        self.credit = new("credit")
        self.ln_free = new("ln_free")
        self.ln_zero = new("ln_zero")
        self.ln_shifted = new("ln_shifted")
        self.ln_copied = new("ln_copied")
        self.ln_centred = new("ln_centred")
        self.ln_squared = new("ln_squared")
        self.ln_var = new("ln_var")
        self.ln_rstd = new("ln_rstd")
        self.ln_rstd2 = new("ln_rstd2")
        self.ln_vy2 = new("ln_vy2")
        self.ln_exact = new("ln_exact")
        self.ln_affine = new("ln_affine")
        self.rms_free = new("rms_free")
        self.rms_product = new("rms_product")
        self.rms_squared = new("rms_squared")
        self.rms_mean = new("rms_mean")
        self.rms_rstd = new("rms_rstd")
        self.rms_rstd2 = new("rms_rstd2")
        self.rms_vy2 = new("rms_vy2")
        self.rms_exact = new("rms_exact")
        self.rms_weight = new("rms_weight")
        self.ff_gelu = new("ff_gelu")
        self.ff_value = new("ff_value")
        self.ff_value_used = new("ff_value_used")
        self.ff_gate = new("ff_gate")
        self.ff_hid_used = new("ff_hid_used")
        self.ff_out_used = new("ff_out_used")
        self.mix_used = new("mix_used")
        self.mix_product = new("mix_product")
        self.mix_sigmoid = new("mix_sigmoid")
        self.gate_product = new("gate_product")
        self.gate_ready = new("gate_ready")
        self.sp_step = new("sp_step")
        self.sp_max = new("sp_max")
        self.sp_coef = new("sp_coef")
        self.decay = new("decay")
        self.decay2 = new("decay2")
        self.keep = new("keep")
        self.scaled = new("scaled")
        self.reset = new("reset")
        self.scanned = new("scanned")
        self.gated = new("gated")
        self.hs2 = new("hs2")
        self.la_init = new("la_init")
        self.la_shifted = new("la_shifted")
        self.la_vprod = new("la_vprod")
        self.la_rot = new("la_rot")
        self.la_rotated = new("la_rotated")
        self.la_qk = new("la_qk")
        self.la_stored = new("la_stored")
        self.la_squared = new("la_squared")
        self.la_product = new("la_product")
        self.la_rnorm = new("la_rnorm")
        self.la_rnorm2 = new("la_rnorm2")
        self.la_vy2 = new("la_vy2")
        self.la_exact = new("la_exact")
        self.la_clamped = new("la_clamped")
        self.la_vread = new("la_vread")
        self.la_norm = new("la_norm")
        self.la_max = new("la_max")
        self.la_score = new("la_score")
        self.la_m2 = new("la_m2")
        self.la_shift = new("la_shift")
        self.la_mt = new("la_mt")
        self.la_prob = new("la_prob")
        self.la_keyed = new("la_keyed")
        self.la_divided = new("la_divided")
        self.la_attended = new("la_attended")
        self.la_turn = new("la_turn")
        self.la_turned = new("la_turned")
        self.la_out = new("la_out")
        self.la_table = new("la_table")
        self.la_rec = new("la_rec")
        self.la_sqsum = new("la_sqsum")
        self.la_qkp = new("la_qkp")
        self.at_parts = new("at_parts")
        self.at_stacked = new("at_stacked")
        self.at_scratch = new("at_scratch")
        self.at_keyed = new("at_keyed")
        self.at_init = new("at_init")
        self.at_vprod = new("at_vprod")
        self.at_fetched = new("at_fetched")
        self.at_used = new("at_used")
        self.at_product = new("at_product")
        self.at_vread = new("at_vread")
        self.at_max = new("at_max")
        self.at_score = new("at_score")
        self.at_m2 = new("at_m2")
        self.at_shift = new("at_shift")
        self.at_mt = new("at_mt")
        self.at_prob = new("at_prob")
        self.at_divided = new("at_divided")
        self.at_attended = new("at_attended")
        self.at_sums = new("at_sums")
        self.at_raw = new("at_raw")
        self.at_zeroed = new("at_zeroed")
        self.at_stored = new("at_stored")
        self.at_out = new("at_out")
        self.at_rec = new("at_rec")
        self.at_hi = new("at_hi")
        self.at_res = new("at_res")
        self.at_mid = new("at_mid")
        self.at_sum = new("at_sum")
        self.at_content = new("at_content")
        self.alibi_loaded = new("alibi_loaded")
        self.alibi_cast = new("alibi_cast")
        self.alibi_rows = new("alibi_rows")
        self.moe_iota = new("moe_iota")
        self.moe_init = new("moe_init")
        self.moe_cleared = new("moe_cleared")
        self.moe_gate = new("moe_gate")
        self.moe_scored = new("moe_scored")
        self.moe_scores = new("moe_scores")
        self.moe_back = new("moe_back")
        self.moe_tokens = new("moe_tokens")
        self.moe_prefix = new("moe_prefix")
        self.moe_hot = new("moe_hot")
        self.moe_pick = new("moe_pick")
        self.moe_order = new("moe_order")
        self.moe_place = new("moe_place")
        self.moe_scattered = new("moe_scattered")
        self.moe_sorted = new("moe_sorted")
        self.moe_fetched = new("moe_fetched")
        self.moe_turned = new("moe_turned")
        self.moe_features = new("moe_features")
        self.moe_hidden = new("moe_hidden")
        self.moe_biased = new("moe_biased")
        self.moe_turn = new("moe_turn")
        self.moe_relu = new("moe_relu")
        self.moe_out = new("moe_out")
        self.moe_stored = new("moe_stored")
        self.moe_kept = new("moe_kept")
        self.moe_gathered0 = new("moe_gathered0")
        self.moe_gathered1 = new("moe_gathered1")
        self.tern = new("tern")
        self.tern_mean = new("tern_mean")
        self.tern_step = new("tern_step")
        self.fold = new("fold")
        self.folded = new("folded")
        self.lin_product = new("lin_product")
        self.silu = new("silu")
        self.gate_times = new("gate_times")
        self.gate_added = new("gate_added")
        self.out_stored = new("out_stored")


def program(nc, x, cast, conf, rope0, alibi_q, alibi_k, l0a, l0f0, l0f1, l1, moe, moeb, l2, l3, out):
    with ExitStack() as ctx:
        k = Core()
        s = Signals(lambda name: ctx.enter_context(nc.semaphore(name)))
        k.nc, k.s = nc, s
        sb = lambda n, shape, dt=F32: ctx.enter_context(nc.sbuf_tensor(n, shape, dt))
        k.X, k.XN, k.S, k.Y = (sb(n, [P, N]) for n in ("x", "xn", "s", "y"))
        castt = sb("cast", [P, CAST[1]], BF16)
        conft = sb("conf", [P, CONF[1]])
        k.eps5, k.eps6 = sb("eps5", [P, 1]), sb("eps6", [P, 1])
        k.cb, k.cf = pack(castt, CAST[0]), pack(conft, CONF[0])
        k.ps = ctx.enter_context(nc.psum_tensor("ps", [P, 8, TILE], F32))
        k.shifts = k.rounds = k.stack_dmas = k.folds = 0
        raw = k.Y[:, 0:CAST[1]]

        stack = ExitStack()
        with stack:
            new = lambda n, shape, dt=F32: stack.enter_context(nc.sbuf_tensor(n, shape, dt))
            f0, f1, r0 = new("w_l0f0", [P, W_L0F[1]]), new("w_l0f1", [P, W_L0F[1]]), new("w_l0t", [P, W_L0T[1]])
            with nc.sbuf_tensor("w_l0a", [P, W_L0A[1]], F32) as a0:
                with nc.Block() as block:
                    @block.sync
                    def _(sp):
                        sp.dma_start(conft[:], conf).then_inc(s.load_const, 16)
                        for t in range(4):
                            cols = slice(t * N // 4, (t + 1) * N // 4)
                            sp.dma_start(k.X[:, cols], x[:, cols]).then_inc(s.load_x, 16)
                        sp.dma_start(raw, cast).then_inc(s.load_const, 16)
                        sp.dma_start(a0[:], l0a).then_inc(s.load_l0a, 16)
                        sp.dma_start(r0[:], rope0).then_inc(s.load_l0f, 16)
                        sp.dma_start(f0[:], l0f0).then_inc(s.load_l0f, 16)
                        sp.dma_start(f1[:], l0f1).then_inc(s.load_l0f, 16)
                        sp.wait_ge(s.load_x, 64)

                    @block.vector
                    def _(dve):
                        nc.vector.memset(k.eps5[:], 1e-5).then_inc(s.credit, 1)
                        nc.vector.memset(k.eps6[:], 1e-6).then_inc(s.credit, 1)
                        nc.vector.sem_inc(s.ln_free, U)
                        nc.vector.sem_inc(s.rms_free, U)
                        nc.vector.sem_inc(s.ff_gelu, CREDIT)
                        nc.vector.sem_inc(s.ff_value_used, CREDIT)
                        nc.vector.sem_inc(s.ff_hid_used, CREDIT)
                        nc.vector.sem_inc(s.ff_out_used, 2)
                        nc.vector.sem_inc(s.mix_used, 2)
                        dve.wait_ge(s.load_const, 32)
                        nc.vector.tensor_copy(castt[:], raw).then_inc(s.cast, 1)

                layer_norm(k, 0, k.X, k.XN)
                w = pack(a0, W_L0A[0])
                with nc.Block() as block:
                    @block.sync
                    def _(sp):
                        sp.wait_ge(s.load_l0a, 16)
                with ExitStack() as inner:
                    work = [inner.enter_context(nc.sbuf_tensor(n, [P, N], F32)) for n in ("mix_h", "mix_gate")]
                    recurrent_mixer(k, w, work)
            rope = pack(r0, W_L0T[0])
            with nc.Block() as block:
                @block.sync
                def _(sp):
                    sp.wait_ge(s.load_l0f, 48)
            hid = k.XN
            for layer, t in enumerate((f0, f1)):
                w = pack(t, W_L0F[0])
                src = k.XN if layer == 0 else k.Y
                local_attention(k, layer, w, rope, src, k.Y)
                layer_norm(k, 1 + layer, k.Y, hid, shift=True, affine=(w("lg"), w("lb")))
                feed_forward(k, 1 + layer, NT * 3 * (1 + layer), hid, HCH,
                             lambda lo, n: w("w1", HID + lo, n), lambda c, n: w("b1g", c, 1, rows=n),
                             lambda lo, n: w("w1", lo, n), lambda c, n: w("b1a", c, 1, rows=n),
                             lambda c, n: w("w2", c * P, P, rows=n), w("b2"), k.Y, k.Y)

        with ExitStack() as inner:
            t1 = inner.enter_context(nc.sbuf_tensor("w_l1", [P, W_L1[1]], F32))
            with nc.Block() as block:
                @block.sync
                def _(sp):
                    sp.dma_start(t1[:], l1).then_inc(s.load_l1, 16)
                    sp.wait_ge(s.load_l1, 16)
            layer_norm(k, 3, k.X, k.XN, gate=0)
            alibi_attention(k, pack(t1, W_L1[0]), (alibi_q, alibi_k))
            experts(k, pack(t1, W_L1[0]), moe, moeb)

        with ExitStack() as inner:
            t2 = inner.enter_context(nc.sbuf_tensor("w_l2", [P, W_L2[1]], F32))
            fold = inner.enter_context(nc.sbuf_tensor("l2_fold", [P, 5, P], F32))
            w2 = pack(t2, W_L2[0])
            with nc.Block() as block:
                @block.sync
                def _(sp):
                    sp.dma_start(t2[:], l2).then_inc(s.load_l2, 16)
                    sp.wait_ge(s.load_l2, 16)
            qa, kva = w2("qaT", rows=64), w2("kvaT", rows=32)
            layer_norm(k, 4, k.X, k.XN, gate=1,
                       jobs=[(fold[:, 0, :], qa, w2("qb", rows=64)), (fold[:, 1, :], qa, w2("qbr", rows=64)),
                             (fold[:, 2, :], kva, w2("kb", rows=32)), (fold[:, 3, :], kva, w2("kbr", rows=32)),
                             (fold[:, 4, :], kva, w2("vb", rows=32))])
            rope8_attention(k, w2, fold)
            ternary(k, 0, w2("f1"))
            ternary(k, 1, w2("f2"))
            feed_forward(k, 3, NT * 9, k.XN, [(c * P, P) for c in range(4)], lambda lo, n: w2("f1", lo, n),
                         lambda c, n: w2("f1b", c, 1), None, None, lambda c, n: w2("f2", c * P, P), w2("f2b"), None, k.Y)

        with ExitStack() as inner:
            t3 = inner.enter_context(nc.sbuf_tensor("w_l3", [P, W_L3[1]], F32))
            fold = inner.enter_context(nc.sbuf_tensor("l3_fold", [P, 5 * P], F32))
            w3 = pack(t3, W_L3[0])
            with nc.Block() as block:
                @block.sync
                def _(sp):
                    sp.dma_start(t3[:], l3).then_inc(s.load_l3, 16)
                    sp.wait_ge(s.load_l3, 16)
            qa = w3("qT", rows=64)
            layer_norm(k, 5, k.X, k.XN, gate=2,
                       jobs=[(fold[:, 0:P], qa, w3("qd", rows=64)), (fold[:, P:5 * P], qa, w3("qr", rows=64))])
            rms_norm(k, 2, None, k.Y, w3("gkv", rows=32), rows=32, mean="mean32", before=(w3("wkv"), k.XN))
            latent_attention(k, w3, fold, k.Y)
            with ExitStack() as dft:
                AT = dft.enter_context(nc.sbuf_tensor("dft_at", [P, 2, P], F32))
                M = dft.enter_context(nc.sbuf_tensor("dft_m", [P, P], F32))
                fold_products(k, None, [(AT[:, 0, :], [(w3("fr"), w3("dc")), (w3("fi"), w3("ds"))]),
                                        (AT[:, 1, :], [(w3("fi"), w3("dc")), (w3("fr"), w3("dsn"))])])
                fold_products(k, None, [(M[:], [(AT[:, 0, :], w3("dcm")), (AT[:, 1, :], w3("dsm"))])])
                gated_linear(k, 3, M[:], w3("fb"), k.XN, out)


def lay(where, **parts):
    packed = np.zeros((P, where[1]), np.float32)
    for name, a in parts.items():
        at, n = where[0][name]
        a = np.asarray(a)
        a = a.reshape(a.shape[0], -1)
        assert a.shape[1] == n, (name, a.shape, n)
        packed[:a.shape[0], at:at + n] = a
    return packed


def chunked(a, rows=P):
    return a.reshape(-1, rows, a.shape[1]).transpose(1, 0, 2).reshape(rows, -1)


def columns(v):
    return v.reshape(-1, P).T


def padded(a, sizes):
    out, at = [], 0
    for n in sizes:
        out.append(np.concatenate([a[at:at + n], np.zeros((P - n, a.shape[1]), a.dtype)], 0))
        at += n
    return np.concatenate(out, 1)


def kernel(**inputs):
    import concourse.bacc as bacc
    from concourse.bass_utils import run_bass_kernel_spmd
    v = {n: np.asarray(a) for n, a in inputs.items()}
    g = lambda layer: {n[len(layer):]: a for n, a in v.items() if n.startswith(layer)}
    packs = {}
    packs["x"] = np.ascontiguousarray(v["L0_attn_hidden_states"].reshape(N, P).T)
    packs["cast"] = np.concatenate([a for _, a in const_cast()], 1).astype(np.float32)
    packs["conf"] = np.concatenate([a for _, a in const_f32()], 1).astype(np.float32)
    packs["rope0"] = np.concatenate([a for _, a in const_local_rope()], 1).astype(np.float32)
    packs["alibi_q"], packs["alibi_k"] = const_alibi()
    a = g("L0_attn_")
    col = lambda x: x.reshape(-1, 1)
    packs["l0a"] = lay(W_L0A, fc=a["fc_w"].T, fr=a["fc_r_w"].T, fi=a["fc_i_w"].T, gate=a["fc_gate_w"].T,
                       mg=a["mlp_gate_w"].T, mf=a["mlp_fc_w"].T, mo=chunked(a["out_w"].T), fc_b=col(a["fc_b"]),
                       fr_b=col(a["fc_r_b"]), fi_b=col(a["fc_i_b"]), gate_b=col(a["fc_gate_b"]), norm=col(a["norm_w"]),
                       norm2=col(a["norm2_w"]), alpha=col(a["alpha"]), mo_b=col(a["out_b"]),
                       mg_b=columns(a["mlp_gate_b"]), mf_b=columns(a["mlp_fc_b"]))
    a = g("L0_ffn_")
    halves = np.arange(512).reshape(2, 4, 2, 32).transpose(0, 2, 1, 3).reshape(-1)
    four = lambda x: col(np.concatenate([x] * 4))
    sizes = [n for _, n in HCH]
    for l in range(2):
        wq, wk, wv = np.split(a["wqkv"][l], 3, 1)
        b1 = a["b1"][l].reshape(-1, 1)
        packs[f"l0f{l}"] = lay(W_L0F, wq=wq[:, halves], wk=wk[:, halves], wv=wv, wo=chunked(a["wo"][l]),
                               w1=a["w1"][l], w2=padded(a["w2"][l], sizes), q1=four(a["q_scale"][l][:32]),
                               q2=four(a["q_scale"][l][32:]), k1=four(a["k_scale"][l][:32]), k2=four(a["k_scale"][l][32:]),
                               lg=col(a["ln_g"][l]), lb=col(a["ln_b"][l]), b1a=padded(b1[:HID], sizes),
                               b1g=padded(b1[HID:], sizes), b2=col(a["b2"][l]))
    a = g("L1_attn_")
    wq, wk, wv = np.split(a["w_attn"], 3, 0)
    f = g("L1_ffn_")
    packs["l1"] = lay(W_L1, wq=wq.T[:, DH], wk=wk.T[:, DH], wv=wv.T, wo=a["w_proj"].T, wg=f["Wg"], bg=col(f["bg"]))
    a = f
    packs["moe"] = lay(W_MOE, w1=a["W1"].transpose(1, 0, 2),
                       w2=chunked(a["W2"].reshape(-1, P)))
    on_all = lambda x: np.broadcast_to(x.reshape(1, -1), (P, x.size))
    packs["moeb"] = lay(W_MOEB, b1=on_all(a["b1"]), b2=on_all(a["b2"]))
    a, f = g("L2_attn_"), g("L2_ffn_")
    kv = a["Wkvb"].reshape(-1, 4, D8, 2)
    kb = np.repeat(kv[..., 0], 4, 1).reshape(-1, P)
    vb = np.repeat(kv[..., 1], 4, 1).reshape(-1, P)
    swap = [h * D8 + (d ^ 1) for d in range(D8) for h in range(H16)]
    packs["l2"] = lay(W_L2, qaT=a["Wqa"].T, qb=a["Wqb"][:, DH], qbr=a["Wqb"][:, swap], kvaT=a["Wkva"].T, kb=kb[:, DH],
                      kbr=kb[:, swap], vb=vb, wo=a["Wout"], bo=col(a["bout"]),
                      cos=dict(const_rope8())["cos"], sin=dict(const_rope8())["sin"],
                      f1=f["W1"].T, f1b=columns(f["b1"]), f2=chunked(f["W2"].T), f2b=col(f["b2"]))
    a, f = g("L3_attn_"), g("L3_ffn_")
    dh32 = [h * 32 + d for d in range(32) for h in range(H16)]
    packs["l3"] = lay(W_L3, wkv=a["W_kv"], gkv=col(a["g_kv"]), kd=a["W_kdec"][:, DH], vd=a["W_vdec"], qT=a["W_q"].T,
                      qd=a["W_qdec"][:, DH], qr=a["W_qrope"][:, dh32], kr=a["W_krope"][:, dh32], wo=a["W_o"],
                      fr=f["w_freq_real"], fi=f["w_freq_imag"], fb=col(f["bias"]),
                      **dict(const_rope32()), **dict(const_dft()))
    nc = bacc.Bacc("TRN2", target_bir_lowering=False, num_devices=1)
    args = [nc.dram_tensor(f"in_{n}", p.shape, F32, kind="ExternalInput").ap() for n, p in packs.items()]
    out = nc.dram_tensor("out_0", (P, N), F32, kind="ExternalOutput").ap()
    program(nc, *args, out)
    r = run_bass_kernel_spmd(nc, [{f"in_{n}": np.ascontiguousarray(p) for n, p in packs.items()}], core_ids=[0])
    return np.ascontiguousarray(r.results[0]["out_0"].T).reshape(B, L, P)
```
